# Optimizing a Trainium2 kernel written in Bass

```python
import numpy as np
import jax
import jax.numpy as jnp

def _softmax(x, axis=-1):
    return jax.nn.softmax(x, axis=axis)

def _gelu(x):
    return jax.nn.gelu(x, approximate=True)

def _silu(x):
    return jax.nn.silu(x)

def _sigmoid(x):
    return jax.nn.sigmoid(x)

def _layernorm(x, axis=-1, eps=1e-05):
    m = jnp.mean(x, axis=axis, keepdims=True)
    v = jnp.var(x, axis=axis, keepdims=True)
    return (x - m) / jnp.sqrt(v + eps)

def _scatter_add(tgt, idx, src, axis=0):
    return tgt.at[idx].add(src)

def _segment_sum(src, seg, n):
    return jax.ops.segment_sum(src, seg, n)
kernel_name = 'mk_prb_d4_jaxref_r8_a3b151'

def setup_inputs(seed: int=0):
    np.random.seed(seed)
    _w = jnp.asarray

    def _L0_attn_setup():
        import jax, jax.numpy as jnp
        import numpy as np
        D_MODEL, STATE, N_EXP, VOCAB = (128, 16, 4, 4000)
        B, L = (4, 256)
        EPS = 1e-05
        key = jax.random.key(seed)
        ks = jax.random.split(key, 20)
        d, s, e, f = (D_MODEL, STATE, N_EXP, 4 * D_MODEL)
        sc = 0.02
        inp = {'x': jax.random.normal(ks[0], (B, L, d), jnp.float32), 'A_log': jnp.log(jax.random.uniform(ks[1], (d, s)) * 0.9 + 0.1), 'D_param': jnp.ones((d,), jnp.float32), 'Wd': jax.random.normal(ks[2], (d, d)) * sc, 'bd': jnp.zeros((d,)), 'WB': jax.random.normal(ks[3], (d, s)) * sc, 'bB': jnp.zeros((s,)), 'WC': jax.random.normal(ks[4], (d, s)) * sc, 'bC': jnp.zeros((s,)), 'Wr': jax.random.normal(ks[5], (d, e)) * sc, 'br': jnp.zeros((e,)), 'up_w': jax.random.normal(ks[6], (e, d, f)) * sc, 'up_b': jnp.zeros((e, f)), 'down_w': jax.random.normal(ks[7], (e, f, d)) * sc, 'down_b': jnp.zeros((e, d)), 'ln_w': jnp.ones((d,)), 'ln_b': jnp.zeros((d,))}
        return inp
    _L0_attn_in = _L0_attn_setup()

    def _L0_ffn_setup():
        import jax, jax.numpy as jnp
        import numpy as np
        H_DIM, E_DIM = (128, 64)
        N_SHARED, N_ROUTED, TOP_K = (2, 16, 4)
        B, S = (4, 256)
        key = jax.random.key(seed)
        ks = jax.random.split(key, 6)
        sc = 1.0 / np.sqrt(H_DIM)
        ec = 1.0 / np.sqrt(E_DIM)
        return {'x': jax.random.normal(ks[0], (B, S, H_DIM), dtype=jnp.float32), 'shared_up': jax.random.uniform(ks[1], (N_SHARED, E_DIM, H_DIM), jnp.float32, -sc, sc), 'shared_down': jax.random.uniform(ks[2], (N_SHARED, H_DIM, E_DIM), jnp.float32, -ec, ec), 'routed_up': jax.random.uniform(ks[3], (N_ROUTED, E_DIM, H_DIM), jnp.float32, -sc, sc), 'routed_down': jax.random.uniform(ks[4], (N_ROUTED, H_DIM, E_DIM), jnp.float32, -ec, ec), 'router_w': jax.random.uniform(ks[5], (N_ROUTED, H_DIM), jnp.float32, -sc, sc)}
    _L0_ffn_in = _L0_ffn_setup()

    def _L1_attn_setup():
        import math
        import jax, jax.numpy as jnp
        import numpy as np
        HEADS = 16
        REL_WINDOW = 128
        key = jax.random.key(seed)
        k1, k2, k3, k4, k5 = jax.random.split(key, 5)
        b, s, d = (2, 256, 128)
        hd = d // HEADS
        R = 2 * REL_WINDOW + 1
        return {'x': jax.random.normal(k1, (b, s, d), dtype=jnp.float32), 'Wqkv': jax.random.normal(k2, (3 * d, d), dtype=jnp.float32) * (1.0 / math.sqrt(d)), 'bqkv': jax.random.normal(k3, (3 * d,), dtype=jnp.float32) * 0.02, 'Wr': jax.random.normal(k4, (R, hd), dtype=jnp.float32) * (1.0 / math.sqrt(hd)), 'br': jax.random.normal(k5, (R,), dtype=jnp.float32) * 0.02}
    _L1_attn_in = _L1_attn_setup()

    def _L1_ffn_setup():
        import jax, jax.numpy as jnp
        import numpy as np
        NUM_EXPERTS = 8
        CAP_FACTOR = 1.0
        MIN_CAP = 8
        key = jax.random.key(seed)
        ks = jax.random.split(key, 10)
        G, S, D, H, E = (4, 512, 128, 512, NUM_EXPERTS)
        s = 0.02
        return {'x': jax.random.normal(ks[0], (G, S, D), dtype=jnp.float32), 'gate': jax.random.normal(ks[1], (D, E), dtype=jnp.float32) * s, 'W1': jax.random.normal(ks[2], (E, D, H), dtype=jnp.float32) * s, 'b1': jnp.zeros((E, H), dtype=jnp.float32), 'W2': jax.random.normal(ks[3], (E, H, D), dtype=jnp.float32) * s, 'b2': jnp.zeros((E, D), dtype=jnp.float32), 'Ws1': jax.random.normal(ks[4], (D, H), dtype=jnp.float32) * s, 'bs1': jnp.zeros((H,), dtype=jnp.float32), 'Ws2': jax.random.normal(ks[5], (H, D), dtype=jnp.float32) * s, 'bs2': jnp.zeros((D,), dtype=jnp.float32)}
    _L1_ffn_in = _L1_ffn_setup()

    def _L2_attn_setup():
        import jax, jax.numpy as jnp
        import numpy as np
        from jax import lax
        RWKV_K_CLAMP = 60.0
        RWKV_K_EPS = 1e-08
        key = jax.random.key(seed)
        ks = jax.random.split(key, 12)
        B, T, C = (4, 128, 128)
        s = 1.0 / np.sqrt(C)
        return {'xq': jax.random.normal(ks[0], (B, T, C), jnp.float32), 'xk': jax.random.normal(ks[1], (B, T, C), jnp.float32), 'xv': jax.random.normal(ks[2], (B, T, C), jnp.float32), 'time_decay': jax.random.normal(ks[3], (C, 1), jnp.float32) * 0.1, 'time_first': jnp.full((C, 1), np.log(0.3), jnp.float32), 'time_mix_k': jax.random.uniform(ks[4], (1, 1, C), jnp.float32), 'time_mix_v': jax.random.uniform(ks[5], (1, 1, C), jnp.float32), 'time_mix_r': jax.random.uniform(ks[6], (1, 1, C), jnp.float32), 'Wk': jax.random.normal(ks[7], (C, C), jnp.float32) * s, 'Wv': jax.random.normal(ks[8], (C, C), jnp.float32) * s, 'Wr': jax.random.normal(ks[9], (C, C), jnp.float32) * s, 'Wo': jax.random.normal(ks[10], (C, C), jnp.float32) * s}
    _L2_attn_in = _L2_attn_setup()

    def _L2_ffn_setup():
        import jax, jax.numpy as jnp
        import numpy as np
        DIM = 128
        DEPTH = 6
        HEADS = 16
        DIM_HEAD = 64
        WINDOW = 32
        INNER = HEADS * DIM_HEAD
        DIM_INNER = int(DIM * 4 * 2 / 3)
        QK_SCALE = 8.0

        def shift_tokens(t):
            a, s = jnp.split(t, 2, -1)
            s = jnp.pad(s, ((0, 0), (1, 0), (0, 0)))[:, :-1]
            return jnp.concatenate([a, s], -1)

        def l2norm(t):
            return t / jnp.maximum(jnp.linalg.norm(t, axis=-1, keepdims=True), 1e-12)

        def rotate_half(x):
            x1, x2 = jnp.split(x, 2, -1)
            return jnp.concatenate([-x2, x1], -1)

        def rotary_tables(n):
            half = jnp.arange(0, DIM_HEAD, 2, dtype=jnp.float32)
            inv_freq = 1.0 / 10000.0 ** (half / DIM_HEAD)
            t = jnp.arange(n, dtype=jnp.float32)
            freqs = t[:, None] * inv_freq[None, :]
            freqs = jnp.concatenate([freqs, freqs], -1)
            base_scale = (half + 0.4 * DIM_HEAD) / (1.4 * DIM_HEAD)
            power = (t - n // 2) / (WINDOW // 2)
            scale = base_scale[None, :] ** power[:, None]
            scale = jnp.concatenate([scale, scale], -1)
            return (freqs, scale)

        def local_attention(q, k, v):
            b, h, n, d = q.shape
            w = WINDOW
            nw = n // w
            bq = q.reshape(b, h, nw, w, d)
            bk = k.reshape(b, h, nw, w, d)
            bv = v.reshape(b, h, nw, w, d)

            def look(t):
                p = jnp.pad(t, ((0, 0), (0, 0), (1, 0), (0, 0), (0, 0)))
                return jnp.concatenate([p[:, :, :nw], p[:, :, 1:]], axis=3)
            bk2, bv2 = (look(bk), look(bv))
            seq = jnp.arange(n).reshape(nw, w)
            seq_p = jnp.pad(seq, ((1, 0), (0, 0)), constant_values=-1)
            jt = jnp.concatenate([seq_p[:nw], seq_p[1:]], axis=1)
            it = seq[:, :, None]
            jb = jt[:, None, :]
            mask = (it < jb) | (it > jb + w) | (jb == -1)
            sim = jnp.einsum('bhwie,bhwje->bhwij', bq, bk2) * QK_SCALE
            sim = jnp.where(mask, -jnp.finfo(sim.dtype).max, sim)
            attn = jax.nn.softmax(sim, -1)
            out = jnp.einsum('bhwij,bhwje->bhwie', attn, bv2)
            return out.reshape(b, h, n, d)

        def attn_layer(x, Wqkv, qs, ksc, Wo):
            b, n, _ = x.shape
            qkv = x @ Wqkv
            q, k, v = jnp.split(qkv, 3, -1)
            sh = lambda t: t.reshape(b, n, HEADS, DIM_HEAD).transpose(0, 2, 1, 3)
            q, k, v = (sh(q), sh(k), sh(v))
            q = l2norm(q) * qs
            k = l2norm(k) * ksc
            freqs, scale = rotary_tables(n)
            cos, sin = (jnp.cos(freqs), jnp.sin(freqs))
            q = q * cos * scale + rotate_half(q) * sin * scale
            inv = 1.0 / scale
            k = k * cos * inv + rotate_half(k) * sin * inv
            out = local_attention(q, k, v)
            out = out.transpose(0, 2, 1, 3).reshape(b, n, INNER)
            return out @ Wo

        def ffn_layer(x, g, bln, W1, b1, W2, b2):
            mu = x.mean(-1, keepdims=True)
            var = ((x - mu) ** 2).mean(-1, keepdims=True)
            xn = (x - mu) / jnp.sqrt(var + 1e-05) * g + bln
            hg = xn @ W1 + b1
            a, gate = jnp.split(hg, 2, -1)
            return a * jax.nn.gelu(gate, approximate=False) @ W2 + b2
        key = jax.random.key(seed)
        ks = jax.random.split(key, 8)
        B, N = (2, 256)
        init = lambda k, shape: jax.random.normal(k, shape, jnp.float32) * 0.02
        return {'x': jax.random.normal(ks[0], (B, N, DIM), jnp.float32), 'Wqkv': init(ks[1], (DEPTH, DIM, 3 * INNER)), 'q_scale': jnp.ones((DEPTH, DIM_HEAD), jnp.float32), 'k_scale': jnp.ones((DEPTH, DIM_HEAD), jnp.float32), 'Wo': init(ks[2], (DEPTH, INNER, DIM)), 'ln_g': jnp.ones((DEPTH, DIM), jnp.float32), 'ln_b': jnp.zeros((DEPTH, DIM), jnp.float32), 'W1': init(ks[3], (DEPTH, DIM, 2 * DIM_INNER)), 'b1': jnp.zeros((DEPTH, 2 * DIM_INNER), jnp.float32), 'W2': init(ks[4], (DEPTH, DIM_INNER, DIM)), 'b2': jnp.zeros((DEPTH, DIM), jnp.float32)}
    _L2_ffn_in = _L2_ffn_setup()

    def _L3_attn_setup():
        import jax, jax.numpy as jnp
        import numpy as np
        D_MODEL, N_HEADS, BATCH, SEQ = (128, 16, 2, 256)

        def get_freqs(seq, n_dim):
            inv_freq = 1.0 / 10000.0 ** (jnp.arange(0, n_dim, 2, dtype=jnp.float32) / n_dim)
            pos = jnp.arange(seq, dtype=jnp.float32)
            return pos[:, None] * inv_freq[None, :]

        def rope(x, freq):
            cos = jnp.cos(freq)[None, :, None, :]
            sin = jnp.sin(freq)[None, :, None, :]
            x1, x2 = (x[..., ::2], x[..., 1::2])
            r1 = x1 * cos - x2 * sin
            r2 = x1 * sin + x2 * cos
            return jnp.stack([r1, r2], axis=-1).reshape(x.shape)
        key = jax.random.key(seed)
        ks = jax.random.split(key, 5)
        w_scale = 0.01
        return {'x': jax.random.normal(ks[0], (BATCH, SEQ, D_MODEL), dtype=jnp.float32), 'qw': jax.random.normal(ks[1], (D_MODEL, D_MODEL), dtype=jnp.float32) * w_scale, 'kw': jax.random.normal(ks[2], (D_MODEL, D_MODEL), dtype=jnp.float32) * w_scale, 'vw': jax.random.normal(ks[3], (D_MODEL, D_MODEL), dtype=jnp.float32) * w_scale, 'ow': jax.random.normal(ks[4], (D_MODEL, D_MODEL), dtype=jnp.float32) * w_scale}
    _L3_attn_in = _L3_attn_setup()

    def _L3_ffn_setup():
        import jax, jax.numpy as jnp
        import numpy as np
        LATENT = 128
        LEAF_W = 64
        DEPTH = 4
        N_LEAVES = 2 ** DEPTH
        N_NODES = 2 ** DEPTH - 1
        B, S = (4, 256)

        def _fff_params(key, prefix):
            ks = jax.random.split(key, 4)
            d, h, l, n = (LATENT, LEAF_W, N_LEAVES, N_NODES)
            s_in = 1.0 / np.sqrt(d).astype(np.float32)
            s_h = 1.0 / np.sqrt(h).astype(np.float32)
            return {f'{prefix}_node_w': jax.random.normal(ks[0], (n, d), jnp.float32) * s_in, f'{prefix}_node_b': jax.random.normal(ks[1], (n,), jnp.float32) * s_in, f'{prefix}_w1': jax.random.normal(ks[2], (l, d, h), jnp.float32) * s_in, f'{prefix}_b1': jnp.zeros((l, h), jnp.float32), f'{prefix}_w2': jax.random.normal(ks[3], (l, h, d), jnp.float32) * s_h, f'{prefix}_b2': jnp.zeros((l, d), jnp.float32)}

        def _fff(x, node_w, node_b, w1, b1, w2, b2):
            Bx, Sx, D = x.shape
            xf = x.reshape(-1, D)
            N = xf.shape[0]
            cur = jnp.zeros((N,), jnp.int32)
            for _ in range(DEPTH):
                pw = node_w[cur]
                score = jnp.einsum('nd,nd->n', xf, pw) + node_b[cur]
                cur = 2 * cur + 1 + (score >= 0).astype(jnp.int32)
            leaf = cur - N_NODES
            sel = jax.nn.one_hot(leaf, N_LEAVES, dtype=xf.dtype)
            hidden_all = jax.nn.relu(jnp.einsum('nd,ldh->lnh', xf, w1) + b1[:, None, :])
            hidden = hidden_all * sel.T[:, :, None]
            out = jnp.einsum('lnh,lho->no', hidden, w2) + sel @ b2
            return out.reshape(Bx, Sx, D)
        key = jax.random.key(seed)
        kx, kq, kk, kv = jax.random.split(key, 4)
        inp = {'x': jax.random.normal(kx, (B, S, LATENT), jnp.float32)}
        inp.update(_fff_params(kq, 'q'))
        inp.update(_fff_params(kk, 'k'))
        inp.update(_fff_params(kv, 'v'))
        return inp
    _L3_ffn_in = _L3_ffn_setup()
    _d = {'L0_attn_x': _L0_attn_in['x'], 'L0_attn_A_log': _L0_attn_in['A_log'], 'L0_attn_D_param': _L0_attn_in['D_param'], 'L0_attn_Wd': _L0_attn_in['Wd'], 'L0_attn_bd': _L0_attn_in['bd'], 'L0_attn_WB': _L0_attn_in['WB'], 'L0_attn_bB': _L0_attn_in['bB'], 'L0_attn_WC': _L0_attn_in['WC'], 'L0_attn_bC': _L0_attn_in['bC'], 'L0_attn_Wr': _L0_attn_in['Wr'], 'L0_attn_br': _L0_attn_in['br'], 'L0_attn_up_w': _L0_attn_in['up_w'], 'L0_attn_up_b': _L0_attn_in['up_b'], 'L0_attn_down_w': _L0_attn_in['down_w'], 'L0_attn_down_b': _L0_attn_in['down_b'], 'L0_attn_ln_w': _L0_attn_in['ln_w'], 'L0_attn_ln_b': _L0_attn_in['ln_b'], 'L0_ffn_shared_up': _L0_ffn_in['shared_up'], 'L0_ffn_shared_down': _L0_ffn_in['shared_down'], 'L0_ffn_routed_up': _L0_ffn_in['routed_up'], 'L0_ffn_routed_down': _L0_ffn_in['routed_down'], 'L0_ffn_router_w': _L0_ffn_in['router_w'], 'L1_attn_Wqkv': _L1_attn_in['Wqkv'], 'L1_attn_bqkv': _L1_attn_in['bqkv'], 'L1_attn_Wr': _L1_attn_in['Wr'], 'L1_attn_br': _L1_attn_in['br'], 'L1_ffn_gate': _L1_ffn_in['gate'], 'L1_ffn_W1': _L1_ffn_in['W1'], 'L1_ffn_b1': _L1_ffn_in['b1'], 'L1_ffn_W2': _L1_ffn_in['W2'], 'L1_ffn_b2': _L1_ffn_in['b2'], 'L1_ffn_Ws1': _L1_ffn_in['Ws1'], 'L1_ffn_bs1': _L1_ffn_in['bs1'], 'L1_ffn_Ws2': _L1_ffn_in['Ws2'], 'L1_ffn_bs2': _L1_ffn_in['bs2'], 'L2_attn_xk': _L2_attn_in['xk'], 'L2_attn_xv': _L2_attn_in['xv'], 'L2_attn_time_decay': _L2_attn_in['time_decay'], 'L2_attn_time_first': _L2_attn_in['time_first'], 'L2_attn_time_mix_k': _L2_attn_in['time_mix_k'], 'L2_attn_time_mix_v': _L2_attn_in['time_mix_v'], 'L2_attn_time_mix_r': _L2_attn_in['time_mix_r'], 'L2_attn_Wk': _L2_attn_in['Wk'], 'L2_attn_Wv': _L2_attn_in['Wv'], 'L2_attn_Wr': _L2_attn_in['Wr'], 'L2_attn_Wo': _L2_attn_in['Wo'], 'L2_ffn_Wqkv': _L2_ffn_in['Wqkv'], 'L2_ffn_q_scale': _L2_ffn_in['q_scale'], 'L2_ffn_k_scale': _L2_ffn_in['k_scale'], 'L2_ffn_Wo': _L2_ffn_in['Wo'], 'L2_ffn_ln_g': _L2_ffn_in['ln_g'], 'L2_ffn_ln_b': _L2_ffn_in['ln_b'], 'L2_ffn_W1': _L2_ffn_in['W1'], 'L2_ffn_b1': _L2_ffn_in['b1'], 'L2_ffn_W2': _L2_ffn_in['W2'], 'L2_ffn_b2': _L2_ffn_in['b2'], 'L3_attn_qw': _L3_attn_in['qw'], 'L3_attn_kw': _L3_attn_in['kw'], 'L3_attn_vw': _L3_attn_in['vw'], 'L3_attn_ow': _L3_attn_in['ow'], 'L3_ffn_q_node_w': _L3_ffn_in['q_node_w'], 'L3_ffn_q_node_b': _L3_ffn_in['q_node_b'], 'L3_ffn_q_w1': _L3_ffn_in['q_w1'], 'L3_ffn_q_b1': _L3_ffn_in['q_b1'], 'L3_ffn_q_w2': _L3_ffn_in['q_w2'], 'L3_ffn_q_b2': _L3_ffn_in['q_b2'], 'L3_ffn_k_node_w': _L3_ffn_in['k_node_w'], 'L3_ffn_k_node_b': _L3_ffn_in['k_node_b'], 'L3_ffn_k_w1': _L3_ffn_in['k_w1'], 'L3_ffn_k_b1': _L3_ffn_in['k_b1'], 'L3_ffn_k_w2': _L3_ffn_in['k_w2'], 'L3_ffn_k_b2': _L3_ffn_in['k_b2'], 'L3_ffn_v_node_w': _L3_ffn_in['v_node_w'], 'L3_ffn_v_node_b': _L3_ffn_in['v_node_b'], 'L3_ffn_v_w1': _L3_ffn_in['v_w1'], 'L3_ffn_v_b1': _L3_ffn_in['v_b1'], 'L3_ffn_v_w2': _L3_ffn_in['v_w2'], 'L3_ffn_v_b2': _L3_ffn_in['v_b2']}
    _x0 = _d['L0_attn_x']
    _d['L0_attn_x'] = jax.random.normal(jax.random.fold_in(jax.random.key(seed), 1), (2, 1024, 128), dtype=_x0.dtype)
    del _x0
    return _d

def reference(L0_attn_x, L0_attn_A_log, L0_attn_D_param, L0_attn_Wd, L0_attn_bd, L0_attn_WB, L0_attn_bB, L0_attn_WC, L0_attn_bC, L0_attn_Wr, L0_attn_br, L0_attn_up_w, L0_attn_up_b, L0_attn_down_w, L0_attn_down_b, L0_attn_ln_w, L0_attn_ln_b, L0_ffn_shared_up, L0_ffn_shared_down, L0_ffn_routed_up, L0_ffn_routed_down, L0_ffn_router_w, L1_attn_Wqkv, L1_attn_bqkv, L1_attn_Wr, L1_attn_br, L1_ffn_gate, L1_ffn_W1, L1_ffn_b1, L1_ffn_W2, L1_ffn_b2, L1_ffn_Ws1, L1_ffn_bs1, L1_ffn_Ws2, L1_ffn_bs2, L2_attn_xk, L2_attn_xv, L2_attn_time_decay, L2_attn_time_first, L2_attn_time_mix_k, L2_attn_time_mix_v, L2_attn_time_mix_r, L2_attn_Wk, L2_attn_Wv, L2_attn_Wr, L2_attn_Wo, L2_ffn_Wqkv, L2_ffn_q_scale, L2_ffn_k_scale, L2_ffn_Wo, L2_ffn_ln_g, L2_ffn_ln_b, L2_ffn_W1, L2_ffn_b1, L2_ffn_W2, L2_ffn_b2, L3_attn_qw, L3_attn_kw, L3_attn_vw, L3_attn_ow, L3_ffn_q_node_w, L3_ffn_q_node_b, L3_ffn_q_w1, L3_ffn_q_b1, L3_ffn_q_w2, L3_ffn_q_b2, L3_ffn_k_node_w, L3_ffn_k_node_b, L3_ffn_k_w1, L3_ffn_k_b1, L3_ffn_k_w2, L3_ffn_k_b2, L3_ffn_v_node_w, L3_ffn_v_node_b, L3_ffn_v_w1, L3_ffn_v_b1, L3_ffn_v_w2, L3_ffn_v_b2):

    def _L0_attn_ref(x, A_log, D_param, Wd, bd, WB, bB, WC, bC, Wr, br, up_w, up_b, down_w, down_b, ln_w, ln_b):
        import jax, jax.numpy as jnp
        import numpy as np
        D_MODEL, STATE, N_EXP, VOCAB = (128, 16, 4, 4000)
        B, L = (4, 256)
        EPS = 1e-05
        Bb, Ll, d = x.shape
        delta = jax.nn.softplus(jnp.einsum('bld,de->ble', x, Wd) + bd)
        Bm = jnp.einsum('bld,ds->bls', x, WB) + bB
        Cm = jnp.einsum('bld,ds->bls', x, WC) + bC
        A = -jnp.exp(A_log)

        def step(h, inps):
            x_t, d_t, B_t, C_t = inps
            bar_A = jnp.exp(jnp.minimum(d_t[:, :, None] * A, 2.0))
            bar_B = jnp.clip(d_t[:, :, None] * B_t[:, None, :], -2.0, 2.0)
            h = jnp.clip(bar_A * h + bar_B * x_t[:, :, None], -100.0, 100.0)
            y = jnp.sum(h * C_t[:, None, :], axis=-1) + x_t * D_param
            return (h, y)
        h0 = jnp.zeros((Bb, d, STATE), x.dtype)
        xs = (jnp.swapaxes(x, 0, 1), jnp.swapaxes(delta, 0, 1), jnp.swapaxes(Bm, 0, 1), jnp.swapaxes(Cm, 0, 1))
        _, ys = jax.lax.scan(step, h0, xs)
        ssm_out = jnp.swapaxes(ys, 0, 1)
        flat = ssm_out.reshape(-1, d)
        routing = jax.nn.softmax(flat @ Wr + br, axis=1)
        top1_w = jnp.max(routing, axis=1)
        top1_i = jnp.argmax(routing, axis=1)
        hid = jax.nn.silu(jnp.einsum('nd,edf->enf', flat, up_w) + up_b[:, None, :])
        all_out = jnp.einsum('enf,efd->end', hid, down_w) + down_b[:, None, :]
        sel = jnp.take_along_axis(jnp.swapaxes(all_out, 0, 1), top1_i[:, None, None], axis=1)[:, 0, :]
        moe_out = (sel * top1_w[:, None]).reshape(Bb, Ll, d)
        out = ssm_out + moe_out
        mu = jnp.mean(out, axis=-1, keepdims=True)
        var = jnp.mean((out - mu) ** 2, axis=-1, keepdims=True)
        return (out - mu) * jax.lax.rsqrt(var + EPS) * ln_w + ln_b

    def _L0_ffn_ref(x, shared_up, shared_down, routed_up, routed_down, router_w):
        import jax, jax.numpy as jnp
        import numpy as np
        H_DIM, E_DIM = (128, 64)
        N_SHARED, N_ROUTED, TOP_K = (2, 16, 4)
        B, S = (4, 256)
        b, s, h = x.shape
        xt = x.reshape(-1, h)
        up_s = jnp.einsum('th,seh->tse', xt, shared_up)
        shared = jnp.einsum('tse,she->th', jax.nn.gelu(up_s, approximate=False), shared_down)
        probs = jax.nn.softmax(xt @ router_w.T, axis=-1)
        topk_p, topk_i = jax.lax.top_k(probs, TOP_K)
        gate = jnp.zeros_like(probs).at[jnp.arange(xt.shape[0])[:, None], topk_i].add(topk_p)
        up_r = jnp.einsum('th,reh->tre', xt, routed_up)
        act = jax.nn.gelu(up_r, approximate=False) * gate[:, :, None]
        routed = jnp.einsum('tre,rhe->th', act, routed_down)
        return (shared + routed).reshape(b, s, h)

    def _L1_attn_ref(x, Wqkv, bqkv, Wr, br):
        import math
        import jax, jax.numpy as jnp
        import numpy as np
        HEADS = 16
        REL_WINDOW = 128
        b, s, d = x.shape
        h = HEADS
        hd = d // h
        w = REL_WINDOW
        scale = math.sqrt(d / h)
        qkv = (x @ Wqkv.T + bqkv).reshape(b, s, h, 3 * hd)
        q, k, v = jnp.split(qkv, 3, axis=-1)
        q = q.transpose(0, 2, 1, 3)
        k = k.transpose(0, 2, 1, 3)
        v = v.transpose(0, 2, 1, 3)
        content = jnp.einsum('bhik,bhjk->bhij', q, k) / scale
        idx = jnp.arange(s)
        offsets = jnp.clip(idx[None, :] - idx[:, None], -w, w) + w
        rp = jnp.einsum('bhik,rk->bhir', q, Wr) + br
        pos = jnp.take_along_axis(rp, jnp.broadcast_to(offsets, (b, h, s, s)), axis=-1)
        attn = jax.nn.softmax(content + pos, axis=-1)
        out = jnp.einsum('bhij,bhjk->bhik', attn, v)
        return out.transpose(0, 2, 1, 3).reshape(b, s, d)

    def _L1_ffn_ref(x, gate, W1, b1, W2, b2, Ws1, bs1, Ws2, bs2):
        import jax, jax.numpy as jnp
        import numpy as np
        NUM_EXPERTS = 8
        CAP_FACTOR = 1.0
        MIN_CAP = 8
        G, S, D = x.shape
        E = gate.shape[1]
        T = G * S
        capacity = max(MIN_CAP, int(CAP_FACTOR * T / E))
        logits = jnp.einsum('gsd,de->gse', x, gate)
        probs = jax.nn.softmax(logits, axis=-1)
        flat_probs = probs.transpose(2, 0, 1).reshape(E, T)
        scores, token_idx = jax.lax.top_k(flat_probs, k=capacity)
        scores = jnp.where(scores > -100000000.0, scores, 0.0)
        flat_x = x.reshape(T, D)
        tok = flat_x[token_idx]
        h = jax.nn.gelu(jnp.einsum('ecd,edh->ech', tok, W1) + b1[:, None, :])
        out_tok = jnp.einsum('ech,ehd->ecd', h, W2) + b2[:, None, :]
        scaled = out_tok * scores[..., None]
        routed = jnp.zeros_like(flat_x).at[token_idx.reshape(-1)].add(scaled.reshape(E * capacity, D)).reshape(G, S, D)
        shared = jax.nn.gelu(jnp.einsum('gsd,dh->gsh', x, Ws1) + bs1)
        shared = jnp.einsum('gsh,hd->gsd', shared, Ws2) + bs2
        return routed + shared

    def _L2_attn_ref(xq, xk, xv, time_decay, time_first, time_mix_k, time_mix_v, time_mix_r, Wk, Wv, Wr, Wo):
        import jax, jax.numpy as jnp
        import numpy as np
        from jax import lax
        RWKV_K_CLAMP = 60.0
        RWKV_K_EPS = 1e-08
        B, T, C = xq.shape
        x = xq
        xx = jnp.pad(x, ((0, 0), (1, 0), (0, 0)))[:, :T]
        k = jnp.einsum('btc,dc->btd', x * time_mix_k + xx * (1 - time_mix_k), Wk)
        v = jnp.einsum('btc,dc->btd', x * time_mix_v + xx * (1 - time_mix_v), Wv)
        r = jnp.einsum('btc,dc->btd', x * time_mix_r + xx * (1 - time_mix_r), Wr)
        sr = jax.nn.sigmoid(r)
        kc = jnp.exp(jnp.minimum(k, RWKV_K_CLAMP)).transpose(0, 2, 1)
        vc = v.transpose(0, 2, 1)
        kv = kc * vc
        curve = jnp.arange(T - 1, dtype=jnp.float32) - (T - 2)
        time_w = jnp.concatenate([jnp.exp(time_decay) * curve[None, :], time_first], axis=-1)
        w = jnp.exp(time_w)[:, None, :]

        def dconv(a):
            ap = jnp.pad(a, ((0, 0), (0, 0), (T - 1, 0)))
            return lax.conv_general_dilated(ap, w, (1,), 'VALID', feature_group_count=C, dimension_numbers=('NCH', 'OIH', 'NCH'))
        wkv = dconv(kv)
        wk = dconv(kc) + RWKV_K_EPS
        out = sr * (wkv / wk).transpose(0, 2, 1)
        return jnp.einsum('btc,dc->btd', out, Wo)

    def _L2_ffn_ref(x, Wqkv, q_scale, k_scale, Wo, ln_g, ln_b, W1, b1, W2, b2):
        import jax, jax.numpy as jnp
        import numpy as np
        DIM = 128
        DEPTH = 6
        HEADS = 16
        DIM_HEAD = 64
        WINDOW = 32
        INNER = HEADS * DIM_HEAD
        DIM_INNER = int(DIM * 4 * 2 / 3)
        QK_SCALE = 8.0

        def shift_tokens(t):
            a, s = jnp.split(t, 2, -1)
            s = jnp.pad(s, ((0, 0), (1, 0), (0, 0)))[:, :-1]
            return jnp.concatenate([a, s], -1)

        def l2norm(t):
            return t / jnp.maximum(jnp.linalg.norm(t, axis=-1, keepdims=True), 1e-12)

        def rotate_half(x):
            x1, x2 = jnp.split(x, 2, -1)
            return jnp.concatenate([-x2, x1], -1)

        def rotary_tables(n):
            half = jnp.arange(0, DIM_HEAD, 2, dtype=jnp.float32)
            inv_freq = 1.0 / 10000.0 ** (half / DIM_HEAD)
            t = jnp.arange(n, dtype=jnp.float32)
            freqs = t[:, None] * inv_freq[None, :]
            freqs = jnp.concatenate([freqs, freqs], -1)
            base_scale = (half + 0.4 * DIM_HEAD) / (1.4 * DIM_HEAD)
            power = (t - n // 2) / (WINDOW // 2)
            scale = base_scale[None, :] ** power[:, None]
            scale = jnp.concatenate([scale, scale], -1)
            return (freqs, scale)

        def local_attention(q, k, v):
            b, h, n, d = q.shape
            w = WINDOW
            nw = n // w
            bq = q.reshape(b, h, nw, w, d)
            bk = k.reshape(b, h, nw, w, d)
            bv = v.reshape(b, h, nw, w, d)

            def look(t):
                p = jnp.pad(t, ((0, 0), (0, 0), (1, 0), (0, 0), (0, 0)))
                return jnp.concatenate([p[:, :, :nw], p[:, :, 1:]], axis=3)
            bk2, bv2 = (look(bk), look(bv))
            seq = jnp.arange(n).reshape(nw, w)
            seq_p = jnp.pad(seq, ((1, 0), (0, 0)), constant_values=-1)
            jt = jnp.concatenate([seq_p[:nw], seq_p[1:]], axis=1)
            it = seq[:, :, None]
            jb = jt[:, None, :]
            mask = (it < jb) | (it > jb + w) | (jb == -1)
            sim = jnp.einsum('bhwie,bhwje->bhwij', bq, bk2) * QK_SCALE
            sim = jnp.where(mask, -jnp.finfo(sim.dtype).max, sim)
            attn = jax.nn.softmax(sim, -1)
            out = jnp.einsum('bhwij,bhwje->bhwie', attn, bv2)
            return out.reshape(b, h, n, d)

        def attn_layer(x, Wqkv, qs, ksc, Wo):
            b, n, _ = x.shape
            qkv = x @ Wqkv
            q, k, v = jnp.split(qkv, 3, -1)
            sh = lambda t: t.reshape(b, n, HEADS, DIM_HEAD).transpose(0, 2, 1, 3)
            q, k, v = (sh(q), sh(k), sh(v))
            q = l2norm(q) * qs
            k = l2norm(k) * ksc
            freqs, scale = rotary_tables(n)
            cos, sin = (jnp.cos(freqs), jnp.sin(freqs))
            q = q * cos * scale + rotate_half(q) * sin * scale
            inv = 1.0 / scale
            k = k * cos * inv + rotate_half(k) * sin * inv
            out = local_attention(q, k, v)
            out = out.transpose(0, 2, 1, 3).reshape(b, n, INNER)
            return out @ Wo

        def ffn_layer(x, g, bln, W1, b1, W2, b2):
            mu = x.mean(-1, keepdims=True)
            var = ((x - mu) ** 2).mean(-1, keepdims=True)
            xn = (x - mu) / jnp.sqrt(var + 1e-05) * g + bln
            hg = xn @ W1 + b1
            a, gate = jnp.split(hg, 2, -1)
            return a * jax.nn.gelu(gate, approximate=False) @ W2 + b2
        for i in range(DEPTH):
            x = attn_layer(shift_tokens(x), Wqkv[i], q_scale[i], k_scale[i], Wo[i]) + x
            x = ffn_layer(shift_tokens(x), ln_g[i], ln_b[i], W1[i], b1[i], W2[i], b2[i]) + x
        return x

    def _L3_attn_ref(x, qw, kw, vw, ow):
        import jax, jax.numpy as jnp
        import numpy as np
        D_MODEL, N_HEADS, BATCH, SEQ = (128, 16, 2, 256)

        def get_freqs(seq, n_dim):
            inv_freq = 1.0 / 10000.0 ** (jnp.arange(0, n_dim, 2, dtype=jnp.float32) / n_dim)
            pos = jnp.arange(seq, dtype=jnp.float32)
            return pos[:, None] * inv_freq[None, :]

        def rope(x, freq):
            cos = jnp.cos(freq)[None, :, None, :]
            sin = jnp.sin(freq)[None, :, None, :]
            x1, x2 = (x[..., ::2], x[..., 1::2])
            r1 = x1 * cos - x2 * sin
            r2 = x1 * sin + x2 * cos
            return jnp.stack([r1, r2], axis=-1).reshape(x.shape)
        batch, seq, dim = x.shape
        n_heads = N_HEADS
        n_dim = dim // n_heads
        Q = (x @ qw).astype(jnp.float32).reshape(batch, seq, n_heads, n_dim)
        K = (x @ kw).astype(jnp.float32).reshape(batch, seq, n_heads, n_dim)
        V = (x @ vw).astype(jnp.float32).reshape(batch, seq, n_heads, n_dim)
        freq = get_freqs(seq, n_dim)
        Q = rope(Q, freq)
        K = rope(K, freq)
        Q = jnp.transpose(Q, (0, 2, 1, 3))
        K = jnp.transpose(K, (0, 2, 1, 3))
        V = jnp.transpose(V, (0, 2, 1, 3))
        scale = jnp.sqrt(jnp.float32(n_dim))
        score = jnp.einsum('bhqd,bhkd->bhqk', Q, K) / scale
        causal = jnp.tril(jnp.ones((1, 1, seq, seq), dtype=jnp.float32))
        score = score - 10000000000.0 * (1.0 - causal)
        score = score - jnp.max(score, axis=-1, keepdims=True)
        weights = jax.nn.softmax(score, axis=-1)
        attn = jnp.einsum('bhqk,bhkd->bhqd', weights, V)
        merged = jnp.transpose(attn, (0, 2, 1, 3)).reshape(batch, seq, dim)
        return (merged @ ow).astype(x.dtype)

    def _L3_ffn_ref(x, q_node_w, q_node_b, q_w1, q_b1, q_w2, q_b2, k_node_w, k_node_b, k_w1, k_b1, k_w2, k_b2, v_node_w, v_node_b, v_w1, v_b1, v_w2, v_b2):
        import jax, jax.numpy as jnp
        import numpy as np
        LATENT = 128
        LEAF_W = 64
        DEPTH = 4
        N_LEAVES = 2 ** DEPTH
        N_NODES = 2 ** DEPTH - 1
        B, S = (4, 256)

        def _fff_params(key, prefix):
            ks = jax.random.split(key, 4)
            d, h, l, n = (LATENT, LEAF_W, N_LEAVES, N_NODES)
            s_in = 1.0 / np.sqrt(d).astype(np.float32)
            s_h = 1.0 / np.sqrt(h).astype(np.float32)
            return {f'{prefix}_node_w': jax.random.normal(ks[0], (n, d), jnp.float32) * s_in, f'{prefix}_node_b': jax.random.normal(ks[1], (n,), jnp.float32) * s_in, f'{prefix}_w1': jax.random.normal(ks[2], (l, d, h), jnp.float32) * s_in, f'{prefix}_b1': jnp.zeros((l, h), jnp.float32), f'{prefix}_w2': jax.random.normal(ks[3], (l, h, d), jnp.float32) * s_h, f'{prefix}_b2': jnp.zeros((l, d), jnp.float32)}

        def _fff(x, node_w, node_b, w1, b1, w2, b2):
            Bx, Sx, D = x.shape
            xf = x.reshape(-1, D)
            N = xf.shape[0]
            cur = jnp.zeros((N,), jnp.int32)
            for _ in range(DEPTH):
                pw = node_w[cur]
                score = jnp.einsum('nd,nd->n', xf, pw) + node_b[cur]
                cur = 2 * cur + 1 + (score >= 0).astype(jnp.int32)
            leaf = cur - N_NODES
            sel = jax.nn.one_hot(leaf, N_LEAVES, dtype=xf.dtype)
            hidden_all = jax.nn.relu(jnp.einsum('nd,ldh->lnh', xf, w1) + b1[:, None, :])
            hidden = hidden_all * sel.T[:, :, None]
            out = jnp.einsum('lnh,lho->no', hidden, w2) + sel @ b2
            return out.reshape(Bx, Sx, D)
        q = _fff(x, q_node_w, q_node_b, q_w1, q_b1, q_w2, q_b2)
        k = _fff(x, k_node_w, k_node_b, k_w1, k_b1, k_w2, k_b2)
        v = _fff(x, v_node_w, v_node_b, v_w1, v_b1, v_w2, v_b2)
        scale = 1.0 / np.sqrt(LATENT).astype(np.float32)
        attn = jax.nn.softmax(jnp.einsum('bqd,bkd->bqk', q, k) * scale, axis=-1)
        return jnp.einsum('bqk,bkd->bqd', attn, v)
    x = L0_attn_x
    xn = _layernorm(x, axis=-1)
    x = x + _L0_attn_ref(xn, L0_attn_A_log, L0_attn_D_param, L0_attn_Wd, L0_attn_bd, L0_attn_WB, L0_attn_bB, L0_attn_WC, L0_attn_bC, L0_attn_Wr, L0_attn_br, L0_attn_up_w, L0_attn_up_b, L0_attn_down_w, L0_attn_down_b, L0_attn_ln_w, L0_attn_ln_b) + _L0_ffn_ref(xn, L0_ffn_shared_up, L0_ffn_shared_down, L0_ffn_routed_up, L0_ffn_routed_down, L0_ffn_router_w)
    xn = _layernorm(x, axis=-1)
    x = x + _L1_attn_ref(xn, L1_attn_Wqkv, L1_attn_bqkv, L1_attn_Wr, L1_attn_br) + _L1_ffn_ref(xn, L1_ffn_gate, L1_ffn_W1, L1_ffn_b1, L1_ffn_W2, L1_ffn_b2, L1_ffn_Ws1, L1_ffn_bs1, L1_ffn_Ws2, L1_ffn_bs2)
    xn = _layernorm(x, axis=-1)
    x = x + _L2_attn_ref(xn, L2_attn_xk, L2_attn_xv, L2_attn_time_decay, L2_attn_time_first, L2_attn_time_mix_k, L2_attn_time_mix_v, L2_attn_time_mix_r, L2_attn_Wk, L2_attn_Wv, L2_attn_Wr, L2_attn_Wo) + _L2_ffn_ref(xn, L2_ffn_Wqkv, L2_ffn_q_scale, L2_ffn_k_scale, L2_ffn_Wo, L2_ffn_ln_g, L2_ffn_ln_b, L2_ffn_W1, L2_ffn_b1, L2_ffn_W2, L2_ffn_b2)
    xn = _layernorm(x, axis=-1)
    x = x + _L3_attn_ref(xn, L3_attn_qw, L3_attn_kw, L3_attn_vw, L3_attn_ow) + _L3_ffn_ref(xn, L3_ffn_q_node_w, L3_ffn_q_node_b, L3_ffn_q_w1, L3_ffn_q_b1, L3_ffn_q_w2, L3_ffn_q_b2, L3_ffn_k_node_w, L3_ffn_k_node_b, L3_ffn_k_w1, L3_ffn_k_b1, L3_ffn_k_w2, L3_ffn_k_b2, L3_ffn_v_node_w, L3_ffn_v_node_b, L3_ffn_v_w1, L3_ffn_v_b1, L3_ffn_v_w2, L3_ffn_v_b2)
    return x

_drawn_inputs = setup_inputs


def setup_inputs(seed=0):
    import zlib

    import numpy as np

    out = dict(_drawn_inputs(seed))
    spreads = {'L0_attn_D_param': (1.0, 0.2),
     'L0_attn_bd': (0.0, 0.8),
     'L0_attn_bB': (0.0, 0.1),
     'L0_attn_bC': (0.0, 0.1),
     'L0_attn_br': (0.0, 0.558),
     'L0_attn_up_b': (0.0, 0.8),
     'L0_attn_down_b': (0.0, 0.466),
     'L0_attn_ln_w': (1.0, 0.2),
     'L0_attn_ln_b': (0.0, 0.1),
     'L1_ffn_b1': (0.0, 0.8),
     'L1_ffn_b2': (0.0, 0.8),
     'L1_ffn_bs1': (0.0, 0.727),
     'L1_ffn_bs2': (0.0, 0.1),
     'L2_attn_time_first': (-1.2039728164672852, 0.6),
     'L2_ffn_q_scale': (1.0, 0.6),
     'L2_ffn_k_scale': (1.0, 0.6),
     'L2_ffn_ln_g': (1.0, 0.6),
     'L2_ffn_ln_b': (0.0, 0.8),
     'L2_ffn_b1': (0.0, 0.8),
     'L2_ffn_b2': (0.0, 0.1),
     'L3_ffn_q_b1': (0.0, 0.8),
     'L3_ffn_q_b2': (0.0, 0.8),
     'L3_ffn_k_b1': (0.0, 0.8),
     'L3_ffn_k_b2': (0.0, 0.8),
     'L3_ffn_v_b1': (0.0, 0.8),
     'L3_ffn_v_b2': (0.0, 0.8)}
    factors = {'L0_attn_Wr': 3.897,
     'L0_attn_up_w': 6.189,
     'L0_attn_down_w': 5.658,
     'L0_ffn_router_w': 2.785,
     'L1_attn_bqkv': 5.409,
     'L1_attn_br': 8.0,
     'L1_ffn_gate': 5.896,
     'L1_ffn_W1': 8.0,
     'L1_ffn_W2': 8.0,
     'L2_attn_time_decay': 8.0,
     'L2_attn_time_mix_r': 3.302,
     'L2_ffn_W1': 5.535,
     'L2_ffn_W2': 5.44,
     'L3_attn_qw': 64.0,
     'L3_attn_kw': 64.0,
     'L3_attn_vw': 22.52,
     'L3_attn_ow': 23.383,
     'L3_ffn_q_node_w': 8.0,
     'L3_ffn_q_node_b': 8.0,
     'L3_ffn_q_w1': 8.0,
     'L3_ffn_q_w2': 8.0,
     'L3_ffn_k_node_w': 8.0,
     'L3_ffn_k_node_b': 8.0,
     'L3_ffn_k_w1': 8.0,
     'L3_ffn_k_w2': 8.0,
     'L3_ffn_v_node_w': 4.078,
     'L3_ffn_v_node_b': 8.0,
     'L3_ffn_v_w1': 5.051}
    for name, (base, spread) in spreads.items():
        noise = np.random.default_rng([zlib.crc32(name.encode()), seed]).standard_normal(out[name].shape)
        drawn = base * np.exp(spread * noise) if base else spread * noise
        out[name] = jnp.asarray(drawn.astype(out[name].dtype))
    for name, factor in factors.items():
        out[name] = (out[name] * factor).astype(out[name].dtype)
    return out
```

```python
from collections import namedtuple
from contextlib import ExitStack, contextmanager

import numpy as np
import concourse.bass as bass
from concourse import mybir

P = 128
B, T = 2, 1024
N = B * T
TILES = N // P
QW = 512
QUARTERS = N // QW
FIRST_SEM = 120

F32 = mybir.dt.float32
BF16 = mybir.dt.bfloat16
ALU = mybir.AluOpType
ACT = mybir.ActivationFunctionType
AX_X = mybir.AxisListType.X
BF16_NP = mybir.dt.np(BF16)



@contextmanager
def stage(nc, *names):
    sems = [nc.alloc_semaphore(n, num=FIRST_SEM + i) for i, n in enumerate(names)]
    with nc.Block() as block:
        yield block, Names(**dict(zip(names, sems)))
    nc.all_engine_barrier(sems_to_clear=range(FIRST_SEM, FIRST_SEM + len(sems)))
    for s in sems:
        nc.release_semaphore(s)


def Names(**things):
    return namedtuple("Names", things)(**things)


class Chain:

    def __init__(self, eng, sem):
        self.eng, self.sem, self.n = eng, sem, 0

    def __call__(self, ins):
        self.n += 1
        ins.then_inc(self.sem, 1)
        self.eng.wait_ge(self.sem, self.n)


class Memory:

    def __init__(self, nc, ctx):
        self.nc, self.ctx = nc, ctx

    def sb(self, name, shape, dt=F32):
        return self.ctx.enter_context(self.nc.sbuf_tensor(name, shape, dt))

    def ps(self, name, shape, dt=F32):
        return self.ctx.enter_context(self.nc.psum_tensor(name, shape, dt))


def cols(i, width):
    return slice(i * width, (i + 1) * width)



def layer_norm(nc, K, name, src, dst, eps=1e-5, gain=None, offset=None, add_to=None):
    with ExitStack() as ctx:
        M = Memory(nc, ctx)
        centred = M.sb(f"{name}_centred", [P, QUARTERS, QW])
        squares = M.sb(f"{name}_squares", [P, 2, QW])
        spread = M.sb(f"{name}_spread", [P, 2, QW])
        root = M.sb(f"{name}_root", [P, 2, QW])
        mean_ps = M.ps(f"{name}_mean_ps", [P, 2, QW])
        var_ps = M.ps(f"{name}_var_ps", [P, 2, QW])
        with stage(nc, "mean_ready", "centred_ready", "squared", "var_ready", "shifted",
                   "rooted", "normed", "dve_chain") as (block, S):

            @block.tensor
            def _(pe):
                for q in range(QUARTERS + 1):
                    if q < QUARTERS:
                        if q >= 2:
                            pe.wait_ge(S.centred_ready, q - 1)
                        pe.matmul(mean_ps[:, q % 2], K.mean[:], src[:, cols(q, QW)], start=True,
                                  stop=True).then_inc(S.mean_ready, 1)
                    if q >= 1:
                        pe.wait_ge(S.squared, q)
                        if q >= 3:
                            pe.wait_ge(S.shifted, q - 2)
                        pe.matmul(var_ps[:, (q - 1) % 2], K.mean[:], squares[:, (q - 1) % 2],
                                  start=True, stop=True).then_inc(S.var_ready, 1)

            @block.scalar
            def _(act):
                for q in range(QUARTERS + 1):
                    if q < QUARTERS:
                        act.wait_ge(S.centred_ready, q + 1)
                        if q >= 2:
                            act.wait_ge(S.var_ready, q - 1)
                        act.activation(squares[:, q % 2], centred[:, q], ACT.Square).then_inc(S.squared, 1)
                    if q >= 1:
                        act.wait_ge(S.shifted, q)
                        if q >= 3:
                            act.wait_ge(S.normed, q - 2)
                        act.activation(root[:, (q - 1) % 2], spread[:, (q - 1) % 2],
                                       ACT.Sqrt).then_inc(S.rooted, 1)

            @block.vector
            def _(dve):
                chain = Chain(dve, S.dve_chain)
                for q in range(QUARTERS + 2):
                    if q < QUARTERS:
                        dve.wait_ge(S.mean_ready, q + 1)
                        dve.tensor_tensor(centred[:, q], src[:, cols(q, QW)], mean_ps[:, q % 2],
                                          ALU.subtract).then_inc(S.centred_ready, 1)
                    if 1 <= q <= QUARTERS:
                        dve.wait_ge(S.var_ready, q)
                        if q >= 3:
                            dve.wait_ge(S.rooted, q - 2)
                        dve.tensor_scalar(spread[:, (q - 1) % 2], var_ps[:, (q - 1) % 2], eps, None,
                                          ALU.add).then_inc(S.shifted, 1)
                    if q >= 2:
                        r = q - 2
                        dve.wait_ge(S.rooted, r + 1)
                        inverse = root[:, r % 2]
                        chain(dve.reciprocal(inverse, inverse))
                        dve.wait_ge(S.centred_ready, r + 1)
                        out = dst[:, cols(r, QW)]
                        if gain is None:
                            dve.tensor_tensor(out, centred[:, r], inverse, ALU.mult).then_inc(S.normed, 1)
                        else:
                            chain(dve.scalar_tensor_tensor(out=centred[:, r], in0=centred[:, r],
                                                           scalar=gain, in1=inverse,
                                                           op0=ALU.mult, op1=ALU.mult))
                            if add_to is None:
                                dve.tensor_scalar(out, centred[:, r], offset, None,
                                                  ALU.add).then_inc(S.normed, 1)
                            else:
                                dve.scalar_tensor_tensor(out=out, in0=centred[:, r], scalar=offset,
                                                         in1=add_to[:, cols(r, QW)], op0=ALU.add,
                                                         op1=ALU.add).then_inc(S.normed, 1)



def router_probs(nc, K, name, flat, weight, bias_row, experts, probs):
    with ExitStack() as ctx:
        M = Memory(nc, ctx)
        wide = TILES * experts
        logits = M.ps(f"{name}_logits", [P, QW])
        top = M.sb(f"{name}_top", [P, TILES])
        total = M.sb(f"{name}_total", [P, TILES])
        lg = logits[:, 0:wide].rearrange("p (t e) -> p t e", e=experts)
        with stage(nc, "logits_ready", "shifted", "exps_ready", "dve_chain") as (block, S):

            @block.tensor
            def _(pe):
                for t in range(TILES):
                    last = pe.matmul(lg[:, t], flat[:, cols(t, P)], weight, start=True,
                                     stop=bias_row is None)
                    if bias_row is not None:
                        last = pe.matmul(lg[:, t], K.ones[0:1, 0:P], bias_row, start=False, stop=True)
                last.then_inc(S.logits_ready, 1)

            @block.vector
            def _(dve):
                chain = Chain(dve, S.dve_chain)
                dve.wait_ge(S.logits_ready, 1)
                chain(dve.tensor_reduce(top[:], lg, AX_X, ALU.max))
                spread = top[:].unsqueeze(2).to_broadcast([P, TILES, experts])
                dve.tensor_tensor(probs[:], lg, spread, ALU.subtract).then_inc(S.shifted, 1)
                dve.wait_ge(S.exps_ready, 1)
                chain(dve.tensor_reduce(total[:], probs[:], AX_X, ALU.add))
                chain(dve.reciprocal(total[:], total[:]))
                spread = total[:].unsqueeze(2).to_broadcast([P, TILES, experts])
                chain(dve.tensor_tensor(probs[:], probs[:], spread, ALU.mult))

            @block.scalar
            def _(act):
                act.wait_ge(S.shifted, 1)
                act.activation(probs[:], probs[:], ACT.Exp).then_inc(S.exps_ready, 1)


def keep_top(nc, name, probs, experts, k):
    with ExitStack() as ctx:
        M = Memory(nc, ctx)
        rank = M.sb(f"{name}_rank", [P, TILES, experts])
        ahead = M.sb(f"{name}_ahead", [P, 2, TILES, experts])
        with stage(nc, "compared", "counted") as (block, S):

            @block.vector
            def _(dve):
                n = 0
                dve.memset(rank[:], 0.0).then_inc(S.counted, 1)
                for e in range(experts):
                    it = probs[:, :, e:e + 1]
                    if e >= 2:
                        dve.wait_ge(S.counted, e)
                    if e > 0:
                        n += 1
                        dve.tensor_tensor(ahead[:, e % 2, :, 0:e], it.to_broadcast([P, TILES, e]),
                                          probs[:, :, 0:e], ALU.is_gt).then_inc(S.compared, 1)
                    n += 1
                    dve.tensor_tensor(ahead[:, e % 2, :, e:], it.to_broadcast([P, TILES, experts - e]),
                                      probs[:, :, e:], ALU.is_ge).then_inc(S.compared, 1)
                    dve.wait_ge(S.compared, n)
                    dve.wait_ge(S.counted, e + 1)
                    dve.tensor_tensor(rank[:], rank[:], ahead[:, e % 2], ALU.add).then_inc(S.counted, 1)
                dve.wait_ge(S.counted, experts + 1)
                dve.scalar_tensor_tensor(out=probs[:], in0=rank[:], scalar=k + 0.5, in1=probs[:],
                                         op0=ALU.is_lt, op1=ALU.mult).then_inc(S.counted, 1)
                dve.wait_ge(S.counted, experts + 2)


def to_rows(nc, K, name, table, rows, dst):
    with ExitStack() as ctx:
        M = Memory(nc, ctx)
        turned = M.ps(f"{name}_turned", [P, QUARTERS, QW])
        per = QW // P
        with stage(nc, "turned_ready", "copied") as (block, S):

            @block.tensor
            def _(pe):
                for t in range(TILES):
                    ins = pe.transpose(turned[0:rows, t // per, cols(t % per, P)], table[:, t],
                                       K.ident[:])
                    if t % per == per - 1:
                        ins.then_inc(S.turned_ready, 1)

            @block.vector
            def _(dve):
                for q in range(QUARTERS):
                    dve.wait_ge(S.turned_ready, q + 1)
                    dve.tensor_copy(dst[0:rows, cols(q, QW)], turned[0:rows, q]).then_inc(S.copied, 1)
                dve.wait_ge(S.copied, QUARTERS)



def mlp(nc, K, name, src, dst, chunks, func, gates=None, gate_rows=0, out_bias=None, add=True):
    n_chunks = len(chunks)
    ring = 4
    gated = [c[3] is not None for c in chunks]
    gated_until = [sum(gated[:i]) for i in range(n_chunks + 1)]
    group = []
    for i, c in enumerate(chunks):
        new = i == 0 or chunks[i - 1][4] != c[4] or not gated[i - 1]
        group.append((group[-1] if group else -1) + (1 if gated[i] and new else 0))
    starts = [gated[i] and (i == 0 or group[i] != group[i - 1]) for i in range(n_chunks)]
    last_gated = {g: max(i for i in range(n_chunks) if gated[i] and group[i] == g)
                  for g in set(group) if g >= 0}
    with ExitStack() as ctx:
        M = Memory(nc, ctx)
        x_q = M.sb(f"{name}_x", [P, QW])
        g_q = M.sb(f"{name}_g", [P, QW])
        hidden = M.sb(f"{name}_hidden", [P, ring, QW])
        scaled = M.sb(f"{name}_scaled", [P, ring, QW])
        h_ps = M.ps(f"{name}_h_ps", [P, 2, QW])
        g_ps = M.ps(f"{name}_g_ps", [P, 2, QW])
        y_ps = M.ps(f"{name}_y_ps", [P, QW])
        with nc.Fori(0, QUARTERS) as q, stage(
                nc, "x_loaded", "h_ready", "g_ready", "h_done", "h_scaled", "y_added",
                "y_ready", "y_stored") as (block, S):
            loads = 2 if gates is not None else 1

            @block.gpsimd
            def _(pool):
                pool.tensor_copy(x_q[:], src[:, bass.ts(q, QW)]).then_inc(S.x_loaded, 1)
                if gates is not None:
                    pool.tensor_copy(g_q[0:gate_rows], gates[0:gate_rows, bass.ts(q, QW)]) \
                        .then_inc(S.x_loaded, 1)

            @block.tensor
            def _(pe):
                def hidden_product(c):
                    w1, _, _, select, _ = chunks[c]
                    if starts[c]:
                        g = group[c]
                        if g >= 2:
                            pe.wait_ge(S.h_scaled, gated_until[last_gated[g - 2] + 1])
                        pe.matmul(g_ps[:, g % 2], select, g_q[0:gate_rows], start=True,
                                  stop=True).then_inc(S.g_ready, 1)
                    if c >= 2:
                        pe.wait_ge(S.h_done, c - 1)
                    pe.matmul(h_ps[:, c % 2], w1, x_q[:], start=True, stop=True).then_inc(S.h_ready, 1)

                def output_product(c):
                    if gated[c]:
                        pe.wait_ge(S.h_scaled, gated_until[c + 1])
                    else:
                        pe.wait_ge(S.h_done, c + 1)
                    h = (scaled if gated[c] else hidden)[:, c % ring]
                    return pe.matmul(y_ps[:], chunks[c][2], h, start=(c == 0),
                                     stop=(c == n_chunks - 1 and out_bias is None)) \
                        .then_inc(S.y_added, 1)

                pe.wait_ge(S.x_loaded, loads)
                for c in range(n_chunks + 2):
                    if c < n_chunks:
                        hidden_product(c)
                    if c >= 2:
                        output_product(c - 2)
                if out_bias is not None:
                    pe.matmul(y_ps[:], out_bias, g_q[0:gate_rows], start=False, stop=True) \
                        .then_inc(S.y_ready, 1)

            @block.scalar
            def _(act):
                for c in range(n_chunks):
                    act.wait_ge(S.h_ready, c + 1)
                    if c >= ring:
                        act.wait_ge(S.y_added, c - ring + 1)
                    b1 = chunks[c][1]
                    kw = {} if b1 is None else {"bias": b1}
                    act.activation(hidden[:, c % ring], h_ps[:, c % 2], func, **kw).then_inc(S.h_done, 1)

            @block.vector
            def _(dve):
                for c in range(n_chunks):
                    if not gated[c]:
                        continue
                    dve.wait_ge(S.h_done, c + 1)
                    if starts[c]:
                        dve.wait_ge(S.g_ready, group[c] + 1)
                    if c >= ring:
                        dve.wait_ge(S.y_added, c - ring + 1)
                    dve.tensor_tensor(scaled[:, c % ring], hidden[:, c % ring], g_ps[:, group[c] % 2],
                                      ALU.mult).then_inc(S.h_scaled, 1)
                if out_bias is not None:
                    dve.wait_ge(S.y_ready, 1)
                else:
                    dve.wait_ge(S.y_added, n_chunks)
                out = dst[:, bass.ts(q, QW)]
                if add:
                    dve.tensor_tensor(out, out, y_ps[:], ALU.add).then_inc(S.y_stored, 1)
                else:
                    dve.tensor_copy(out, y_ps[:]).then_inc(S.y_stored, 1)
                dve.wait_ge(S.y_stored, 1)



def load(nc, name, pairs):
    with stage(nc, "loaded") as (block, S):
        half = (len(pairs) + 1) // 2

        @block.sync
        def _(sp):
            for dst, src in pairs[:half]:
                sp.dma_start(dst, src).then_inc(S.loaded, 16)
            sp.wait_ge(S.loaded, 16 * len(pairs))

        @block.scalar
        def _(act):
            for dst, src in pairs[half:]:
                act.dma_start(dst, src).then_inc(S.loaded, 16)


SHARED0, ROUTED0, WIDE0, TOP0 = 2, 16, 64, 4


def block0_ffn(nc, K, W, xn, x):
    with ExitStack() as ctx:
        M = Memory(nc, ctx)
        pairs = ROUTED0 // 2
        up = M.sb("b0f_up", [P, pairs + 1, P])
        down = M.sb("b0f_down", [P, pairs + 1, P])
        rw = M.sb("b0f_router", [P, ROUTED0])
        gates = M.sb("b0f_gates", [ROUTED0, N])
        load(nc, "b0f", [(up[:], W["b0f_up"]), (down[:], W["b0f_down"]), (rw[:], W["b0f_router"])])
        with ExitStack() as inner:
            probs = Memory(nc, inner).sb("b0f_probs", [P, TILES, ROUTED0])
            router_probs(nc, K, "b0f", xn, rw[:], None, ROUTED0, probs)
            keep_top(nc, "b0f", probs, ROUTED0, TOP0)
            to_rows(nc, K, "b0f", probs, ROUTED0, gates)
        chunks = [(up[:, c], None, down[:, c], K.pick16[:, c], c) for c in range(pairs)]
        chunks.append((up[:, pairs], None, down[:, pairs], None, -1))
        mlp(nc, K, "b0f", xn, x, chunks, ACT.Gelu, gates, ROUTED0)



STATES = 16
H_LIMIT = 100.0


def ssm_states(nc, K, w, name, xn, delta, flat, peak, stepwise):
    units = [(s, q) for s in range(STATES) for q in range(QUARTERS)]
    per_seq = T // QW
    with ExitStack() as ctx:
        M = Memory(nc, ctx)
        decay = M.sb(f"{name}_decay", [P, 3, QW])
        raw = M.sb(f"{name}_raw", [P, 2, QW])
        drive = M.sb(f"{name}_drive", [P, 2, QW])
        h = M.sb(f"{name}_h", [P, 3, QW])
        hc = M.sb(f"{name}_hc", [P, 3, QW])
        peaks = M.sb(f"{name}_peaks", [P, len(units)])
        b_ps = M.ps(f"{name}_b_ps", [P, 2, QW])
        c_ps = M.ps(f"{name}_c_ps", [P, 2, QW])
        y_ps = M.ps(f"{name}_y_ps", [P, QUARTERS, QW])
        with stage(nc, "b_ready", "c_ready", "decay_ready", "clipped", "drive_ready", "state_ready",
                   "peak_read", "hc_ready", "y_added", "dve_chain") as (block, S):

            @block.tensor
            def _(pe):
                for u in range(len(units) + 2):
                    if u < len(units):
                        s, q = units[u]
                        if u >= 2:
                            pe.wait_ge(S.clipped, u - 1)
                            pe.wait_ge(S.hc_ready, u - 1)
                        pe.matmul(b_ps[:, u % 2], w.wb[:, s:s + 1].to_broadcast([P, P]),
                                  xn[:, cols(q, QW)], start=True, stop=True).then_inc(S.b_ready, 1)
                        pe.matmul(c_ps[:, u % 2], w.wc[:, s:s + 1].to_broadcast([P, P]),
                                  xn[:, cols(q, QW)], start=True, stop=True).then_inc(S.c_ready, 1)
                    if u >= 2:
                        s, q = units[u - 2]
                        pe.wait_ge(S.hc_ready, u - 1)
                        pe.matmul(y_ps[:, q], K.ident[:], hc[:, (u - 2) % 3], start=(s == 0),
                                  stop=(s == STATES - 1)).then_inc(S.y_added, 1)

            @block.scalar
            def _(act):
                for u, (s, q) in enumerate(units):
                    if u >= 3:
                        act.wait_ge(S.state_ready, u - 2)
                    act.activation(decay[:, u % 3], delta[:, cols(q, QW)], ACT.Exp,
                                   scale=w.a[:, s:s + 1]).then_inc(S.decay_ready, 1)

            @block.gpsimd
            def _(pool):
                for u, (s, q) in enumerate(units):
                    pool.wait_ge(S.clipped, u + 1)
                    if u >= 2:
                        pool.wait_ge(S.state_ready, u - 1)
                    pool.tensor_tensor(drive[:, u % 2], raw[:, u % 2], xn[:, cols(q, QW)], ALU.mult) \
                        .then_inc(S.drive_ready, 1)

            @block.vector
            def _(dve):
                chain = Chain(dve, S.dve_chain)

                def drive_factor(u):
                    s, q = units[u]
                    dve.wait_ge(S.b_ready, u + 1)
                    if u >= 2:
                        dve.wait_ge(S.drive_ready, u - 1)
                    chain(dve.scalar_tensor_tensor(out=raw[:, u % 2], in0=b_ps[:, u % 2],
                                                   scalar=w.bb[:, s:s + 1], in1=delta[:, cols(q, QW)],
                                                   op0=ALU.add, op1=ALU.mult))
                    dve.tensor_scalar(raw[:, u % 2], raw[:, u % 2], 2.0, -2.0, ALU.min, ALU.max) \
                        .then_inc(S.clipped, 1)

                def scan(u):
                    s, q = units[u]
                    initial = 0.0 if q % per_seq == 0 else h[:, (u - 1) % 3, QW - 1:QW]
                    dve.wait_ge(S.drive_ready, u + 1)
                    dve.wait_ge(S.decay_ready, u + 1)
                    if u >= 3:
                        dve.wait_ge(S.peak_read, u - 2)
                    dve.tensor_tensor_scan(h[:, u % 3], decay[:, u % 3], drive[:, u % 2], initial,
                                           ALU.mult, ALU.add).then_inc(S.state_ready, 1)

                def walk(u):
                    s, q = units[u]
                    now, dec, drv = h[:, u % 3], decay[:, u % 3], drive[:, u % 2]
                    dve.wait_ge(S.drive_ready, u + 1)
                    dve.wait_ge(S.decay_ready, u + 1)
                    if q % per_seq == 0:
                        chain(dve.tensor_copy(now[:, 0:1], drv[:, 0:1]))
                    else:
                        chain(dve.scalar_tensor_tensor(out=now[:, 0:1], in0=h[:, (u - 1) % 3, QW - 1:QW],
                                                       scalar=dec[:, 0:1], in1=drv[:, 0:1],
                                                       op0=ALU.mult, op1=ALU.add))
                    chain(dve.tensor_scalar(now[:, 0:1], now[:, 0:1], H_LIMIT, -H_LIMIT,
                                            ALU.min, ALU.max))
                    with dve.Fori(1, QW) as t:
                        dve.drain()
                        dve.tensor_tensor(now[:, bass.ds(t, 1)], now[:, bass.ds(t - 1, 1)],
                                          dec[:, bass.ds(t, 1)], ALU.mult)
                        dve.drain()
                        dve.tensor_tensor(now[:, bass.ds(t, 1)], now[:, bass.ds(t, 1)],
                                          drv[:, bass.ds(t, 1)], ALU.add)
                        dve.drain()
                        dve.tensor_scalar(now[:, bass.ds(t, 1)], now[:, bass.ds(t, 1)], H_LIMIT,
                                          -H_LIMIT, ALU.min, ALU.max)
                    dve.drain()
                    dve.tensor_copy(now[:, 0:1], now[:, 0:1]).then_inc(S.state_ready, 1)

                def output(u):
                    s, q = units[u]
                    dve.wait_ge(S.state_ready, u + 1)
                    dve.tensor_reduce(peaks[:, u:u + 1], h[:, u % 3], AX_X, ALU.max,
                                      apply_absolute_value=True).then_inc(S.peak_read, 1)
                    dve.wait_ge(S.c_ready, u + 1)
                    if u >= 3:
                        dve.wait_ge(S.y_added, u - 2)
                    dve.scalar_tensor_tensor(out=hc[:, u % 3], in0=c_ps[:, u % 2],
                                             scalar=w.bc[:, s:s + 1], in1=h[:, u % 3],
                                             op0=ALU.add, op1=ALU.mult).then_inc(S.hc_ready, 1)

                for u in range(len(units) + 1):
                    if u < len(units):
                        drive_factor(u)
                    if u >= 1:
                        (walk if stepwise else scan)(u - 1)
                        output(u - 1)
                for q in range(QUARTERS):
                    dve.wait_ge(S.y_added, len(units) - QUARTERS + q + 1)
                    chain(dve.scalar_tensor_tensor(out=flat[:, cols(q, QW)], in0=xn[:, cols(q, QW)],
                                                   scalar=w.d[:], in1=y_ps[:, q], op0=ALU.mult,
                                                   op1=ALU.add))
                dve.wait_ge(S.peak_read, len(units))
                chain(dve.tensor_reduce(peak, peaks[:], AX_X, ALU.max))


def block0_attn(nc, K, W, xn, x):
    with ExitStack() as ctx:
        M = Memory(nc, ctx)
        wd = M.sb("b0a_wd", [P, P])
        small = M.sb("b0a_small", [P, 5 * STATES + 8])
        w = Names(wb=small[:, 0:16], wc=small[:, 16:32], bb=small[:, 32:48],
                            bc=small[:, 48:64], a=small[:, 64:80], d=small[:, 80:81],
                            bd=small[:, 81:82], ln_w=small[:, 82:83], ln_b=small[:, 83:84])
        flat = M.sb("b0a_flat", [P, N])
        peak = M.sb("b0a_peak", [P, 1])
        load(nc, "b0a", [(wd[:], W["b0a_wd"]), (small[:], W["b0a_small"])])
        with ExitStack() as inner:
            delta = Memory(nc, inner).sb("b0a_delta", [P, N])
            softplus_delta(nc, K, w, wd, xn, delta)
            ssm_states(nc, K, w, "b0s", xn, delta, flat, peak[:], stepwise=False)
            over = clipped_somewhere(nc, K, peak)
            with nc.If(over > 0):
                ssm_states(nc, K, w, "b0w", xn, delta, flat, peak[:], stepwise=True)
            with nc.Else():
                nc.all_engine_barrier()
        with ExitStack() as inner:
            I = Memory(nc, inner)
            up = I.sb("b0m_up", [P, 4, 4, P])
            down = I.sb("b0m_down", [P, 4, 4, P])
            b1 = I.sb("b0m_b1", [P, 16])
            b2 = I.sb("b0m_b2", [4, P])
            rw = I.sb("b0m_router", [P, 4])
            rb = I.sb("b0m_router_b", [1, 4])
            gates = I.sb("b0m_gates", [4, N])
            moe = I.sb("b0m_out", [P, N])
            load(nc, "b0m", [(up[:], W["b0m_up"]), (down[:], W["b0m_down"]), (b1[:], W["b0m_b1"]),
                             (b2[:], W["b0m_b2"]), (rw[:], W["b0m_router"]), (rb[:], W["b0m_router_b"])])
            with ExitStack() as rt:
                probs = Memory(nc, rt).sb("b0m_probs", [P, TILES, 4])
                router_probs(nc, K, "b0m", flat, rw[:], rb[:], 4, probs)
                keep_top(nc, "b0m", probs, 4, 1)
                to_rows(nc, K, "b0m", probs, 4, gates)
            chunks = [(up[:, e, c], b1[:, 4 * e + c:4 * e + c + 1], down[:, e, c],
                       K.pick4[:, e], e) for e in range(4) for c in range(4)]
            mlp(nc, K, "b0m", flat, moe, chunks, ACT.Silu, gates, 4, b2[:], add=False)
            add_tokens(nc, flat[:], moe[:])
        layer_norm(nc, K, "b0n", flat, x, gain=w.ln_w, offset=w.ln_b, add_to=x)


def add_tokens(nc, dst, src):
    with stage(nc, "added") as (block, S):

        @block.vector
        def _(dve):
            dve.tensor_tensor(dst, dst, src, ALU.add).then_inc(S.added, 1)
            dve.wait_ge(S.added, 1)


def softplus_delta(nc, K, w, wd, xn, delta):
    with ExitStack() as ctx:
        M = Memory(nc, ctx)
        u_ps = M.ps("sp_u", [P, QUARTERS, QW])
        tail = M.sb("sp_tail", [P, QUARTERS, QW])
        with stage(nc, "u_ready", "tail_ready", "stored", "act_chain") as (block, S):

            @block.tensor
            def _(pe):
                for q in range(QUARTERS):
                    pe.matmul(u_ps[:, q], wd[:], xn[:, cols(q, QW)], start=True, stop=True) \
                        .then_inc(S.u_ready, 1)

            @block.scalar
            def _(act):
                chain = Chain(act, S.act_chain)
                act.wait_ge(S.u_ready, QUARTERS)
                chain(act.activation(tail[:], u_ps[:], ACT.Abs, bias=w.bd))
                chain(act.activation(tail[:], tail[:], ACT.Exp, scale=-1.0))
                act.activation(tail[:], tail[:], ACT.Ln, bias=1.0).then_inc(S.tail_ready, 1)
                chain(act.activation(w.a, w.a, ACT.Exp))
                chain(act.mul(w.a, w.a, -1.0))

            @block.vector
            def _(dve):
                dve.wait_ge(S.u_ready, QUARTERS)
                dve.wait_ge(S.act_chain, 1)
                dve.tensor_scalar(delta[:], u_ps[:].rearrange("p q n -> p (q n)"), w.bd, 0.0,
                                  ALU.add, ALU.max).then_inc(S.stored, 1)
                dve.wait_ge(S.tail_ready, 1)
                dve.wait_ge(S.stored, 1)
                dve.tensor_tensor(delta[:], delta[:], tail[:].rearrange("p q n -> p (q n)"),
                                  ALU.add).then_inc(S.stored, 1)
                dve.wait_ge(S.stored, 2)


def clipped_somewhere(nc, K, peak):
    flag = K.flag
    with ExitStack() as ctx:
        M = Memory(nc, ctx)
        row = M.ps("peak_row", [P, QW])
        within = M.sb("peak_within", [1, 2])
        with stage(nc, "row_ready", "dve_chain") as (block, S):

            @block.tensor
            def _(pe):
                pe.transpose(row[0:1, 0:P], peak[:], K.ident[:]).then_inc(S.row_ready, 1)

            @block.vector
            def _(dve):
                chain = Chain(dve, S.dve_chain)
                dve.wait_ge(S.row_ready, 1)
                chain(dve.tensor_reduce(within[:, 0:1], row[0:1, 0:P], AX_X, ALU.max))
                chain(dve.tensor_scalar(within[:, 1:2], within[:, 0:1], H_LIMIT, None, ALU.is_le))
                chain(dve.tensor_scalar(flag[:], within[:, 1:2], -1.0, 1.0, ALU.mult, ALU.add))
    return nc.values_load(flag[:], min_val=0, max_val=1)



EXPERTS1, CAPACITY1, HIDDEN1 = 8, N // 8, 512


def choose_tokens(nc, gates):
    with ExitStack() as ctx:
        M = Memory(nc, ctx)
        left = M.sb("b1f_left", [EXPERTS1, N])
        best = M.sb("b1f_best", [EXPERTS1, 8])
        with stage(nc, "dve_chain") as (block, S):

            @block.vector
            def _(dve):
                chain = Chain(dve, S.dve_chain)
                chain(dve.tensor_copy(left[:], gates[0:EXPERTS1]))
                for _ in range(CAPACITY1 // 8):
                    chain(dve.max(best[:], left[:]))
                    chain(dve.match_replace(left[:], best[:], left[:], -1.0))
                chain(dve.scalar_tensor_tensor(out=gates[0:EXPERTS1], in0=left[:], scalar=0.0,
                                               in1=gates[0:EXPERTS1], op0=ALU.is_lt, op1=ALU.mult))


def block1_ffn(nc, K, W, xn, x):
    with ExitStack() as ctx:
        M = Memory(nc, ctx)
        parts = HIDDEN1 // P
        up = M.sb("b1f_up", [P, EXPERTS1 + 1, parts, P])
        down = M.sb("b1f_down", [P, EXPERTS1 + 1, parts, P])
        b1 = M.sb("b1f_b1", [P, (EXPERTS1 + 1) * parts])
        b2 = M.sb("b1f_b2", [EXPERTS1 + 1, P])
        gate_w = M.sb("b1f_gate_w", [P, EXPERTS1])
        gates = M.sb("b1f_gates", [EXPERTS1 + 1, N])
        load(nc, "b1f", [(up[:], W["b1f_up"]), (down[:], W["b1f_down"]), (b1[:], W["b1f_b1"]),
                         (b2[:], W["b1f_b2"]), (gate_w[:], W["b1f_gate_w"]),
                         (gates[EXPERTS1:EXPERTS1 + 1], W["c_one_row"])])
        with ExitStack() as rt:
            probs = Memory(nc, rt).sb("b1f_probs", [P, TILES, EXPERTS1])
            router_probs(nc, K, "b1f", xn, gate_w[:], None, EXPERTS1, probs)
            to_rows(nc, K, "b1f", probs, EXPERTS1, gates)
        choose_tokens(nc, gates)
        chunks = [(up[:, e, c], b1[:, parts * e + c:parts * e + c + 1], down[:, e, c],
                   K.pick9[:, e] if e < EXPERTS1 else None, e)
                  for e in range(EXPERTS1 + 1) for c in range(parts)]
        mlp(nc, K, "b1f", xn, x, chunks, ACT.Gelu_apprx_tanh, gates, EXPERTS1 + 1, b2[:])



K_CLAMP, K_EPS = 60.0, 1e-8


def block2_attn(nc, K, W, xn, x):
    with ExitStack() as ctx:
        M = Memory(nc, ctx)
        w = M.sb("b2a_w", [P, 4, P])
        small = M.sb("b2a_small", [P, 5])
        inv_mix = M.sb("b2a_inv_mix", [P, 3])
        lam = M.sb("b2a_lam", [P, QW])
        mixed = M.sb("b2a_mixed", [P, 3, QW])
        part = M.sb("b2a_part", [P, 3, QW])
        kc = M.sb("b2a_kc", [P, QW])
        kv = M.sb("b2a_kv", [P, QW])
        sr = M.sb("b2a_sr", [P, QW])
        sums = M.sb("b2a_sums", [P, 2, 1 + QW])
        den = M.sb("b2a_den", [P, QW])
        out = M.sb("b2a_out", [P, QW])
        prev = M.sb("b2a_prev", [P, 1 + N])
        kvr_ps = M.ps("b2a_kvr_ps", [P, 3, QW])
        o_ps = M.ps("b2a_o_ps", [P, QW])
        load(nc, "b2a", [(w[:], W["b2a_w"]), (small[:], W["b2a_small"])])
        with stage(nc, "decayed", "mixed_ready", "projected", "act_done", "kc_clamped", "out_ready",
                   "o_ready", "stored", "dve_chain", "act_chain") as (block, S):

            @block.scalar
            def _(act):
                chain = Chain(act, S.act_chain)
                chain(act.activation(small[:, 0:1], small[:, 0:1], ACT.Exp))
                chain(act.activation(small[:, 0:1], small[:, 0:1], ACT.Exp, scale=-1.0))
                act.activation(small[:, 1:2], small[:, 1:2], ACT.Exp).then_inc(S.decayed, 1)
                for q in range(QUARTERS):
                    act.wait_ge(S.kc_clamped, q + 1)
                    act.activation(kc[:], kc[:], ACT.Exp).then_inc(S.act_done, 1)
                    act.activation(sr[:], kvr_ps[:, 2], ACT.Sigmoid).then_inc(S.act_done, 1)

            @block.tensor
            def _(pe):
                for q in range(QUARTERS):
                    pe.wait_ge(S.mixed_ready, q + 1)
                    if q >= 1:
                        pe.wait_ge(S.out_ready, q)
                    for i in range(3):
                        ins = pe.matmul(kvr_ps[:, i], w[:, i], mixed[:, i], start=True, stop=True)
                    ins.then_inc(S.projected, 1)
                    pe.wait_ge(S.out_ready, q + 1)
                    pe.matmul(o_ps[:], w[:, 3], out[:], start=True, stop=True).then_inc(S.o_ready, 1)

            @block.vector
            def _(dve):
                chain = Chain(dve, S.dve_chain)
                chain(dve.tensor_scalar(inv_mix[:], small[:, 2:5], -1.0, 1.0, ALU.mult, ALU.add))
                chain(dve.tensor_copy(prev[:, 1:], xn[:]))
                for b in range(B):
                    chain(dve.memset(prev[:, b * T:b * T + 1], 0.0))
                chain(dve.memset(lam[:], 0.0))
                dve.wait_ge(S.decayed, 1)
                chain(dve.tensor_scalar(lam[:], lam[:], small[:, 0:1], None, ALU.add))
                for q in range(QUARTERS):
                    x_q, prev_q = xn[:, cols(q, QW)], prev[:, cols(q, QW)]
                    for i in range(3):
                        chain(dve.tensor_scalar(part[:, i], x_q, small[:, 2 + i:3 + i], None, ALU.mult))
                    for i in range(3):
                        ins = dve.scalar_tensor_tensor(out=mixed[:, i], in0=prev_q,
                                                       scalar=inv_mix[:, i:i + 1], in1=part[:, i],
                                                       op0=ALU.mult, op1=ALU.add)
                        if i < 2:
                            chain(ins)
                    ins.then_inc(S.mixed_ready, 1)
                    dve.wait_ge(S.projected, q + 1)
                    dve.tensor_scalar(kc[:], kvr_ps[:, 0], K_CLAMP, None, ALU.min) \
                        .then_inc(S.kc_clamped, 1)
                    dve.wait_ge(S.act_done, 2 * q + 2)
                    chain(dve.tensor_tensor(kv[:], kc[:], kvr_ps[:, 1], ALU.mult))
                    for i, a in enumerate((kv, kc)):
                        if q % (T // QW) == 0:
                            chain(dve.memset(sums[:, i, 0:1], 0.0))
                        else:
                            chain(dve.tensor_copy(sums[:, i, 0:1], sums[:, i, QW:QW + 1]))
                        chain(dve.tensor_tensor_scan(sums[:, i, 1:], lam[:], a[:], sums[:, i, 0:1],
                                                     ALU.mult, ALU.add))
                    chain(dve.scalar_tensor_tensor(out=den[:], in0=kc[:], scalar=small[:, 1:2],
                                                   in1=sums[:, 1, 0:QW], op0=ALU.mult, op1=ALU.add))
                    chain(dve.tensor_scalar(den[:], den[:], K_EPS, None, ALU.add))
                    chain(dve.reciprocal(den[:], den[:]))
                    chain(dve.scalar_tensor_tensor(out=kv[:], in0=kv[:], scalar=small[:, 1:2],
                                                   in1=sums[:, 0, 0:QW], op0=ALU.mult, op1=ALU.add))
                    chain(dve.tensor_tensor(kv[:], kv[:], den[:], ALU.mult))
                    if q >= 1:
                        dve.wait_ge(S.o_ready, q)
                    dve.tensor_tensor(out[:], kv[:], sr[:], ALU.mult).then_inc(S.out_ready, 1)
                    dve.wait_ge(S.o_ready, q + 1)
                    x_out = x[:, cols(q, QW)]
                    dve.tensor_tensor(x_out, x_out, o_ps[:], ALU.add).then_inc(S.stored, 1)
                dve.wait_ge(S.stored, QUARTERS)



HEADS, HD = 16, 8
PAIRS = HEADS // 2
WINDOW1 = 128
BAND = 3 * P
QT = T // P
SLOTS_Q = (0, 0, 1, 0, 1, 2)
SLOTS_K = (0, 1, 0, 2, 1, 0)
ONES_AT = HD * len(SLOTS_Q)


def split_parts(chain, dve, src, parts, rest):
    chain(dve.tensor_copy(parts[0], src))
    chain(dve.tensor_tensor(rest, src, parts[0], ALU.subtract))
    chain(dve.tensor_copy(parts[1], rest))
    chain(dve.tensor_tensor(rest, rest, parts[1], ALU.subtract))
    chain(dve.tensor_copy(parts[2], rest))


def masked_parts(chain, dve, parts, masks, out):
    chain(dve.tensor_scalar(out, parts[0], masks[:, 0:1], None, ALU.mult))
    for i in (1, 2):
        chain(dve.scalar_tensor_tensor(out=out, in0=parts[i], scalar=masks[:, i:i + 1], in1=out,
                                       op0=ALU.mult, op1=ALU.add))


def head_attention(nc, K, W, key, xn, x, relative):
    kinds = 3 if relative else 1
    with ExitStack() as ctx:
        M = Memory(nc, ctx)
        n_w = 3 if relative else 6
        w = M.sb(f"{key}_w", [P, n_w, P])
        small = M.sb(f"{key}_small", [P, 12])
        stack_q = M.sb(f"{key}_pick_q", [P, PAIRS, 3, P], BF16)
        stack_k = M.sb(f"{key}_pick_k", [P, PAIRS, 3, P], BF16)
        x_b = M.sb(f"{key}_x_b", [P, T])
        parts = M.sb(f"{key}_parts", [P, 1 + kinds, 3, T], BF16)
        values = M.sb(f"{key}_values", [P, QT, HEADS, HD + 1])
        merged = M.sb(f"{key}_merged", [P, QT, PAIRS, 2 * HD])
        bias_cols = M.sb(f"{key}_bias_cols", [P, 1 + kinds])
        v_bias = M.sb(f"{key}_v_bias", [1, P])
        pick_f = M.sb(f"{key}_pick_f", [P, 2, 3 * P], BF16)
        v_f = M.sb(f"{key}_v_f", [P, QT, 2, HD + 1])
        qk = M.sb(f"{key}_qk", [P, 1 + kinds, T], BF16)
        table = M.sb(f"{key}_table", [P, QW], BF16) if relative else None
        pairs = [(w[:], W[f"{key}_w"]), (small[:], W[f"{key}_small"]),
                 (stack_q[:], W["c_stack_q"]), (stack_k[:], W["c_stack_k"])]
        if relative:
            pairs.append((v_bias[:], W[f"{key}_v_bias"]))
        load(nc, key, pairs)
        if relative:
            position_table(nc, W, key, small, table, bias_cols)
        with nc.Fori(0, B) as b:
            project_heads(nc, K, W, key, xn, b, x_b, w, small, parts, values, v_bias, relative)
            with nc.Fori(0, PAIRS) as pair:
                stack_pair(nc, K, key, pair, parts, stack_q, stack_k, pick_f, values, v_f, qk,
                           bias_cols, relative)
                attend_pair(nc, K, key, pair, qk, table, v_f, merged, relative)
            merge_heads(nc, K, key, b, merged, x, w, relative)


def position_table(nc, W, key, small, table, bias_cols):
    with ExitStack() as ctx:
        M = Memory(nc, ctx)
        full = M.sb(f"{key}_full", [P, QW + 2])
        rest = M.sb(f"{key}_rest", [P, QW + 2])
        parts = M.sb(f"{key}_table_parts", [P, 3, QW + 2], BF16)
        chosen = M.sb(f"{key}_chosen", [P, QW + 2])
        with stage(nc, "loaded", "dve_chain") as (block, S):

            @block.sync
            def _(sp):
                sp.dma_start(full[:], W[f"{key}_positions"]).then_inc(S.loaded, 16)

            @block.vector
            def _(dve):
                chain = Chain(dve, S.dve_chain)
                dve.wait_ge(S.loaded, 16)
                split_parts(chain, dve, full[:], [parts[:, i] for i in range(3)], rest[:])
                masked_parts(chain, dve, [parts[:, i] for i in range(3)], small[:, 6:9], chosen[:])
                chain(dve.tensor_copy(table[:], chosen[:, 0:QW]))
                chain(dve.tensor_copy(bias_cols[:, 0:1], small[:, 9:10]))
                chain(dve.memset(bias_cols[:, 1:2], 0.0))
                chain(dve.tensor_copy(bias_cols[:, 2:4], chosen[:, QW:QW + 2]))


def project_heads(nc, K, W, key, xn, b, x_b, w, small, parts, values, v_bias, relative):
    with ExitStack() as ctx:
        M = Memory(nc, ctx)
        half = T // QW
        q_f = M.sb(f"{key}_q_f", [P, T])
        k_f = M.sb(f"{key}_k_f", [P, 3, T])
        rest = M.sb(f"{key}_split_rest", [P, T])
        turn = M.sb(f"{key}_turn", [P, 2, T]) if not relative else None
        qk_ps = M.ps(f"{key}_qk_ps", [P, 3, half, QW])
        v_ps = M.ps(f"{key}_v_ps", [P, 2, 4, P])
        with stage(nc, "x_loaded", "turn_loaded", "q_ready", "k_ready", "v_ready", "rotated_ready",
                   "values_ready", "ps_free", "dve_chain", "v_copied") as (block, S):

            @block.gpsimd
            def _(pool):
                pool.tensor_copy(x_b[:], xn[:, bass.ts(b, T)]).then_inc(S.x_loaded, 1)
                pool.memset(values[:, :, :, HD:HD + 1], 1.0).then_inc(S.v_copied, 1)
                pool.wait_ge(S.v_copied, 1)

            if not relative:
                @block.sync
                def _(sp):
                    sp.dma_start(turn[:], W["c_turn"]).then_inc(S.turn_loaded, 16)

            @block.tensor
            def _(pe):
                pe.wait_ge(S.x_loaded, 1)

                def product(i, slot):
                    for j in range(half):
                        ins = pe.matmul(qk_ps[:, slot, j], w[:, i], x_b[:, cols(j, QW)], start=True,
                                        stop=True)
                    return ins

                product(0, 0).then_inc(S.q_ready, 1)
                product(1, 1).then_inc(S.k_ready, 1)
                if not relative:
                    product(3, 2).then_inc(S.rotated_ready, 1)
                    pe.wait_ge(S.ps_free, 1)
                    product(4, 2).then_inc(S.rotated_ready, 1)
                for t in range(QT):
                    ins = pe.matmul(v_ps[:, t // 4, t % 4], x_b[:, cols(t, P)], w[:, 2], start=True,
                                    stop=not relative)
                    if relative:
                        ins = pe.matmul(v_ps[:, t // 4, t % 4], K.ones[0:1, 0:P], v_bias[:],
                                        start=False, stop=True)
                ins.then_inc(S.v_ready, 1)

            @block.vector
            def _(dve):
                chain = Chain(dve, S.dve_chain)
                flat = lambda slot: qk_ps[:, slot].rearrange("p j n -> p (j n)")
                dve.wait_ge(S.q_ready, 1)
                if relative:
                    chain(dve.tensor_scalar(q_f[:], flat(0), small[:, 0:1], None, ALU.add))
                    dve.wait_ge(S.k_ready, 1)
                    chain(dve.tensor_scalar(k_f[:, 0], flat(1), small[:, 1:2], float(HD) ** -0.5,
                                            ALU.add, ALU.mult))
                    chain(dve.tensor_scalar(k_f[:, 1], k_f[:, 0], small[:, 3:4], None, ALU.add))
                    chain(dve.tensor_scalar(k_f[:, 2], k_f[:, 0], small[:, 4:5], None, ALU.add))
                else:
                    dve.wait_ge(S.turn_loaded, 16)
                    for i, dst in enumerate((q_f[:], k_f[:, 0])):
                        if i == 1:
                            dve.wait_ge(S.k_ready, 1)
                        chain(dve.tensor_tensor(dst, flat(i), turn[:, 0], ALU.mult))
                        dve.wait_ge(S.rotated_ready, i + 1)
                        ins = dve.tensor_tensor(rest[:], flat(2), turn[:, 1], ALU.mult)
                        ins.then_inc(S.ps_free, 1)
                        dve.wait_ge(S.ps_free, i + 1)
                        chain(dve.tensor_tensor(dst, dst, rest[:], ALU.add))
                    chain(dve.tensor_scalar(k_f[:, 0], k_f[:, 0], float(HD) ** -0.5, None, ALU.mult))
                split_parts(chain, dve, q_f[:], [parts[:, 0, i] for i in range(3)], rest[:])
                for kind in range(parts.shape[1] - 1):
                    split_parts(chain, dve, k_f[:, kind], [parts[:, 1 + kind, i] for i in range(3)],
                                rest[:])
                dve.wait_ge(S.v_ready, 1)
                chain(dve.tensor_copy(values[:, :, :, 0:HD],
                                      v_ps[:].rearrange("p a c (h d) -> p (a c) h d", d=HD)))


def stack_pair(nc, K, key, pair, parts, stack_q, stack_k, pick_f, values, v_f, qk, bias_cols,
               relative):
    with ExitStack() as ctx:
        M = Memory(nc, ctx)
        half = T // QW
        s_ps = M.ps(f"{key}_stack_ps", [P, 4, half, QW])
        n = qk.shape[1]
        with stage(nc, "picked", "stacked", "copied", "v_copied") as (block, S):

            @block.gpsimd
            def _(pool):
                pool.tensor_copy(pick_f[:, 0].rearrange("p (i n) -> p i n", i=3),
                                 stack_q[:, bass.ds(pair, 1)].squeeze()).then_inc(S.picked, 1)
                pool.tensor_copy(pick_f[:, 1].rearrange("p (i n) -> p i n", i=3),
                                 stack_k[:, bass.ds(pair, 1)].squeeze()).then_inc(S.picked, 1)
                pool.tensor_copy(v_f[:], values[:, :, bass.ds(pair * 2, 2), :]).then_inc(S.v_copied, 1)
                pool.wait_ge(S.v_copied, 1)

            @block.tensor
            def _(pe):
                pe.wait_ge(S.picked, 2)
                for i in range(n):
                    for j in range(half):
                        for part in range(3):
                            ins = pe.matmul(s_ps[:, i, j], pick_f[:, min(i, 1), cols(part, P)],
                                            parts[:, i, part, cols(j, QW)], start=(part == 0),
                                            stop=(part == 2))
                    ins.then_inc(S.stacked, 1)

            @block.scalar
            def _(act):
                for i in range(0, n, 2):
                    act.wait_ge(S.stacked, i + 1)
                    kw = {"bias": bias_cols[:, i:i + 1]} if relative else {}
                    act.activation(qk[:, i], s_ps[:, i].rearrange("p j n -> p (j n)"), ACT.Identity,
                                   **kw).then_inc(S.copied, 1)
                act.wait_ge(S.copied, n)

            @block.vector
            def _(dve):
                for i in range(1, n, 2):
                    dve.wait_ge(S.stacked, i + 1)
                    src = s_ps[:, i].rearrange("p j n -> p (j n)")
                    if relative:
                        dve.tensor_scalar(qk[:, i], src, bias_cols[:, i:i + 1], None, ALU.add) \
                            .then_inc(S.copied, 1)
                    else:
                        dve.tensor_copy(qk[:, i], src).then_inc(S.copied, 1)


def attend_pair(nc, K, key, pair, qk, table, v_f, merged, relative):
    units = [(t, h) for t in range(QT) for h in range(2)]
    n_units = len(units)
    e_lead = 6
    ring = 4
    with ExitStack() as ctx:
        M = Memory(nc, ctx)
        weights = M.sb(f"{key}_weights", [P, 2, T])
        turned = M.sb(f"{key}_turned", [P, 2, QT, P])
        neg_max = M.sb(f"{key}_neg_max", [P, n_units])
        recip = M.sb(f"{key}_recip", [P, QT, 2])
        s_ps = M.ps(f"{key}_s_ps", [P, 2, T])
        t_ps = M.ps(f"{key}_t_ps", [P, 2, 4, P])
        o_ps = M.ps(f"{key}_o_ps", [P, QT, 2, HD + 1])
        if relative:
            e_sb = M.sb(f"{key}_e_sb", [P, ring, 2, QW])
            band = M.sb(f"{key}_band", [P, ring, 2, BAND])
            e_ps = M.ps(f"{key}_e_ps", [P, QW])
            scratch = K.scratch
        with stage(nc, "scores_ready", "masked", "max_ready", "exps_ready", "turned_ready",
                   "copied_dve", "copied_act", "out_ready", "e_ready", "e_copied", "e_written",
                   "band_loaded", "dve_chain") as (block, S):

            def width(t):
                return T if relative else (t + 1) * P

            def blocks(t):
                return width(t) // P

            def near(t):
                return max(0, (t - 1) * P), min(T, (t + 2) * P)

            @block.tensor
            def _(pe):
                def positions(n):
                    t, h = units[n]
                    if n >= 1:
                        pe.wait_ge(S.e_copied, n)
                    rows = slice(64 * h, 64 * h + 64)
                    pe.matmul(e_ps[:], qk[rows, 0, cols(t, P)], table[rows, :], start=True,
                              stop=True).then_inc(S.e_ready, 1)

                def scores(n):
                    t, h = units[n]
                    if n >= 2:
                        pe.wait_ge(S.exps_ready, n - 1)
                    rows = slice(64 * h, 64 * h + 64)
                    if relative:
                        lo, hi = near(t)
                        spans = [(0, lo, 2), (lo, hi, 1), (hi, T, 3)]
                    else:
                        spans = [(0, width(t), 1)]
                    cuts = [(max(a, c), min(z, c + QW), kind) for a, z, kind in spans
                            for c in range(0, T, QW) if max(a, c) < min(z, c + QW)]
                    for a, z, kind in cuts:
                        ins = pe.matmul(s_ps[:, n % 2, a:z], qk[rows, 0, cols(t, P)],
                                        qk[rows, kind, a:z], start=True, stop=True)
                    ins.then_inc(S.scores_ready, 1)

                def turn(n):
                    t, h = units[n]
                    pe.wait_ge(S.exps_ready, n + 1)
                    if n >= 1:
                        pe.wait_ge(S.copied_dve, n)
                        pe.wait_ge(S.copied_act, n)
                    for j in range(blocks(t)):
                        ins = pe.transpose(t_ps[:, j // 4, j % 4], weights[:, n % 2, cols(j, P)],
                                           K.ident[:])
                    ins.then_inc(S.turned_ready, 1)

                def weighted(n):
                    t, h = units[n]
                    pe.wait_ge(S.copied_dve, n + 1)
                    pe.wait_ge(S.copied_act, n + 1)
                    for j in range(blocks(t)):
                        ins = pe.matmul(o_ps[:, t, h], turned[:, n % 2, j], v_f[:, j, h],
                                        start=(j == 0), stop=(j == blocks(t) - 1))
                    ins.then_inc(S.out_ready, 1)

                if relative:
                    for n in range(e_lead):
                        positions(n)
                for n in range(n_units + 2):
                    if n < n_units:
                        scores(n)
                    if relative and n + e_lead < n_units:
                        positions(n + e_lead)
                    if 1 <= n <= n_units:
                        turn(n - 1)
                    if n >= 2:
                        weighted(n - 2)

            @block.scalar
            def _(act):
                def copy_positions(n):
                    t, h = units[n]
                    act.wait_ge(S.e_ready, n + 1)
                    if t >= ring:
                        act.wait_ge(S.e_written, 16 * (t - ring + 1))
                    act.activation(e_sb[:, t % ring, h], e_ps[:], ACT.Copy).then_inc(S.e_copied, 1)

                def exps(n):
                    t, h = units[n]
                    act.wait_ge(S.max_ready, n + 1)
                    if n >= 2:
                        act.wait_ge(S.turned_ready, n - 1)
                    act.activation(weights[:, n % 2, 0:width(t)], s_ps[:, n % 2, 0:width(t)], ACT.Exp,
                                   bias=neg_max[:, n:n + 1]).then_inc(S.exps_ready, 1)

                def copy_turned(n):
                    t, h = units[n]
                    act.wait_ge(S.turned_ready, n + 1)
                    if n >= 2:
                        act.wait_ge(S.out_ready, n - 1)
                    if blocks(t) > 4:
                        act.activation(turned[:, n % 2, 4:blocks(t)], t_ps[:, 1, 0:blocks(t) - 4],
                                       ACT.Copy).then_inc(S.copied_act, 1)
                    else:
                        act.sem_inc(S.copied_act, 1)

                if relative:
                    for n in range(e_lead):
                        copy_positions(n)
                for n in range(n_units + 1):
                    if n < n_units:
                        exps(n)
                    if relative and n + e_lead < n_units:
                        copy_positions(n + e_lead)
                    if n >= 1:
                        copy_turned(n - 1)

            if relative:
                @block.sync
                def _(sp):
                    for t in range(QT):
                        sp.wait_ge(S.e_copied, 2 * (t + 1))
                        if t >= ring:
                            sp.wait_ge(S.band_loaded, 16 * (t - ring + 1))
                        slot = scratch[t % ring]
                        sp.dma_start(slot.rearrange("h p n -> p h n"), e_sb[:, t % ring]) \
                            .then_inc(S.e_written, 16)
                        sp.wait_ge(S.e_written, 16 * (t + 1))
                        if t >= ring:
                            sp.wait_ge(S.masked, 2 * (t - ring + 1))
                        skewed = bass.AP(slot.tensor, slot.offset + P - 1,
                                         [[QW - 1, P], [P * QW, 2], [1, BAND]])
                        sp.dma_start(band[:, t % ring], skewed).then_inc(S.band_loaded, 16)

            @block.vector
            def _(dve):
                chain = Chain(dve, S.dve_chain)

                def maxima(n):
                    t, h = units[n]
                    dve.wait_ge(S.scores_ready, n + 1)
                    if relative:
                        lo, hi = near(t)
                        at = lo - (t - 1) * P
                        dve.wait_ge(S.band_loaded, 16 * (t + 1))
                        add = band[:, t % ring, h, at:at + hi - lo]
                    else:
                        lo, hi = t * P, (t + 1) * P
                        add = K.causal[:]
                    dve.tensor_tensor(s_ps[:, n % 2, lo:hi], s_ps[:, n % 2, lo:hi], add, ALU.add) \
                        .then_inc(S.masked, 1)
                    dve.wait_ge(S.masked, n + 1)
                    dve.tensor_reduce(neg_max[:, n:n + 1], s_ps[:, n % 2, 0:width(t)], AX_X, ALU.max,
                                      negate=True).then_inc(S.max_ready, 1)

                def copy_turned(n):
                    t, h = units[n]
                    dve.wait_ge(S.turned_ready, n + 1)
                    if n >= 2:
                        dve.wait_ge(S.out_ready, n - 1)
                    k = min(4, blocks(t))
                    dve.tensor_copy(turned[:, n % 2, 0:k], t_ps[:, 0, 0:k]).then_inc(S.copied_dve, 1)

                for n in range(n_units + 1):
                    if n < n_units:
                        maxima(n)
                    if n >= 1:
                        copy_turned(n - 1)
                dve.wait_ge(S.out_ready, n_units)
                chain(dve.reciprocal(recip[:], o_ps[:, :, :, HD]))
                out = merged[:, :, bass.ds(pair, 1), :].rearrange("p t o (h d) -> p t (o h) d", h=2)
                chain(dve.tensor_tensor(out, o_ps[:, :, :, 0:HD],
                                        recip[:].unsqueeze(3).to_broadcast([P, QT, 2, HD]), ALU.mult))


def merge_heads(nc, K, key, b, merged, x, w, relative):
    with ExitStack() as ctx:
        M = Memory(nc, ctx)
        half = T // QW
        rows = M.sb(f"{key}_rows", [P, T])
        m_ps = M.ps(f"{key}_m_ps", [P, half, QW])
        p_ps = M.ps(f"{key}_p_ps", [P, half, QW])
        with stage(nc, "turned_ready", "copied", "projected", "added") as (block, S):

            @block.tensor
            def _(pe):
                for t in range(QT):
                    ins = pe.transpose(m_ps[:, t // 4, cols(t % 4, P)],
                                       merged[:, t].rearrange("p a c -> p (a c)"), K.ident[:])
                ins.then_inc(S.turned_ready, 1)
                if not relative:
                    pe.wait_ge(S.copied, 1)
                    for j in range(half):
                        ins = pe.matmul(p_ps[:, j], w[:, 5], rows[:, cols(j, QW)], start=True,
                                        stop=True)
                    ins.then_inc(S.projected, 1)

            @block.vector
            def _(dve):
                dve.wait_ge(S.turned_ready, 1)
                src = m_ps
                if not relative:
                    dve.tensor_copy(rows[:], m_ps[:].rearrange("p j n -> p (j n)")) \
                        .then_inc(S.copied, 1)
                    dve.wait_ge(S.projected, 1)
                    src = p_ps
                out = x[:, bass.ts(b, T)]
                dve.tensor_tensor(out, out, src[:].rearrange("p j n -> p (j n)"), ALU.add) \
                    .then_inc(S.added, 1)
                dve.wait_ge(S.added, 1)



LEAVES, DEPTH3 = 16, 4
NODES = LEAVES - 1


def walk_tree(nc, K, name, xn, node_w, node_b, reach):
    with ExitStack() as ctx:
        M = Memory(nc, ctx)
        right = M.sb(f"{name}_right", [P, TILES, LEAVES])
        left = M.sb(f"{name}_left", [P, TILES, LEAVES])
        level = M.sb(f"{name}_level", [P, 2, TILES, LEAVES])
        scores = M.ps(f"{name}_scores", [P, TILES, LEAVES])
        with stage(nc, "scores_ready", "dve_chain") as (block, S):

            @block.tensor
            def _(pe):
                for t in range(TILES):
                    pe.matmul(scores[:, t], xn[:, cols(t, P)], node_w, start=True, stop=False)
                    last = pe.matmul(scores[:, t], K.ones[0:1, 0:P], node_b, start=False, stop=True)
                last.then_inc(S.scores_ready, 1)

            @block.vector
            def _(dve):
                chain = Chain(dve, S.dve_chain)
                chain(dve.memset(level[:, 0], 1.0))
                dve.wait_ge(S.scores_ready, 1)
                chain(dve.tensor_scalar(right[:], scores[:], 0.0, None, ALU.is_ge))
                chain(dve.tensor_scalar(left[:], right[:], -1.0, 1.0, ALU.mult, ALU.add))
                for d in range(DEPTH3):
                    n = 1 << d
                    here = level[:, d % 2, :, 0:n]
                    if d == DEPTH3 - 1:
                        below = reach[:]
                    else:
                        below = level[:, (d + 1) % 2, :, 0:2 * n]
                    below = below.rearrange("p t (n two) -> p t n two", two=2)
                    nodes = slice(n - 1, 2 * n - 1)
                    chain(dve.tensor_tensor(below[:, :, :, 0], here, left[:, :, nodes], ALU.mult))
                    chain(dve.tensor_tensor(below[:, :, :, 1], here, right[:, :, nodes], ALU.mult))


def block3_ffn(nc, K, W, xn, x):
    with ExitStack() as ctx:
        M = Memory(nc, ctx)
        qkv = [M.sb(f"b3f_{n}", [P, N]) for n in "qkv"]
        with ExitStack() as inner:
            I = Memory(nc, inner)
            halves = LEAVES // 2
            up = I.sb("b3f_up", [P, halves, P])
            down = I.sb("b3f_down", [P, halves, P])
            b1 = I.sb("b3f_b1", [P, halves])
            b2 = I.sb("b3f_b2", [LEAVES, P])
            node_w = I.sb("b3f_node_w", [P, LEAVES])
            node_b = I.sb("b3f_node_b", [1, LEAVES])
            reach = I.sb("b3f_reach", [P, TILES, LEAVES])
            gates = I.sb("b3f_gates", [LEAVES, N])
            for n, dst in zip("qkv", qkv):
                load(nc, f"b3f_{n}", [(up[:], W[f"b3f_{n}_up"]), (down[:], W[f"b3f_{n}_down"]),
                                      (b1[:], W[f"b3f_{n}_b1"]), (b2[:], W[f"b3f_{n}_b2"]),
                                      (node_w[:], W[f"b3f_{n}_node_w"]),
                                      (node_b[:], W[f"b3f_{n}_node_b"])])
                walk_tree(nc, K, f"b3f_{n}", xn, node_w[:], node_b[:], reach)
                to_rows(nc, K, f"b3f_{n}", reach, LEAVES, gates)
                chunks = [(up[:, c], b1[:, c:c + 1], down[:, c], K.pick16[:, c], c)
                          for c in range(halves)]
                mlp(nc, K, f"b3f_{n}", xn, dst, chunks, ACT.Relu, gates, LEAVES, b2[:], add=False)
        one_head(nc, K, qkv, x)


def one_head(nc, K, qkv, x):
    q_all, k_all, v_all = qkv
    scale = float(P) ** -0.5
    units = [(b, t) for b in range(B) for t in range(QT)]
    n_units = len(units)
    with ExitStack() as ctx:
        M = Memory(nc, ctx)
        v_rows = M.sb("b3f_v_rows", [P, TILES, P])
        weights = M.sb("b3f_weights", [P, 2, T])
        turned = M.sb("b3f_turned", [P, 2, QT, P])
        stats = M.sb("b3f_stats", [P, 4, n_units])
        s_ps = M.ps("b3f_s_ps", [P, 2, T])
        t_ps = M.ps("b3f_t_ps", [P, 2, 4, P])
        o_ps = M.ps("b3f_o_ps", [P, P])
        with stage(nc, "v_turned", "v_copied", "scores_ready", "max_ready", "exps_ready",
                   "weights_ready", "turned_ready", "copied_act", "copied_dve", "out_ready",
                   "stored", "dve_chain") as (block, S):

            @block.tensor
            def _(pe):
                for t in range(TILES):
                    if t % 8 == 0 and t > 0:
                        pe.wait_ge(S.v_copied, t // 8)
                    ins = pe.transpose(t_ps[:, t % 8 // 4, t % 4], v_all[:, cols(t, P)], K.ident[:])
                    if t % 8 == 7:
                        ins.then_inc(S.v_turned, 1)
                pe.wait_ge(S.v_copied, TILES // 8)
                for n in range(n_units + 2):
                    if n < n_units:
                        b, t = units[n]
                        if n >= 2:
                            pe.wait_ge(S.exps_ready, n - 1)
                        for j in range(T // QW):
                            ins = pe.matmul(s_ps[:, n % 2, cols(j, QW)],
                                            q_all[:, cols(b * QT + t, P)],
                                            k_all[:, cols(b * (T // QW) + j, QW)], start=True,
                                            stop=True)
                        ins.then_inc(S.scores_ready, 1)
                    if 1 <= n <= n_units:
                        m = n - 1
                        pe.wait_ge(S.weights_ready, m + 1)
                        pe.wait_ge(S.copied_dve, m)
                        pe.wait_ge(S.copied_act, m)
                        for j in range(QT):
                            ins = pe.transpose(t_ps[:, j // 4, j % 4], weights[:, m % 2, cols(j, P)],
                                               K.ident[:])
                        ins.then_inc(S.turned_ready, 1)
                    if n >= 2:
                        m = n - 2
                        b, t = units[m]
                        pe.wait_ge(S.copied_dve, m + 1)
                        pe.wait_ge(S.copied_act, m + 1)
                        pe.wait_ge(S.stored, m)
                        for j in range(QT):
                            ins = pe.matmul(o_ps[:], v_rows[:, b * QT + j], turned[:, m % 2, j],
                                            start=(j == 0), stop=(j == QT - 1))
                        ins.then_inc(S.out_ready, 1)

            @block.scalar
            def _(act):
                for n in range(n_units + 1):
                    if n < n_units:
                        act.wait_ge(S.max_ready, n + 1)
                        if n >= 2:
                            act.wait_ge(S.turned_ready, n - 1)
                        act.activation(weights[:, n % 2], s_ps[:, n % 2], ACT.Exp, scale=scale,
                                       bias=stats[:, 1, n:n + 1],
                                       accum_out=stats[:, 2, n:n + 1]).then_inc(S.exps_ready, 1)
                    if n >= 1:
                        m = n - 1
                        act.wait_ge(S.turned_ready, m + 1)
                        if m >= 2:
                            act.wait_ge(S.out_ready, m - 1)
                        act.activation(turned[:, m % 2, 4:], t_ps[:, 1], ACT.Copy) \
                            .then_inc(S.copied_act, 1)

            @block.vector
            def _(dve):
                chain = Chain(dve, S.dve_chain)
                for i in range(TILES // 8):
                    dve.wait_ge(S.v_turned, i + 1)
                    dve.tensor_copy(v_rows[:, 8 * i:8 * i + 8], t_ps[:].rearrange("p a c n -> p (a c) n")) \
                        .then_inc(S.v_copied, 1)
                for n in range(n_units + 2):
                    if n < n_units:
                        dve.wait_ge(S.scores_ready, n + 1)
                        chain(dve.tensor_reduce(stats[:, 0, n:n + 1], s_ps[:, n % 2], AX_X, ALU.max))
                        dve.tensor_scalar(stats[:, 1, n:n + 1], stats[:, 0, n:n + 1], -scale, None,
                                          ALU.mult).then_inc(S.max_ready, 1)
                        dve.wait_ge(S.exps_ready, n + 1)
                        chain(dve.reciprocal(stats[:, 3, n:n + 1], stats[:, 2, n:n + 1]))
                        dve.tensor_scalar(weights[:, n % 2], weights[:, n % 2], stats[:, 3, n:n + 1],
                                          None, ALU.mult).then_inc(S.weights_ready, 1)
                    if 1 <= n <= n_units:
                        m = n - 1
                        dve.wait_ge(S.turned_ready, m + 1)
                        if m >= 2:
                            dve.wait_ge(S.out_ready, m - 1)
                        dve.tensor_copy(turned[:, m % 2, 0:4], t_ps[:, 0]).then_inc(S.copied_dve, 1)
                    if n >= 2:
                        b, t = units[n - 2]
                        dve.wait_ge(S.out_ready, n - 1)
                        out = x[:, cols(b * QT + t, P)]
                        dve.tensor_tensor(out, out, o_ps[:], ALU.add).then_inc(S.stored, 1)
                dve.wait_ge(S.stored, n_units)



LAYERS, HD2, WIN = 6, 64, 32
WINS = P // WIN
INNER = HEADS * HD2
FF, FF_PAD = 341, 384
LEAD = WIN
SEQ_COLS = LEAD + T
QK_SCALE = 8.0


def block2_ffn(nc, K, W, xn, x):
    with ExitStack() as ctx:
        M = Memory(nc, ctx)
        cur_all = M.sb("b2f_cur", [P, 3 * P + N])
        mid_all = M.sb("b2f_mid", [P, 3 * P + N])
        G = Names(
            cur_all=cur_all, mid_all=mid_all, cur=cur_all[:, 2 * P:2 * P + N], mid=mid_all[:, 2 * P:2 * P + N],
            shifted=M.sb("b2f_shifted", [P, B * SEQ_COLS + 3 * (LEAD + P)]),
            wqkv=M.sb("b2f_wqkv", [P, 3 * INNER]), wo=M.sb("b2f_wo", [P, PAIRS, P]),
            w1=M.sb("b2f_w1", [P, 6, P]), w2=M.sb("b2f_w2", [P, 3, P]),
            small=M.sb("b2f_small", [P, 9]), scales=M.sb("b2f_scales", [P, 4, HD2]),
            rotary=M.sb("b2f_rotary", [P, QT, 4, HD2]), mask=M.sb("b2f_mask", [P, QT, HD2]),
            qt=M.sb("b2f_qt", [P, PAIRS, P]), kt=M.sb("b2f_kt", [P, PAIRS, WIN + P]),
            values=M.sb("b2f_values", [P, 2, WINS, PAIRS * HD2]),
            o_sb=M.sb("b2f_o", [P, PAIRS, P]), minus_half=M.sb("b2f_minus_half", [P, 2 * HEADS]), xt=M.sb("b2f_xt", [P, WIN + P]),
            turn=M.sb("b2f_turn", [P, 4, HD2]), mask_t=M.sb("b2f_mask_t", [P, 2, HD2]),
            keep=M.sb("b2f_keep", [P, QT]), keep_t=M.sb("b2f_keep_t", [P, 1]))
        with stage(nc, "copied") as (block, S):

            @block.vector
            def _(dve):
                dve.memset(G.cur_all[:, 0:2 * P], 0.0).then_inc(S.copied, 1)
                dve.memset(G.o_sb[:], 0.0).then_inc(S.copied, 1)
                dve.memset(G.minus_half[:], -0.5).then_inc(S.copied, 1)
                dve.memset(G.qt[:], 0.0).then_inc(S.copied, 1)
                dve.memset(G.values[:], 0.0).then_inc(S.copied, 1)
                dve.memset(G.mask_t[:], 0.0).then_inc(S.copied, 1)
                dve.tensor_copy(G.cur, xn[:]).then_inc(S.copied, 1)
                dve.memset(G.shifted[:], 0.0).then_inc(S.copied, 1)
                dve.memset(G.kt[:], 0.0).then_inc(S.copied, 1)
                dve.wait_ge(S.copied, 9)
        load(nc, "b2f_mask", [(G.mask[:], W["c_local_mask"]), (G.keep[:], W["c_keep"])])
        with nc.Fori(0, LAYERS) as layer:
            layer_weights(nc, W, G, layer)
            with nc.Fori(0, TILES + 2, 2) as first:
                local_tiles(nc, K, G, first)
            shift_tokens(nc, G.mid, G.shifted, 0)
            layer_norm(nc, K, "b2n", G.shifted, G.shifted, gain=G.small[:, 0:1],
                       offset=G.small[:, 1:2])
            gated_ffn(nc, K, G)
        add_tokens(nc, x[:], G.cur)


def shift_tokens(nc, src, dst, lead):
    with stage(nc, "moved") as (block, S):
        step = lead + T

        @block.vector
        def _(dve):
            for b in range(B):
                at = b * step + lead
                dve.tensor_copy(dst[0:64, at:at + T], src[0:64, b * T:(b + 1) * T]).then_inc(S.moved, 1)
                dve.memset(dst[64:P, at:at + 1], 0.0).then_inc(S.moved, 1)

        @block.gpsimd
        def _(pool):
            for b in range(B):
                at = b * step + lead
                pool.tensor_copy(dst[64:P, at + 1:at + T], src[64:P, b * T:(b + 1) * T - 1]) \
                    .then_inc(S.moved, 1)
            pool.wait_ge(S.moved, 3 * B)


def layer_weights(nc, W, G, layer):
    with stage(nc, "loaded", "scaled") as (block, S):

        @block.sync
        def _(sp):
            i = layer
            sp.dma_start(G.wqkv[:], W["b2f_wqkv"][bass.ds(i, 1)].squeeze()).then_inc(S.loaded, 16)
            sp.dma_start(G.wo[:], W["b2f_wo"][bass.ds(i, 1)].squeeze()).then_inc(S.loaded, 16)
            sp.dma_start(G.w1[:], W["b2f_w1"][bass.ds(i, 1)].squeeze()).then_inc(S.loaded, 16)
            sp.dma_start(G.w2[:], W["b2f_w2"][bass.ds(i, 1)].squeeze()).then_inc(S.loaded, 16)
            sp.dma_start(G.small[:], W["b2f_small"][bass.ds(i, 1)].squeeze()).then_inc(S.loaded, 16)
            sp.dma_start(G.scales[:], W["b2f_scales"][bass.ds(i, 1)].squeeze()).then_inc(S.loaded, 16)
            sp.dma_start(G.rotary[:], W["c_rotary2"]).then_inc(S.loaded, 16)

        @block.vector
        def _(dve):
            dve.wait_ge(S.loaded, 16 * 7)
            dve.tensor_tensor(G.rotary[:], G.rotary[:],
                              G.scales[:].unsqueeze(1).to_broadcast([P, QT, 4, HD2]), ALU.mult) \
                .then_inc(S.scaled, 1)
            dve.wait_ge(S.scaled, 1)
    shift_tokens(nc, G.cur, G.shifted, LEAD)


def local_tiles(nc, K, G, first):
    with ExitStack() as ctx:
        M = Memory(nc, ctx)
        sq = M.sb("b2t_sq", [P, 2 * HEADS, HD2])
        part = M.sb("b2t_part", [P, 2 * HEADS, HD2])
        qk = M.sb("b2t_qk", [P, 2 * HEADS, HD2])
        norm = M.sb("b2t_norm", [P, 2 * HEADS])
        prob = M.sb("b2t_prob", [P, PAIRS, 2, HD2])
        top = M.sb("b2t_top", [P, PAIRS, 2])
        total = M.sb("b2t_total", [P, PAIRS, 2])
        pt = M.sb("b2t_pt", [P, PAIRS, P])
        qk_ps = M.ps("b2t_qk_ps", [P, 4, QW])
        s_ps = M.ps("b2t_s_ps", [P, 2, QW])
        w_ps = M.ps("b2t_w_ps", [P, 2, QW])
        with stage(nc, "xt_loaded", "qk_ready", "squared", "inverted", "summed", "normed",
                   "qk_turned", "qt_copied", "kt_carried", "scores_ready", "masked", "shifted",
                   "exps_ready", "probs_ready", "probs_turned", "pt_low", "pt_high", "out_ready",
                   "o_copied", "y_ready", "y_stored", "v_ready", "v_copied", "v_carried",
                   "table_loaded", "mask_loaded", "dve_chain", "pool_chain") as (block, S):
            PER = {"qk_ready": 4, "squared": 4, "normed": 2, "qk_turned": 4, "qt_copied": 4,
                   "probs_turned": 2, "out_ready": 2, "o_copied": 2, "v_copied": 10}

            def due(k, name, n):
                return k * PER.get(name, 1) + n

            @block.gpsimd
            def _(pool):
                chain = Chain(pool, S.pool_chain)
                for k in range(2):
                    tile = first + k
                    if k:
                        pool.wait_ge(S.v_ready, due(k, "v_ready", 0))
                    pool.tensor_copy(G.xt[:], G.shifted[:, bass.ds(tile * P + (tile // QT) * LEAD,
                                                                   WIN + P)]).then_inc(S.xt_loaded, 1)
                    if k:
                        pool.wait_ge(S.normed, due(k, "normed", 0))
                        pool.wait_ge(S.shifted, due(k, "shifted", 0))
                    pool.tensor_copy(G.turn[:], G.rotary[:, bass.ds(tile % QT, 1)].squeeze()) \
                        .then_inc(S.table_loaded, 1)
                    pool.tensor_copy(G.mask_t[:, k], G.mask[:, bass.ds(tile % QT, 1)].squeeze()) \
                        .then_inc(S.mask_loaded, 1)
                    chain(pool.tensor_copy(G.keep_t[:], G.keep[:, bass.ds(tile % QT, 1)]))
                    pool.wait_ge(S.scores_ready, due(k, "scores_ready", 1))
                    pool.tensor_scalar(G.kt[:, :, 0:WIN], G.kt[:, :, P:P + WIN], G.keep_t[:], None,
                                       ALU.mult).then_inc(S.kt_carried, 1)
                    pool.wait_ge(S.summed, due(k, "summed", 1))
                    pool.tensor_tensor(norm[:], norm[:], G.minus_half[:], ALU.pow) \
                        .then_inc(S.inverted, 1)
                    if k:
                        pool.wait_ge(S.out_ready, due(k, "out_ready", 0))
                        pool.wait_ge(S.v_copied, due(k, "v_copied", 0))
                    pool.wait_ge(S.inverted, due(k, "inverted", 1))
                    for h in range(2):
                        pool.tensor_copy(G.values[HD2 * h:HD2 * h + WIN, k, 0],
                                         G.values[HD2 * h + WIN:HD2 * h + 2 * WIN, 1 - k, WINS - 1]) \
                            .then_inc(S.v_carried, 1)
                        pool.wait_ge(S.v_carried, 2 * k + h + 1)

            @block.tensor
            def _(pe):
                for k in range(2):
                    if k:
                        pe.wait_ge(S.qt_copied, due(k, "qt_copied", 0))
                        pe.wait_ge(S.o_copied, due(k, "o_copied", 0))
                    for h in range(2):
                        for p in range(PAIRS):
                            for w in range(WINS):
                                rows = slice(HD2 * h, HD2 * h + HD2)
                                ins = pe.matmul(s_ps[WIN * w:WIN * w + WIN, h, cols(p, HD2)],
                                                G.qt[rows, p, cols(w, WIN)],
                                                G.kt[rows, p, WIN * w:WIN * w + 2 * WIN],
                                                start=True, stop=True)
                    ins.then_inc(S.scores_ready, 1)
                    pe.wait_ge(S.xt_loaded, due(k, "xt_loaded", 1))
                    for j in range(4):
                        pe.matmul(qk_ps[:, j], G.xt[:, WIN:], G.wqkv[:, cols(j, QW)], start=True,
                                  stop=True).then_inc(S.qk_ready, 1)
                    wv = G.wqkv[:, 2 * INNER:].rearrange("k (p h d) -> k p h d", h=2, d=HD2)
                    for h in range(2):
                        ins = pe.matmul(w_ps[:, h], G.xt[:, WIN:], wv[:, :, h], start=True, stop=True)
                    ins.then_inc(S.v_ready, 1)
                    pe.wait_ge(S.masked, due(k, "masked", 1))
                    for p in range(PAIRS):
                        ins = pe.matmul(s_ps[:, 0, 0:P], G.wo[:, p], G.o_sb[:, p], start=(p == 0),
                                        stop=(p == PAIRS - 1))
                    ins.then_inc(S.y_ready, 1)
                    pe.wait_ge(S.probs_ready, due(k, "probs_ready", 1))
                    pe.wait_ge(S.v_copied, due(k, "v_copied", PER["v_copied"]))
                    for p in range(PAIRS):
                        ins = pe.transpose(w_ps[:, p // 4, cols(p % 4, P)],
                                           prob[:, p].rearrange("q h j -> q (h j)"), K.ident[:])
                        if p % 4 == 3:
                            ins.then_inc(S.probs_turned, 1)
                    pe.wait_ge(S.y_stored, due(k, "y_stored", 1))
                    if k:
                        pe.wait_ge(S.v_carried, 2)
                    for p in range(PAIRS):
                        if p == 0:
                            pe.wait_ge(S.pt_low, due(k, "pt_low", 1))
                        if p == 4:
                            pe.wait_ge(S.pt_high, due(k, "pt_high", 1))
                        for h in range(2):
                            rows = slice(HD2 * h, HD2 * h + HD2)
                            for w in range(WINS):
                                at = (p % 4) * P + WIN * w
                                ins = pe.matmul(s_ps[rows, p // 4, at:at + WIN],
                                                G.values[rows, 1 - k, w, cols(p, HD2)],
                                                pt[rows, p, cols(w, WIN)], start=True, stop=True)
                        if p % 4 == 3:
                            ins.then_inc(S.out_ready, 1)
                    for j in range(4):
                        if j % 2 == 0:
                            pe.wait_ge(S.normed, due(k, "normed", j // 2 + 1))
                        for c in range(4):
                            n = 4 * j + c
                            src = qk[:, 2 * n:2 * n + 2].rearrange("t h d -> t (h d)")
                            ins = pe.transpose(qk_ps[:, j, cols(c, P)], src, K.ident[:])
                        ins.then_inc(S.qk_turned, 1)

            @block.scalar
            def _(act):
                for k in range(2):
                    if k:
                        act.wait_ge(S.summed, due(k, "summed", 0))
                    for j in range(4):
                        act.wait_ge(S.qk_ready, due(k, "qk_ready", j + 1))
                        act.activation(sq[:, 8 * j:8 * j + 8].rearrange("t h d -> t (h d)"),
                                       qk_ps[:, j], ACT.Square).then_inc(S.squared, 1)
                    act.wait_ge(S.shifted, due(k, "shifted", 1))
                    act.activation(prob[:], prob[:], ACT.Exp).then_inc(S.exps_ready, 1)
                    act.wait_ge(S.v_ready, due(k, "v_ready", 1))
                    if k:
                        act.wait_ge(S.out_ready, due(k, "out_ready", 0))
                    for h in range(2):
                        for w, src, dst, n in ((1, 0, 0, 64), (3, 64, 0, 64), (2, 32, 0, 32),
                                               (2, 64, 32, 32), (0, 0, 32, 32)):
                            at = HD2 * h + dst
                            act.activation(G.values[at:at + n, k, w], w_ps[src:src + n, h], ACT.Copy) \
                                .then_inc(S.v_copied, 1)
                    act.wait_ge(S.probs_turned, due(k, "probs_turned", 2))
                    if k:
                        act.wait_ge(S.out_ready, due(k, "out_ready", 0))
                    act.activation(pt[:, 4:], w_ps[:, 1], ACT.Copy).then_inc(S.pt_high, 1)
                    act.wait_ge(S.y_ready, due(k, "y_ready", 1))
                    for i in range(2):
                        act.wait_ge(S.out_ready, due(k, "out_ready", i + 1))
                        act.activation(G.o_sb[:, 4 * i:4 * i + 4], s_ps[:, i], ACT.Copy) \
                            .then_inc(S.o_copied, 1)
                    for j in range(4):
                        act.wait_ge(S.qk_turned, due(k, "qk_turned", j + 1))
                        if j < 2:
                            dst = G.qt[:, 4 * j:4 * j + 4]
                        else:
                            act.wait_ge(S.kt_carried, due(k, "kt_carried", 1))
                            dst = G.kt[:, 4 * (j - 2):4 * (j - 2) + 4, WIN:]
                        act.activation(dst, qk_ps[:, j].rearrange("p (c n) -> p c n", c=4), ACT.Copy) \
                            .then_inc(S.qt_copied, 1)
                act.wait_ge(S.qt_copied, 8)

            @block.vector
            def _(dve):
                chain = Chain(dve, S.dve_chain)
                for k in range(2):
                    dve.wait_ge(S.scores_ready, due(k, "scores_ready", 1))
                    if k:
                        dve.wait_ge(S.probs_turned, due(k, "probs_turned", 0))
                        dve.wait_ge(S.mask_loaded, 1)
                    for h in range(2):
                        ins = dve.scalar_tensor_tensor(
                            out=prob[:, :, h], in0=s_ps[:, h].rearrange("q (p j) -> q p j", p=PAIRS),
                            scalar=QK_SCALE,
                            in1=G.mask_t[:, 1 - k].unsqueeze(1).to_broadcast([P, PAIRS, HD2]),
                            op0=ALU.mult, op1=ALU.add)
                        if h == 0:
                            chain(ins)
                    ins.then_inc(S.masked, 1)
                    dve.wait_ge(S.masked, k + 1)
                    chain(dve.tensor_reduce(top[:], prob[:], AX_X, ALU.max))
                    flat = prob[:].rearrange("q p h j -> q (p h) j")
                    bc = lambda a: a[:].rearrange("q p h -> q (p h)").unsqueeze(2).to_broadcast(
                        [P, HEADS, HD2])
                    dve.tensor_tensor(flat, flat, bc(top), ALU.subtract).then_inc(S.shifted, 1)
                    dve.wait_ge(S.squared, due(k, "squared", 4))
                    chain(dve.tensor_reduce(norm[:], sq[:], AX_X, ALU.add))
                    dve.tensor_scalar(norm[:], norm[:], 1e-24, None, ALU.max).then_inc(S.summed, 1)
                    dve.wait_ge(S.exps_ready, due(k, "exps_ready", 1))
                    chain(dve.tensor_reduce(total[:], prob[:], AX_X, ALU.add))
                    chain(dve.reciprocal(total[:], total[:]))
                    dve.tensor_tensor(flat, flat, bc(total), ALU.mult).then_inc(S.probs_ready, 1)
                    dve.wait_ge(S.y_ready, due(k, "y_ready", 1))
                    dve.tensor_tensor(G.mid_all[:, bass.ds((first + k) * P, P)],
                                      G.cur_all[:, bass.ds((first + k) * P, P)], s_ps[:, 0, 0:P],
                                      ALU.add).then_inc(S.y_stored, 1)
                    dve.wait_ge(S.probs_turned, due(k, "probs_turned", 1))
                    if k:
                        dve.wait_ge(S.out_ready, due(k, "out_ready", 0))
                    dve.tensor_copy(pt[:, 0:4], w_ps[:, 0].rearrange("p (a n) -> p a n", a=4)) \
                        .then_inc(S.pt_low, 1)
                    dve.wait_ge(S.table_loaded, due(k, "table_loaded", 1))
                    if k:
                        dve.wait_ge(S.qk_turned, due(k, "qk_turned", 0))
                    raw = qk_ps[:].rearrange("t j n -> t (j n)").rearrange("t (k h d) -> t k h d",
                                                                           k=2, h=HEADS)
                    qk_v = qk[:].rearrange("t (k h) d -> t k h d", k=2)
                    part_v = part[:].rearrange("t (k h) d -> t k h d", k=2)
                    half = HD2 // 2
                    for i in range(2):
                        cos = G.turn[:, 2 * i:2 * i + 1].to_broadcast([P, HEADS, HD2])
                        chain(dve.tensor_tensor(qk_v[:, i], raw[:, i], cos, ALU.mult))
                        for lo, hi in ((0, half), (half, 0)):
                            sin = G.turn[:, 2 * i + 1:2 * i + 2, lo:lo + half].to_broadcast(
                                [P, HEADS, half])
                            chain(dve.tensor_tensor(part_v[:, i, :, lo:lo + half],
                                                    raw[:, i, :, hi:hi + half], sin, ALU.mult))
                        chain(dve.tensor_tensor(qk_v[:, i], qk_v[:, i], part_v[:, i], ALU.add))
                        if i == 0:
                            dve.wait_ge(S.inverted, due(k, "inverted", 1))
                        dve.tensor_tensor(qk_v[:, i], qk_v[:, i],
                                          norm[:, cols(i, HEADS)].unsqueeze(2).to_broadcast(
                                              [P, HEADS, HD2]), ALU.mult).then_inc(S.normed, 1)
                dve.wait_ge(S.normed, 4)


def gated_ffn(nc, K, G):
    chunks = FF_PAD // P
    units = [(q, c) for q in range(QUARTERS) for c in range(chunks)]
    with ExitStack() as ctx:
        M = Memory(nc, ctx)
        gate = M.sb("b2g_gate", [P, 3, QW])
        hidden = M.sb("b2g_hidden", [P, 3, QW])
        a_ps = M.ps("b2g_a_ps", [P, 2, QW])
        g_ps = M.ps("b2g_g_ps", [P, 2, QW])
        y_ps = M.ps("b2g_y_ps", [P, 2, QW])
        with stage(nc, "g_ready", "a_ready", "gelu_ready", "hidden_ready", "y_added",
                   "stored") as (block, S):

            @block.tensor
            def _(pe):
                for u in range(len(units) + 2):
                    if u < len(units):
                        q, c = units[u]
                        if u >= 2:
                            pe.wait_ge(S.hidden_ready, u - 1)
                        x_q = G.shifted[:, cols(q, QW)]
                        pe.matmul(g_ps[:, u % 2], G.w1[:, chunks + c], x_q, start=True, stop=True) \
                            .then_inc(S.g_ready, 1)
                        pe.matmul(a_ps[:, u % 2], G.w1[:, c], x_q, start=True, stop=True) \
                            .then_inc(S.a_ready, 1)
                    if u >= 2:
                        q, c = units[u - 2]
                        pe.wait_ge(S.hidden_ready, u - 1)
                        if c == 0 and q >= 2:
                            pe.wait_ge(S.stored, q - 1)
                        pe.matmul(y_ps[:, q % 2], G.w2[:, c], hidden[:, (u - 2) % 3],
                                  start=(c == 0), stop=(c == chunks - 1)).then_inc(S.y_added, 1)

            @block.scalar
            def _(act):
                for u, (q, c) in enumerate(units):
                    act.wait_ge(S.g_ready, u + 1)
                    if u >= 3:
                        act.wait_ge(S.hidden_ready, u - 2)
                    act.activation(gate[:, u % 3], g_ps[:, u % 2], ACT.Gelu,
                                   bias=G.small[:, 5 + c:6 + c]).then_inc(S.gelu_ready, 1)

            @block.vector
            def _(dve):
                for u, (q, c) in enumerate(units):
                    dve.wait_ge(S.gelu_ready, u + 1)
                    dve.wait_ge(S.a_ready, u + 1)
                    if u >= 3:
                        dve.wait_ge(S.y_added, u - 2)
                    dve.scalar_tensor_tensor(out=hidden[:, u % 3], in0=a_ps[:, u % 2],
                                             scalar=G.small[:, 2 + c:3 + c], in1=gate[:, u % 3],
                                             op0=ALU.add, op1=ALU.mult).then_inc(S.hidden_ready, 1)
                    if c == chunks - 1:
                        dve.wait_ge(S.y_added, u + 1)
                        dve.scalar_tensor_tensor(out=G.cur[:, cols(q, QW)], in0=y_ps[:, q % 2],
                                                 scalar=G.small[:, 8:9], in1=G.mid[:, cols(q, QW)],
                                                 op0=ALU.add, op1=ALU.add).then_inc(S.stored, 1)
                dve.wait_ge(S.stored, QUARTERS)



def rotary_tables2():
    f = np.float32
    half = np.arange(0, HD2, 2, dtype=f)
    inv_freq = (1.0 / (f(10000.0) ** (half / f(HD2)))).astype(f)
    t = np.arange(T, dtype=f)
    freqs = (t[:, None] * inv_freq[None, :]).astype(f)
    freqs = np.concatenate([freqs, freqs], -1)
    base = ((half + f(0.4 * HD2)) / f(1.4 * HD2)).astype(f)
    power = ((t - T // 2) / f(WIN // 2)).astype(f)
    scale = (base[None, :] ** power[:, None]).astype(f)
    scale = np.concatenate([scale, scale], -1)
    sign = np.where(np.arange(HD2) < HD2 // 2, f(-1.0), f(1.0))
    table = np.stack([np.cos(freqs) * scale, np.sin(freqs) * scale * sign,
                      np.cos(freqs) / scale, np.sin(freqs) / scale * sign], axis=1).astype(f)
    return table.reshape(QT, P, 4, HD2).transpose(1, 0, 2, 3)


def local_mask():
    i = np.arange(P)[:, None] % WIN
    j = np.arange(2 * WIN)[None, :]
    seen = (j >= i) & (j <= i + WIN)
    first = seen & ((j >= WIN) | (np.arange(P)[:, None] >= WIN))
    m = np.repeat(seen[:, None], QT, 1)
    m[:, 0] = first
    return np.where(m, 0.0, -3e38).astype(np.float32)


def stack_matrix(slots):
    m = np.zeros((P, PAIRS, 3, P), np.float32)
    for pair in range(PAIRS):
        for h in range(2):
            for slot, part in enumerate(slots):
                for d in range(HD):
                    m[(2 * pair + h) * HD + d, pair, part, 64 * h + HD * slot + d] = 1.0
    return m


def rotary_heads():
    freq = (1.0 / 10000.0 ** (np.arange(0, HD, 2, dtype=np.float32) / HD)).astype(np.float32)
    angle = np.arange(T, dtype=np.float32)[None, :] * freq[:, None]
    angle = angle.astype(np.float32)
    table = np.zeros((HD, 2, T), np.float32)
    table[0::2, 0] = table[1::2, 0] = np.cos(angle)
    table[0::2, 1] = -np.sin(angle)
    table[1::2, 1] = np.sin(angle)
    return np.tile(table, (HEADS, 1, 1))


def row_masks():
    m = np.zeros((P, 4), np.float32)
    for h in range(2):
        for slot, part in enumerate(SLOTS_K):
            m[64 * h + HD * slot:64 * h + HD * (slot + 1), part] = 1.0
        for part in range(3):
            m[64 * h + ONES_AT + part, part] = 1.0
            m[64 * h + ONES_AT + part, 3] = 1.0
    return m


def pick_matrix(experts, per_expert):
    chunks = max(1, experts * per_expert // P)
    if per_expert >= P:
        m = np.zeros((experts, experts, P), np.float32)
        m[np.arange(experts), np.arange(experts)] = 1.0
        return m
    m = np.zeros((experts, chunks, P), np.float32)
    for c in range(chunks):
        for p in range(P):
            m[(c * P + p) // per_expert, c, p] = 1.0
    return m


def constants():
    return {
        "c_ident": np.eye(P, dtype=np.float32),
        "c_mean": np.full((P, P), 1.0 / P, np.float32),
        "c_ones": np.ones((P, QW), np.float32),
        "c_pick16": pick_matrix(16, 64),
        "c_pick4": pick_matrix(4, 512),
        "c_pick9": pick_matrix(9, 512),
        "c_one_row": np.ones((1, N), np.float32),
        "c_stack_q": stack_matrix(SLOTS_Q).astype(BF16_NP),
        "c_stack_k": stack_matrix(SLOTS_K).astype(BF16_NP),
        "c_turn": rotary_heads(),
        "c_rotary2": rotary_tables2(),
        "c_local_mask": local_mask(),
        "c_keep": np.repeat((np.arange(QT) > 0).astype(np.float32)[None], P, 0),
        "c_causal": np.where(np.tril(np.ones((P, P))) > 0, 0.0, -1e10).astype(np.float32),
    }


def layouts(v):
    a = {}
    a["x"] = v["L0_attn_x"].reshape(N, P).T
    up = np.concatenate([v["L0_ffn_routed_up"], v["L0_ffn_shared_up"]]).reshape(9, P, P)
    a["b0f_up"] = up.transpose(2, 0, 1)
    down = np.concatenate([v["L0_ffn_routed_down"], v["L0_ffn_shared_down"]])
    a["b0f_down"] = down.transpose(0, 2, 1).reshape(9, P, P).transpose(1, 0, 2)
    a["b0f_router"] = v["L0_ffn_router_w"].T
    a["b0a_wd"] = v["L0_attn_Wd"]
    rep = lambda r: np.repeat(r.reshape(1, -1), P, 0)
    col = lambda c: c.reshape(P, 1)
    a["b0a_small"] = np.concatenate(
        [v["L0_attn_WB"], v["L0_attn_WC"], rep(v["L0_attn_bB"]), rep(v["L0_attn_bC"]),
         v["L0_attn_A_log"], col(v["L0_attn_D_param"]), col(v["L0_attn_bd"]), col(v["L0_attn_ln_w"]),
         col(v["L0_attn_ln_b"]), np.zeros((P, 4), np.float32)], axis=1)
    a["b0m_up"] = v["L0_attn_up_w"].reshape(4, P, 4, P).transpose(1, 0, 2, 3)
    a["b0m_down"] = v["L0_attn_down_w"].reshape(4, 4, P, P).transpose(2, 0, 1, 3)
    a["b0m_b1"] = v["L0_attn_up_b"].reshape(16, P).T
    a["b0m_b2"] = v["L0_attn_down_b"]
    a["b0m_router"] = v["L0_attn_Wr"]
    a["b0m_router_b"] = v["L0_attn_br"].reshape(1, 4)
    w1 = np.concatenate([v["L1_ffn_W1"], v["L1_ffn_Ws1"][None]])
    w2 = np.concatenate([v["L1_ffn_W2"], v["L1_ffn_Ws2"][None]])
    a["b1f_up"] = w1.reshape(9, P, 4, P).transpose(1, 0, 2, 3)
    a["b1f_down"] = w2.reshape(9, 4, P, P).transpose(2, 0, 1, 3)
    a["b1f_b1"] = np.concatenate([v["L1_ffn_b1"], v["L1_ffn_bs1"][None]]).reshape(36, P).T
    a["b1f_b2"] = np.concatenate([v["L1_ffn_b2"], v["L1_ffn_bs2"][None]])
    a["b1f_gate_w"] = v["L1_ffn_gate"]
    wqkv = v["L1_attn_Wqkv"].reshape(HEADS, 3, HD, P).transpose(3, 1, 0, 2).reshape(P, 3, P)
    bqkv = v["L1_attn_bqkv"].reshape(HEADS, 3, HD).transpose(1, 0, 2).reshape(3, P)
    a["b1a_w"] = wqkv
    a["b1a_v_bias"] = bqkv[2:3]
    wr, br = v["L1_attn_Wr"], v["L1_attn_br"]
    near_at = np.clip(np.arange(QW) - (2 * P - 1), -WINDOW1, WINDOW1) + WINDOW1
    masks = row_masks()
    positions = np.zeros((P, QW + 2), wr.dtype)
    for h in range(2):
        for slot in range(len(SLOTS_K)):
            rows = slice(64 * h + HD * slot, 64 * h + HD * (slot + 1))
            positions[rows, 0:QW] = wr[near_at].T
        rows = slice(64 * h + ONES_AT, 64 * h + ONES_AT + 3)
        positions[rows, 0:QW] = br[near_at]
        positions[rows, QW] = br[0]
        positions[rows, QW + 1] = br[-1]
    a["b1a_positions"] = positions
    a["b1a_small"] = np.concatenate(
        [bqkv.T, np.tile(wr[0], HEADS)[:, None], np.tile(wr[-1], HEADS)[:, None],
         np.zeros((P, 1), np.float32), masks, np.zeros((P, 2), np.float32)], axis=1)
    swap = np.arange(P) ^ 1
    a["b3a_w"] = np.stack([v["L3_attn_qw"], v["L3_attn_kw"], v["L3_attn_vw"],
                           v["L3_attn_qw"][:, swap], v["L3_attn_kw"][:, swap],
                           v["L3_attn_ow"]], axis=1)
    a["b2f_wqkv"] = v["L2_ffn_Wqkv"]
    a["b2f_wo"] = v["L2_ffn_Wo"].reshape(LAYERS, PAIRS, P, P).transpose(0, 2, 1, 3)
    zeros = lambda *shape: np.zeros(shape, np.float32)
    w1 = v["L2_ffn_W1"].reshape(LAYERS, P, 2, FF)
    a["b2f_w1"] = np.concatenate([w1, zeros(LAYERS, P, 2, FF_PAD - FF)], 3).reshape(LAYERS, P, 6, P)
    w2 = np.concatenate([v["L2_ffn_W2"], zeros(LAYERS, FF_PAD - FF, P)], 1)
    a["b2f_w2"] = w2.reshape(LAYERS, 3, P, P).transpose(0, 2, 1, 3)
    fb1 = np.concatenate([v["L2_ffn_b1"].reshape(LAYERS, 2, FF), zeros(LAYERS, 2, FF_PAD - FF)], 2)
    a["b2f_small"] = np.concatenate(
        [v["L2_ffn_ln_g"][:, :, None], v["L2_ffn_ln_b"][:, :, None],
         fb1.reshape(LAYERS, 6, P).transpose(0, 2, 1), v["L2_ffn_b2"][:, :, None]], axis=2)
    rot = np.arange(HD2) ^ (HD2 // 2)
    qs, ks = v["L2_ffn_q_scale"], v["L2_ffn_k_scale"]
    scales = np.stack([qs, qs[:, rot], ks, ks[:, rot]], axis=1)
    a["b2f_scales"] = np.repeat(scales[:, None], P, 1)
    for n in "qkv":
        f = lambda key: v[f"L3_ffn_{n}_{key}"]
        a[f"b3f_{n}_up"] = f("w1").reshape(8, 2, P, 64).transpose(2, 0, 1, 3).reshape(P, 8, P)
        a[f"b3f_{n}_down"] = f("w2").reshape(8, P, P).transpose(1, 0, 2)
        a[f"b3f_{n}_b1"] = f("b1").reshape(8, P).T
        a[f"b3f_{n}_b2"] = f("b2")
        a[f"b3f_{n}_node_w"] = np.concatenate([f("node_w").T, np.zeros((P, 1), np.float32)], axis=1)
        a[f"b3f_{n}_node_b"] = np.concatenate([f("node_b"), np.zeros(1, np.float32)])[None]
    a["b3a_small"] = np.zeros((P, 12), np.float32)
    a["b2a_w"] = np.stack([v["L2_attn_Wk"].T, v["L2_attn_Wv"].T, v["L2_attn_Wr"].T,
                           v["L2_attn_Wo"].T], axis=1)
    a["b2a_small"] = np.concatenate(
        [v["L2_attn_time_decay"], v["L2_attn_time_first"], v["L2_attn_time_mix_k"][0].T,
         v["L2_attn_time_mix_v"][0].T, v["L2_attn_time_mix_r"][0].T], axis=1)
    return {k: np.ascontiguousarray(x) for k, x in a.items()}


def load_constants(nc, M, W):
    shapes = {"ident": [P, P], "mean": [P, P], "ones": [P, QW], "pick16": [16, 8, P], "pick4": [4, 4, P],
              "pick9": [9, 9, P], "causal": [P, P]}
    tiles = {n: M.sb(f"c_{n}", s) for n, s in shapes.items()}
    load(nc, "constants", [(tiles[n][:], W[f"c_{n}"]) for n in shapes])
    return Names(flag=M.sb("c_flag", [1, 1], mybir.dt.int32),
                 scratch=nc.dram_tensor("position_scratch", [4, 2, P, QW], F32, kind="Internal").ap(),
                 **tiles)



def build(nc, W, out):
    with ExitStack() as ctx:
        M = Memory(nc, ctx)
        K = load_constants(nc, M, W)
        x = M.sb("x", [P, N])
        xn = M.sb("xn", [P, N])
        load(nc, "x", [(x[:], W["x"])])
        layer_norm(nc, K, "n0", x, xn)
        block0_attn(nc, K, W, xn, x)
        block0_ffn(nc, K, W, xn, x)
        layer_norm(nc, K, "n1", x, xn)
        head_attention(nc, K, W, "b1a", xn, x, relative=True)
        block1_ffn(nc, K, W, xn, x)
        layer_norm(nc, K, "n2", x, xn)
        block2_attn(nc, K, W, xn, x)
        block2_ffn(nc, K, W, xn, x)
        layer_norm(nc, K, "n3", x, xn)
        head_attention(nc, K, W, "b3a", xn, x, relative=False)
        block3_ffn(nc, K, W, xn, x)
        load(nc, "out", [(out, x[:])])


def kernel(**inputs):
    import concourse.bacc as bacc
    from concourse.bass_utils import run_bass_kernel_spmd

    nc = bacc.Bacc("TRN2", target_bir_lowering=False, num_devices=1)
    arrays = {**constants(), **layouts({k: np.asarray(a) for k, a in inputs.items()})}
    W = {name: nc.dram_tensor(f"in_{name}", a.shape, mybir.dt.from_np(a.dtype),
                              kind="ExternalInput").ap() for name, a in arrays.items()}
    out = nc.dram_tensor("out", (P, N), F32, kind="ExternalOutput").ap()
    build(nc, W, out)
    run = run_bass_kernel_spmd(nc, [{f"in_{n}": a for n, a in arrays.items()}], core_ids=[0])
    return np.ascontiguousarray(run.results[0]["out"].T).reshape(B, T, P)
```

```python
from collections import namedtuple
from contextlib import ExitStack, contextmanager

import numpy as np
import concourse.bass as bass
from concourse import mybir

P = 128
B, T = 2, 1024
N = B * T
TILES = N // P
QW = 512
QUARTERS = N // QW
FIRST_SEM = 120

F32 = mybir.dt.float32
BF16 = mybir.dt.bfloat16
ALU = mybir.AluOpType
ACT = mybir.ActivationFunctionType
AX_X = mybir.AxisListType.X
BF16_NP = mybir.dt.np(BF16)



@contextmanager
def stage(nc, *names):
    sems = [nc.alloc_semaphore(n, num=FIRST_SEM + i) for i, n in enumerate(names)]
    with nc.Block() as block:
        yield block, Names(**dict(zip(names, sems)))
    nc.all_engine_barrier(sems_to_clear=range(FIRST_SEM, FIRST_SEM + len(sems)))
    for s in sems:
        nc.release_semaphore(s)


def Names(**things):
    return namedtuple("Names", things)(**things)


class Chain:

    def __init__(self, eng, sem):
        self.eng, self.sem, self.n = eng, sem, 0

    def __call__(self, ins):
        self.n += 1
        ins.then_inc(self.sem, 1)
        self.eng.wait_ge(self.sem, self.n)


class Memory:

    def __init__(self, nc, ctx):
        self.nc, self.ctx = nc, ctx

    def sb(self, name, shape, dt=F32):
        return self.ctx.enter_context(self.nc.sbuf_tensor(name, shape, dt))

    def ps(self, name, shape, dt=F32):
        return self.ctx.enter_context(self.nc.psum_tensor(name, shape, dt))


def cols(i, width):
    return slice(i * width, (i + 1) * width)



def layer_norm(nc, K, name, src, dst, eps=1e-5, gain=None, offset=None, add_to=None):
    with ExitStack() as ctx:
        M = Memory(nc, ctx)
        centred = M.sb(f"{name}_centred", [P, QUARTERS, QW])
        squares = M.sb(f"{name}_squares", [P, 2, QW])
        spread = M.sb(f"{name}_spread", [P, 2, QW])
        root = M.sb(f"{name}_root", [P, 2, QW])
        mean_ps = M.ps(f"{name}_mean_ps", [P, 2, QW])
        var_ps = M.ps(f"{name}_var_ps", [P, 2, QW])
        with stage(nc, "mean_ready", "centred_ready", "squared", "var_ready", "shifted",
                   "rooted", "normed", "dve_chain") as (block, S):

            @block.tensor
            def _(pe):
                for q in range(QUARTERS + 1):
                    if q < QUARTERS:
                        if q >= 2:
                            pe.wait_ge(S.centred_ready, q - 1)
                        pe.matmul(mean_ps[:, q % 2], K.mean[:], src[:, cols(q, QW)], start=True,
                                  stop=True).then_inc(S.mean_ready, 1)
                    if q >= 1:
                        pe.wait_ge(S.squared, q)
                        if q >= 3:
                            pe.wait_ge(S.shifted, q - 2)
                        pe.matmul(var_ps[:, (q - 1) % 2], K.mean[:], squares[:, (q - 1) % 2],
                                  start=True, stop=True).then_inc(S.var_ready, 1)

            @block.scalar
            def _(act):
                for q in range(QUARTERS + 1):
                    if q < QUARTERS:
                        act.wait_ge(S.centred_ready, q + 1)
                        if q >= 2:
                            act.wait_ge(S.var_ready, q - 1)
                        act.activation(squares[:, q % 2], centred[:, q], ACT.Square).then_inc(S.squared, 1)
                    if q >= 1:
                        act.wait_ge(S.shifted, q)
                        if q >= 3:
                            act.wait_ge(S.normed, q - 2)
                        act.activation(root[:, (q - 1) % 2], spread[:, (q - 1) % 2],
                                       ACT.Sqrt).then_inc(S.rooted, 1)

            @block.vector
            def _(dve):
                chain = Chain(dve, S.dve_chain)
                for q in range(QUARTERS + 2):
                    if q < QUARTERS:
                        dve.wait_ge(S.mean_ready, q + 1)
                        dve.tensor_tensor(centred[:, q], src[:, cols(q, QW)], mean_ps[:, q % 2],
                                          ALU.subtract).then_inc(S.centred_ready, 1)
                    if 1 <= q <= QUARTERS:
                        dve.wait_ge(S.var_ready, q)
                        if q >= 3:
                            dve.wait_ge(S.rooted, q - 2)
                        dve.tensor_scalar(spread[:, (q - 1) % 2], var_ps[:, (q - 1) % 2], eps, None,
                                          ALU.add).then_inc(S.shifted, 1)
                    if q >= 2:
                        r = q - 2
                        dve.wait_ge(S.rooted, r + 1)
                        inverse = root[:, r % 2]
                        chain(dve.reciprocal(inverse, inverse))
                        dve.wait_ge(S.centred_ready, r + 1)
                        out = dst[:, cols(r, QW)]
                        if gain is None:
                            dve.tensor_tensor(out, centred[:, r], inverse, ALU.mult).then_inc(S.normed, 1)
                        else:
                            chain(dve.scalar_tensor_tensor(out=centred[:, r], in0=centred[:, r],
                                                           scalar=gain, in1=inverse,
                                                           op0=ALU.mult, op1=ALU.mult))
                            if add_to is None:
                                dve.tensor_scalar(out, centred[:, r], offset, None,
                                                  ALU.add).then_inc(S.normed, 1)
                            else:
                                dve.scalar_tensor_tensor(out=out, in0=centred[:, r], scalar=offset,
                                                         in1=add_to[:, cols(r, QW)], op0=ALU.add,
                                                         op1=ALU.add).then_inc(S.normed, 1)



def router_probs(nc, K, name, flat, weight, bias_row, experts, probs):
    with ExitStack() as ctx:
        M = Memory(nc, ctx)
        wide = TILES * experts
        logits = M.ps(f"{name}_logits", [P, QW])
        top = M.sb(f"{name}_top", [P, TILES])
        total = M.sb(f"{name}_total", [P, TILES])
        lg = logits[:, 0:wide].rearrange("p (t e) -> p t e", e=experts)
        with stage(nc, "logits_ready", "shifted", "exps_ready", "dve_chain") as (block, S):

            @block.tensor
            def _(pe):
                for t in range(TILES):
                    last = pe.matmul(lg[:, t], flat[:, cols(t, P)], weight, start=True,
                                     stop=bias_row is None)
                    if bias_row is not None:
                        last = pe.matmul(lg[:, t], K.ones[0:1, 0:P], bias_row, start=False, stop=True)
                last.then_inc(S.logits_ready, 1)

            @block.vector
            def _(dve):
                chain = Chain(dve, S.dve_chain)
                dve.wait_ge(S.logits_ready, 1)
                chain(dve.tensor_reduce(top[:], lg, AX_X, ALU.max))
                spread = top[:].unsqueeze(2).to_broadcast([P, TILES, experts])
                dve.tensor_tensor(probs[:], lg, spread, ALU.subtract).then_inc(S.shifted, 1)
                dve.wait_ge(S.exps_ready, 1)
                chain(dve.tensor_reduce(total[:], probs[:], AX_X, ALU.add))
                chain(dve.reciprocal(total[:], total[:]))
                spread = total[:].unsqueeze(2).to_broadcast([P, TILES, experts])
                chain(dve.tensor_tensor(probs[:], probs[:], spread, ALU.mult))

            @block.scalar
            def _(act):
                act.wait_ge(S.shifted, 1)
                act.activation(probs[:], probs[:], ACT.Exp).then_inc(S.exps_ready, 1)


def keep_top(nc, name, probs, experts, k):
    with ExitStack() as ctx:
        M = Memory(nc, ctx)
        rank = M.sb(f"{name}_rank", [P, TILES, experts])
        ahead = M.sb(f"{name}_ahead", [P, 2, TILES, experts])
        with stage(nc, "compared", "counted") as (block, S):

            @block.vector
            def _(dve):
                n = 0
                dve.memset(rank[:], 0.0).then_inc(S.counted, 1)
                for e in range(experts):
                    it = probs[:, :, e:e + 1]
                    if e >= 2:
                        dve.wait_ge(S.counted, e)
                    if e > 0:
                        n += 1
                        dve.tensor_tensor(ahead[:, e % 2, :, 0:e], it.to_broadcast([P, TILES, e]),
                                          probs[:, :, 0:e], ALU.is_gt).then_inc(S.compared, 1)
                    n += 1
                    dve.tensor_tensor(ahead[:, e % 2, :, e:], it.to_broadcast([P, TILES, experts - e]),
                                      probs[:, :, e:], ALU.is_ge).then_inc(S.compared, 1)
                    dve.wait_ge(S.compared, n)
                    dve.wait_ge(S.counted, e + 1)
                    dve.tensor_tensor(rank[:], rank[:], ahead[:, e % 2], ALU.add).then_inc(S.counted, 1)
                dve.wait_ge(S.counted, experts + 1)
                dve.scalar_tensor_tensor(out=probs[:], in0=rank[:], scalar=k + 0.5, in1=probs[:],
                                         op0=ALU.is_lt, op1=ALU.mult).then_inc(S.counted, 1)
                dve.wait_ge(S.counted, experts + 2)


def to_rows(nc, K, name, table, rows, dst):
    with ExitStack() as ctx:
        M = Memory(nc, ctx)
        turned = M.ps(f"{name}_turned", [P, QUARTERS, QW])
        per = QW // P
        with stage(nc, "turned_ready", "copied") as (block, S):

            @block.tensor
            def _(pe):
                for t in range(TILES):
                    ins = pe.transpose(turned[0:rows, t // per, cols(t % per, P)], table[:, t],
                                       K.ident[:])
                    if t % per == per - 1:
                        ins.then_inc(S.turned_ready, 1)

            @block.vector
            def _(dve):
                for q in range(QUARTERS):
                    dve.wait_ge(S.turned_ready, q + 1)
                    dve.tensor_copy(dst[0:rows, cols(q, QW)], turned[0:rows, q]).then_inc(S.copied, 1)
                dve.wait_ge(S.copied, QUARTERS)



def mlp(nc, K, name, src, dst, chunks, func, gates=None, gate_rows=0, out_bias=None, add=True):
    n_chunks = len(chunks)
    quarters = 2
    ring = 4
    units = [(i, c) for i in range(quarters) for c in range(n_chunks)]
    gated = [chunks[c][3] is not None for i, c in units]
    gated_until = [sum(gated[:u]) for u in range(len(units) + 1)]
    starts = [gated[u] and (c == 0 or not gated[u - 1] or chunks[c - 1][4] != chunks[c][4])
              for u, (i, c) in enumerate(units)]
    group = [sum(starts[:u + 1]) - 1 for u in range(len(units))]
    last_gated = {g: max(u for u in range(len(units)) if gated[u] and group[u] == g)
                  for g in set(group) if g >= 0}
    with ExitStack() as ctx:
        M = Memory(nc, ctx)
        hidden = M.sb(f"{name}_hidden", [P, ring, QW])
        scaled = M.sb(f"{name}_scaled", [P, ring, QW])
        h_ps = M.ps(f"{name}_h_ps", [P, 3, QW])
        g_ps = M.ps(f"{name}_g_ps", [P, 2, QW])
        y_ps = M.ps(f"{name}_y_ps", [P, quarters, QW])
        with nc.Fori(0, QUARTERS // quarters) as turn, stage(
                nc, "h_ready", "g_ready", "h_done", "h_scaled", "y_added",
                "y_ready", "y_stored") as (block, S):

            def tokens(i):
                return bass.ds((turn * quarters + i) * QW, QW)

            @block.tensor
            def _(pe):
                def hidden_product(u):
                    i, c = units[u]
                    w1, _, _, select, _ = chunks[c]
                    if starts[u]:
                        g = group[u]
                        if g >= 2:
                            pe.wait_ge(S.h_scaled, gated_until[last_gated[g - 2] + 1])
                        pe.matmul(g_ps[:, g % 2], select, gates[0:gate_rows, tokens(i)],
                                  start=True, stop=True).then_inc(S.g_ready, 1)
                    if u >= 3:
                        pe.wait_ge(S.h_done, u - 2)
                    pe.matmul(h_ps[:, u % 3], w1, src[:, tokens(i)], start=True, stop=True) \
                        .then_inc(S.h_ready, 1)

                def output_product(u):
                    i, c = units[u]
                    if gated[u]:
                        pe.wait_ge(S.h_scaled, gated_until[u + 1])
                    else:
                        pe.wait_ge(S.h_done, u + 1)
                    h = (scaled if gated[u] else hidden)[:, u % ring]
                    last = c == n_chunks - 1
                    pe.matmul(y_ps[:, i], chunks[c][2], h, start=(c == 0),
                              stop=(last and out_bias is None)).then_inc(S.y_added, 1)
                    if last and out_bias is not None:
                        pe.matmul(y_ps[:, i], out_bias, gates[0:gate_rows, tokens(i)], start=False,
                                  stop=True).then_inc(S.y_ready, 1)

                for u in range(len(units) + 2):
                    if u < len(units):
                        hidden_product(u)
                    if u >= 2:
                        output_product(u - 2)

            @block.scalar
            def _(act):
                for u, (i, c) in enumerate(units):
                    act.wait_ge(S.h_ready, u + 1)
                    if u >= ring:
                        act.wait_ge(S.y_added, u - ring + 1)
                    b1 = chunks[c][1]
                    kw = {} if b1 is None else {"bias": b1}
                    act.activation(hidden[:, u % ring], h_ps[:, u % 3], func, **kw).then_inc(S.h_done, 1)

            @block.vector
            def _(dve):
                for u, (i, c) in enumerate(units):
                    if gated[u]:
                        dve.wait_ge(S.h_done, u + 1)
                        if starts[u]:
                            dve.wait_ge(S.g_ready, group[u] + 1)
                        if u >= ring:
                            dve.wait_ge(S.y_added, u - ring + 1)
                        dve.tensor_tensor(scaled[:, u % ring], hidden[:, u % ring],
                                          g_ps[:, group[u] % 2], ALU.mult).then_inc(S.h_scaled, 1)
                    if c == n_chunks - 1:
                        if out_bias is not None:
                            dve.wait_ge(S.y_ready, i + 1)
                        else:
                            dve.wait_ge(S.y_added, u + 1)
                        out = dst[:, tokens(i)]
                        if add:
                            dve.tensor_tensor(out, out, y_ps[:, i], ALU.add).then_inc(S.y_stored, 1)
                        else:
                            dve.tensor_copy(out, y_ps[:, i]).then_inc(S.y_stored, 1)
                dve.wait_ge(S.y_stored, quarters)



def load(nc, name, pairs):
    with stage(nc, "loaded") as (block, S):
        half = (len(pairs) + 1) // 2

        @block.sync
        def _(sp):
            for dst, src in pairs[:half]:
                sp.dma_start(dst, src).then_inc(S.loaded, 16)
            sp.wait_ge(S.loaded, 16 * len(pairs))

        @block.scalar
        def _(act):
            for dst, src in pairs[half:]:
                act.dma_start(dst, src).then_inc(S.loaded, 16)


SHARED0, ROUTED0, WIDE0, TOP0 = 2, 16, 64, 4


def block0_ffn(nc, K, W, xn, x):
    with ExitStack() as ctx:
        M = Memory(nc, ctx)
        pairs = ROUTED0 // 2
        up = M.sb("b0f_up", [P, pairs + 1, P])
        down = M.sb("b0f_down", [P, pairs + 1, P])
        rw = M.sb("b0f_router", [P, ROUTED0])
        gates = M.sb("b0f_gates", [ROUTED0, N])
        load(nc, "b0f", [(up[:], W["b0f_up"]), (down[:], W["b0f_down"]), (rw[:], W["b0f_router"])])
        with ExitStack() as inner:
            probs = Memory(nc, inner).sb("b0f_probs", [P, TILES, ROUTED0])
            router_probs(nc, K, "b0f", xn, rw[:], None, ROUTED0, probs)
            keep_top(nc, "b0f", probs, ROUTED0, TOP0)
            to_rows(nc, K, "b0f", probs, ROUTED0, gates)
        chunks = [(up[:, c], None, down[:, c], K.pick16[:, c], c) for c in range(pairs)]
        chunks.append((up[:, pairs], None, down[:, pairs], None, -1))
        mlp(nc, K, "b0f", xn, x, chunks, ACT.Gelu, gates, ROUTED0)



STATES = 16
H_LIMIT = 100.0


def ssm_states(nc, K, w, name, xn, delta, flat, peak, stepwise):
    units = [(s, q) for s in range(STATES) for q in range(QUARTERS)]
    per_seq = T // QW
    with ExitStack() as ctx:
        M = Memory(nc, ctx)
        decay = M.sb(f"{name}_decay", [P, 3, QW])
        raw = M.sb(f"{name}_raw", [P, 2, QW])
        drive = M.sb(f"{name}_drive", [P, 2, QW])
        h = M.sb(f"{name}_h", [P, 3, QW])
        hc = M.sb(f"{name}_hc", [P, 3, QW])
        peaks = M.sb(f"{name}_peaks", [P, len(units)])
        b_ps = M.ps(f"{name}_b_ps", [P, 2, QW])
        c_ps = M.ps(f"{name}_c_ps", [P, 2, QW])
        y_ps = M.ps(f"{name}_y_ps", [P, QUARTERS, QW])
        with stage(nc, "b_ready", "c_ready", "decay_ready", "clipped", "drive_ready", "state_ready",
                   "peak_read", "hc_ready", "y_added", "dve_chain") as (block, S):

            @block.tensor
            def _(pe):
                for u in range(len(units) + 2):
                    if u < len(units):
                        s, q = units[u]
                        if u >= 2:
                            pe.wait_ge(S.clipped, u - 1)
                            pe.wait_ge(S.hc_ready, u - 1)
                        pe.matmul(b_ps[:, u % 2], w.wb[:, s:s + 1].to_broadcast([P, P]),
                                  xn[:, cols(q, QW)], start=True, stop=True).then_inc(S.b_ready, 1)
                        pe.matmul(c_ps[:, u % 2], w.wc[:, s:s + 1].to_broadcast([P, P]),
                                  xn[:, cols(q, QW)], start=True, stop=True).then_inc(S.c_ready, 1)
                    if u >= 2:
                        s, q = units[u - 2]
                        pe.wait_ge(S.hc_ready, u - 1)
                        pe.matmul(y_ps[:, q], K.ident[:], hc[:, (u - 2) % 3], start=(s == 0),
                                  stop=(s == STATES - 1)).then_inc(S.y_added, 1)

            @block.scalar
            def _(act):
                for u, (s, q) in enumerate(units):
                    if u >= 3:
                        act.wait_ge(S.state_ready, u - 2)
                    act.activation(decay[:, u % 3], delta[:, cols(q, QW)], ACT.Exp,
                                   scale=w.a[:, s:s + 1]).then_inc(S.decay_ready, 1)

            @block.gpsimd
            def _(pool):
                for u, (s, q) in enumerate(units):
                    pool.wait_ge(S.clipped, u + 1)
                    if u >= 2:
                        pool.wait_ge(S.state_ready, u - 1)
                    pool.tensor_tensor(drive[:, u % 2], raw[:, u % 2], xn[:, cols(q, QW)], ALU.mult) \
                        .then_inc(S.drive_ready, 1)

            @block.vector
            def _(dve):
                chain = Chain(dve, S.dve_chain)

                def drive_factor(u):
                    s, q = units[u]
                    dve.wait_ge(S.b_ready, u + 1)
                    if u >= 2:
                        dve.wait_ge(S.drive_ready, u - 1)
                    chain(dve.scalar_tensor_tensor(out=raw[:, u % 2], in0=b_ps[:, u % 2],
                                                   scalar=w.bb[:, s:s + 1], in1=delta[:, cols(q, QW)],
                                                   op0=ALU.add, op1=ALU.mult))
                    dve.tensor_scalar(raw[:, u % 2], raw[:, u % 2], 2.0, -2.0, ALU.min, ALU.max) \
                        .then_inc(S.clipped, 1)

                def scan(u):
                    s, q = units[u]
                    initial = 0.0 if q % per_seq == 0 else h[:, (u - 1) % 3, QW - 1:QW]
                    dve.wait_ge(S.drive_ready, u + 1)
                    dve.wait_ge(S.decay_ready, u + 1)
                    if u >= 3:
                        dve.wait_ge(S.peak_read, u - 2)
                    dve.tensor_tensor_scan(h[:, u % 3], decay[:, u % 3], drive[:, u % 2], initial,
                                           ALU.mult, ALU.add).then_inc(S.state_ready, 1)

                def walk(u):
                    s, q = units[u]
                    now, dec, drv = h[:, u % 3], decay[:, u % 3], drive[:, u % 2]
                    dve.wait_ge(S.drive_ready, u + 1)
                    dve.wait_ge(S.decay_ready, u + 1)
                    if q % per_seq == 0:
                        chain(dve.tensor_copy(now[:, 0:1], drv[:, 0:1]))
                    else:
                        chain(dve.scalar_tensor_tensor(out=now[:, 0:1], in0=h[:, (u - 1) % 3, QW - 1:QW],
                                                       scalar=dec[:, 0:1], in1=drv[:, 0:1],
                                                       op0=ALU.mult, op1=ALU.add))
                    chain(dve.tensor_scalar(now[:, 0:1], now[:, 0:1], H_LIMIT, -H_LIMIT,
                                            ALU.min, ALU.max))
                    with dve.Fori(1, QW) as t:
                        dve.drain()
                        dve.tensor_tensor(now[:, bass.ds(t, 1)], now[:, bass.ds(t - 1, 1)],
                                          dec[:, bass.ds(t, 1)], ALU.mult)
                        dve.drain()
                        dve.tensor_tensor(now[:, bass.ds(t, 1)], now[:, bass.ds(t, 1)],
                                          drv[:, bass.ds(t, 1)], ALU.add)
                        dve.drain()
                        dve.tensor_scalar(now[:, bass.ds(t, 1)], now[:, bass.ds(t, 1)], H_LIMIT,
                                          -H_LIMIT, ALU.min, ALU.max)
                    dve.drain()
                    dve.tensor_copy(now[:, 0:1], now[:, 0:1]).then_inc(S.state_ready, 1)

                def output(u):
                    s, q = units[u]
                    dve.wait_ge(S.state_ready, u + 1)
                    dve.tensor_reduce(peaks[:, u:u + 1], h[:, u % 3], AX_X, ALU.max,
                                      apply_absolute_value=True).then_inc(S.peak_read, 1)
                    dve.wait_ge(S.c_ready, u + 1)
                    if u >= 3:
                        dve.wait_ge(S.y_added, u - 2)
                    dve.scalar_tensor_tensor(out=hc[:, u % 3], in0=c_ps[:, u % 2],
                                             scalar=w.bc[:, s:s + 1], in1=h[:, u % 3],
                                             op0=ALU.add, op1=ALU.mult).then_inc(S.hc_ready, 1)

                for u in range(len(units) + 1):
                    if u < len(units):
                        drive_factor(u)
                    if u >= 1:
                        (walk if stepwise else scan)(u - 1)
                        output(u - 1)
                for q in range(QUARTERS):
                    dve.wait_ge(S.y_added, len(units) - QUARTERS + q + 1)
                    chain(dve.scalar_tensor_tensor(out=flat[:, cols(q, QW)], in0=xn[:, cols(q, QW)],
                                                   scalar=w.d[:], in1=y_ps[:, q], op0=ALU.mult,
                                                   op1=ALU.add))
                dve.wait_ge(S.peak_read, len(units))
                chain(dve.tensor_reduce(peak, peaks[:], AX_X, ALU.max))


def block0_attn(nc, K, W, xn, x):
    with ExitStack() as ctx:
        M = Memory(nc, ctx)
        wd = M.sb("b0a_wd", [P, P])
        small = M.sb("b0a_small", [P, 5 * STATES + 8])
        w = Names(wb=small[:, 0:16], wc=small[:, 16:32], bb=small[:, 32:48],
                            bc=small[:, 48:64], a=small[:, 64:80], d=small[:, 80:81],
                            bd=small[:, 81:82], ln_w=small[:, 82:83], ln_b=small[:, 83:84])
        flat = M.sb("b0a_flat", [P, N])
        peak = M.sb("b0a_peak", [P, 1])
        load(nc, "b0a", [(wd[:], W["b0a_wd"]), (small[:], W["b0a_small"])])
        with ExitStack() as inner:
            delta = Memory(nc, inner).sb("b0a_delta", [P, N])
            softplus_delta(nc, K, w, wd, xn, delta)
            ssm_states(nc, K, w, "b0s", xn, delta, flat, peak[:], stepwise=False)
            over = clipped_somewhere(nc, K, peak)
            with nc.If(over > 0):
                ssm_states(nc, K, w, "b0w", xn, delta, flat, peak[:], stepwise=True)
            with nc.Else():
                nc.all_engine_barrier()
        with ExitStack() as inner:
            I = Memory(nc, inner)
            up = I.sb("b0m_up", [P, 4, 4, P])
            down = I.sb("b0m_down", [P, 4, 4, P])
            b1 = I.sb("b0m_b1", [P, 16])
            b2 = I.sb("b0m_b2", [4, P])
            rw = I.sb("b0m_router", [P, 4])
            rb = I.sb("b0m_router_b", [1, 4])
            gates = I.sb("b0m_gates", [4, N])
            moe = I.sb("b0m_out", [P, N])
            load(nc, "b0m", [(up[:], W["b0m_up"]), (down[:], W["b0m_down"]), (b1[:], W["b0m_b1"]),
                             (b2[:], W["b0m_b2"]), (rw[:], W["b0m_router"]), (rb[:], W["b0m_router_b"])])
            with ExitStack() as rt:
                probs = Memory(nc, rt).sb("b0m_probs", [P, TILES, 4])
                router_probs(nc, K, "b0m", flat, rw[:], rb[:], 4, probs)
                keep_top(nc, "b0m", probs, 4, 1)
                to_rows(nc, K, "b0m", probs, 4, gates)
            chunks = [(up[:, e, c], b1[:, 4 * e + c:4 * e + c + 1], down[:, e, c],
                       K.pick4[:, e], e) for e in range(4) for c in range(4)]
            mlp(nc, K, "b0m", flat, moe, chunks, ACT.Silu, gates, 4, b2[:], add=False)
            add_tokens(nc, flat[:], moe[:])
        layer_norm(nc, K, "b0n", flat, x, gain=w.ln_w, offset=w.ln_b, add_to=x)


def add_tokens(nc, dst, src):
    with stage(nc, "added") as (block, S):

        @block.vector
        def _(dve):
            dve.tensor_tensor(dst, dst, src, ALU.add).then_inc(S.added, 1)
            dve.wait_ge(S.added, 1)


def softplus_delta(nc, K, w, wd, xn, delta):
    with ExitStack() as ctx:
        M = Memory(nc, ctx)
        u_ps = M.ps("sp_u", [P, QUARTERS, QW])
        tail = M.sb("sp_tail", [P, QUARTERS, QW])
        with stage(nc, "u_ready", "tail_ready", "stored", "act_chain") as (block, S):

            @block.tensor
            def _(pe):
                for q in range(QUARTERS):
                    pe.matmul(u_ps[:, q], wd[:], xn[:, cols(q, QW)], start=True, stop=True) \
                        .then_inc(S.u_ready, 1)

            @block.scalar
            def _(act):
                chain = Chain(act, S.act_chain)
                act.wait_ge(S.u_ready, QUARTERS)
                chain(act.activation(tail[:], u_ps[:], ACT.Abs, bias=w.bd))
                chain(act.activation(tail[:], tail[:], ACT.Exp, scale=-1.0))
                act.activation(tail[:], tail[:], ACT.Ln, bias=1.0).then_inc(S.tail_ready, 1)
                chain(act.activation(w.a, w.a, ACT.Exp))
                chain(act.mul(w.a, w.a, -1.0))

            @block.vector
            def _(dve):
                dve.wait_ge(S.u_ready, QUARTERS)
                dve.wait_ge(S.act_chain, 1)
                dve.tensor_scalar(delta[:], u_ps[:].rearrange("p q n -> p (q n)"), w.bd, 0.0,
                                  ALU.add, ALU.max).then_inc(S.stored, 1)
                dve.wait_ge(S.tail_ready, 1)
                dve.wait_ge(S.stored, 1)
                dve.tensor_tensor(delta[:], delta[:], tail[:].rearrange("p q n -> p (q n)"),
                                  ALU.add).then_inc(S.stored, 1)
                dve.wait_ge(S.stored, 2)


def clipped_somewhere(nc, K, peak):
    flag = K.flag
    with ExitStack() as ctx:
        M = Memory(nc, ctx)
        row = M.ps("peak_row", [P, QW])
        within = M.sb("peak_within", [1, 2])
        with stage(nc, "row_ready", "dve_chain") as (block, S):

            @block.tensor
            def _(pe):
                pe.transpose(row[0:1, 0:P], peak[:], K.ident[:]).then_inc(S.row_ready, 1)

            @block.vector
            def _(dve):
                chain = Chain(dve, S.dve_chain)
                dve.wait_ge(S.row_ready, 1)
                chain(dve.tensor_reduce(within[:, 0:1], row[0:1, 0:P], AX_X, ALU.max))
                chain(dve.tensor_scalar(within[:, 1:2], within[:, 0:1], H_LIMIT, None, ALU.is_le))
                chain(dve.tensor_scalar(flag[:], within[:, 1:2], -1.0, 1.0, ALU.mult, ALU.add))
    return nc.values_load(flag[:], min_val=0, max_val=1)



EXPERTS1, CAPACITY1, HIDDEN1 = 8, N // 8, 512


def choose_tokens(nc, gates):
    with ExitStack() as ctx:
        M = Memory(nc, ctx)
        left = M.sb("b1f_left", [EXPERTS1, N])
        best = M.sb("b1f_best", [EXPERTS1, 8])
        with stage(nc, "dve_chain") as (block, S):

            @block.vector
            def _(dve):
                chain = Chain(dve, S.dve_chain)
                chain(dve.tensor_copy(left[:], gates[0:EXPERTS1]))
                for _ in range(CAPACITY1 // 8):
                    chain(dve.max(best[:], left[:]))
                    chain(dve.match_replace(left[:], best[:], left[:], -1.0))
                chain(dve.scalar_tensor_tensor(out=gates[0:EXPERTS1], in0=left[:], scalar=0.0,
                                               in1=gates[0:EXPERTS1], op0=ALU.is_lt, op1=ALU.mult))


def block1_ffn(nc, K, W, xn, x):
    with ExitStack() as ctx:
        M = Memory(nc, ctx)
        parts = HIDDEN1 // P
        up = M.sb("b1f_up", [P, EXPERTS1 + 1, parts, P])
        down = M.sb("b1f_down", [P, EXPERTS1 + 1, parts, P])
        b1 = M.sb("b1f_b1", [P, (EXPERTS1 + 1) * parts])
        b2 = M.sb("b1f_b2", [EXPERTS1 + 1, P])
        gate_w = M.sb("b1f_gate_w", [P, EXPERTS1])
        gates = M.sb("b1f_gates", [EXPERTS1 + 1, N])
        load(nc, "b1f", [(up[:], W["b1f_up"]), (down[:], W["b1f_down"]), (b1[:], W["b1f_b1"]),
                         (b2[:], W["b1f_b2"]), (gate_w[:], W["b1f_gate_w"]),
                         (gates[EXPERTS1:EXPERTS1 + 1], W["c_one_row"])])
        with ExitStack() as rt:
            probs = Memory(nc, rt).sb("b1f_probs", [P, TILES, EXPERTS1])
            router_probs(nc, K, "b1f", xn, gate_w[:], None, EXPERTS1, probs)
            to_rows(nc, K, "b1f", probs, EXPERTS1, gates)
        choose_tokens(nc, gates)
        chunks = [(up[:, e, c], b1[:, parts * e + c:parts * e + c + 1], down[:, e, c],
                   K.pick9[:, e] if e < EXPERTS1 else None, e)
                  for e in range(EXPERTS1 + 1) for c in range(parts)]
        mlp(nc, K, "b1f", xn, x, chunks, ACT.Gelu_apprx_tanh, gates, EXPERTS1 + 1, b2[:])



K_CLAMP, K_EPS = 60.0, 1e-8


def block2_attn(nc, K, W, xn, x):
    with ExitStack() as ctx:
        M = Memory(nc, ctx)
        w = M.sb("b2a_w", [P, 4, P])
        small = M.sb("b2a_small", [P, 5])
        inv_mix = M.sb("b2a_inv_mix", [P, 3])
        lam = M.sb("b2a_lam", [P, QW])
        mixed = M.sb("b2a_mixed", [P, 3, QW])
        part = M.sb("b2a_part", [P, 3, QW])
        kc = M.sb("b2a_kc", [P, QW])
        kv = M.sb("b2a_kv", [P, QW])
        sr = M.sb("b2a_sr", [P, QW])
        sums = M.sb("b2a_sums", [P, 2, 1 + QW])
        den = M.sb("b2a_den", [P, QW])
        out = M.sb("b2a_out", [P, QW])
        prev = M.sb("b2a_prev", [P, 1 + N])
        kvr_ps = M.ps("b2a_kvr_ps", [P, 3, QW])
        o_ps = M.ps("b2a_o_ps", [P, QW])
        load(nc, "b2a", [(w[:], W["b2a_w"]), (small[:], W["b2a_small"])])
        with stage(nc, "decayed", "mixed_ready", "projected", "act_done", "kc_clamped", "out_ready",
                   "o_ready", "stored", "dve_chain", "act_chain") as (block, S):

            @block.scalar
            def _(act):
                chain = Chain(act, S.act_chain)
                chain(act.activation(small[:, 0:1], small[:, 0:1], ACT.Exp))
                chain(act.activation(small[:, 0:1], small[:, 0:1], ACT.Exp, scale=-1.0))
                act.activation(small[:, 1:2], small[:, 1:2], ACT.Exp).then_inc(S.decayed, 1)
                for q in range(QUARTERS):
                    act.wait_ge(S.kc_clamped, q + 1)
                    act.activation(kc[:], kc[:], ACT.Exp).then_inc(S.act_done, 1)
                    act.activation(sr[:], kvr_ps[:, 2], ACT.Sigmoid).then_inc(S.act_done, 1)

            @block.tensor
            def _(pe):
                for q in range(QUARTERS):
                    pe.wait_ge(S.mixed_ready, q + 1)
                    if q >= 1:
                        pe.wait_ge(S.out_ready, q)
                    for i in range(3):
                        ins = pe.matmul(kvr_ps[:, i], w[:, i], mixed[:, i], start=True, stop=True)
                    ins.then_inc(S.projected, 1)
                    pe.wait_ge(S.out_ready, q + 1)
                    pe.matmul(o_ps[:], w[:, 3], out[:], start=True, stop=True).then_inc(S.o_ready, 1)

            @block.vector
            def _(dve):
                chain = Chain(dve, S.dve_chain)
                chain(dve.tensor_scalar(inv_mix[:], small[:, 2:5], -1.0, 1.0, ALU.mult, ALU.add))
                chain(dve.tensor_copy(prev[:, 1:], xn[:]))
                for b in range(B):
                    chain(dve.memset(prev[:, b * T:b * T + 1], 0.0))
                chain(dve.memset(lam[:], 0.0))
                dve.wait_ge(S.decayed, 1)
                chain(dve.tensor_scalar(lam[:], lam[:], small[:, 0:1], None, ALU.add))
                for q in range(QUARTERS):
                    x_q, prev_q = xn[:, cols(q, QW)], prev[:, cols(q, QW)]
                    for i in range(3):
                        chain(dve.tensor_scalar(part[:, i], x_q, small[:, 2 + i:3 + i], None, ALU.mult))
                    for i in range(3):
                        ins = dve.scalar_tensor_tensor(out=mixed[:, i], in0=prev_q,
                                                       scalar=inv_mix[:, i:i + 1], in1=part[:, i],
                                                       op0=ALU.mult, op1=ALU.add)
                        if i < 2:
                            chain(ins)
                    ins.then_inc(S.mixed_ready, 1)
                    dve.wait_ge(S.projected, q + 1)
                    dve.tensor_scalar(kc[:], kvr_ps[:, 0], K_CLAMP, None, ALU.min) \
                        .then_inc(S.kc_clamped, 1)
                    dve.wait_ge(S.act_done, 2 * q + 2)
                    chain(dve.tensor_tensor(kv[:], kc[:], kvr_ps[:, 1], ALU.mult))
                    for i, a in enumerate((kv, kc)):
                        if q % (T // QW) == 0:
                            chain(dve.memset(sums[:, i, 0:1], 0.0))
                        else:
                            chain(dve.tensor_copy(sums[:, i, 0:1], sums[:, i, QW:QW + 1]))
                        chain(dve.tensor_tensor_scan(sums[:, i, 1:], lam[:], a[:], sums[:, i, 0:1],
                                                     ALU.mult, ALU.add))
                    chain(dve.scalar_tensor_tensor(out=den[:], in0=kc[:], scalar=small[:, 1:2],
                                                   in1=sums[:, 1, 0:QW], op0=ALU.mult, op1=ALU.add))
                    chain(dve.tensor_scalar(den[:], den[:], K_EPS, None, ALU.add))
                    chain(dve.reciprocal(den[:], den[:]))
                    chain(dve.scalar_tensor_tensor(out=kv[:], in0=kv[:], scalar=small[:, 1:2],
                                                   in1=sums[:, 0, 0:QW], op0=ALU.mult, op1=ALU.add))
                    chain(dve.tensor_tensor(kv[:], kv[:], den[:], ALU.mult))
                    if q >= 1:
                        dve.wait_ge(S.o_ready, q)
                    dve.tensor_tensor(out[:], kv[:], sr[:], ALU.mult).then_inc(S.out_ready, 1)
                    dve.wait_ge(S.o_ready, q + 1)
                    x_out = x[:, cols(q, QW)]
                    dve.tensor_tensor(x_out, x_out, o_ps[:], ALU.add).then_inc(S.stored, 1)
                dve.wait_ge(S.stored, QUARTERS)



HEADS, HD = 16, 8
PAIRS = HEADS // 2
WINDOW1 = 128
BAND = 3 * P
QT = T // P
SLOTS_Q = (0, 0, 1, 0, 1, 2)
SLOTS_K = (0, 1, 0, 2, 1, 0)
ONES_AT = HD * len(SLOTS_Q)


OUT_ROWS = 32


def split_parts(chain, dve, src, parts, rest):
    chain(dve.tensor_copy(parts[0], src))
    chain(dve.tensor_tensor(rest, src, parts[0], ALU.subtract))
    chain(dve.tensor_copy(parts[1], rest))
    chain(dve.tensor_tensor(rest, rest, parts[1], ALU.subtract))
    chain(dve.tensor_copy(parts[2], rest))


def masked_parts(chain, dve, parts, masks, out):
    chain(dve.tensor_scalar(out, parts[0], masks[:, 0:1], None, ALU.mult))
    for i in (1, 2):
        chain(dve.scalar_tensor_tensor(out=out, in0=parts[i], scalar=masks[:, i:i + 1], in1=out,
                                       op0=ALU.mult, op1=ALU.add))


def head_attention(nc, K, W, key, xn, x, relative):
    kinds = 3 if relative else 1
    with ExitStack() as ctx:
        M = Memory(nc, ctx)
        n_w = 3 if relative else 6
        w = M.sb(f"{key}_w", [P, n_w, P])
        small = M.sb(f"{key}_small", [P, 12])
        stack_q = M.sb(f"{key}_pick_q", [P, PAIRS, 3, P], BF16)
        stack_k = M.sb(f"{key}_pick_k", [P, PAIRS, 3, P], BF16)
        x_b = M.sb(f"{key}_x_b", [P, T])
        parts = M.sb(f"{key}_parts", [P, 1 + kinds, 3, T], BF16)
        values = M.sb(f"{key}_values", [P, QT, HEADS, HD + 1])
        merged = M.sb(f"{key}_merged", [P, QT, PAIRS, 2 * HD])
        bias_cols = M.sb(f"{key}_bias_cols", [P, 1 + kinds])
        v_bias = M.sb(f"{key}_v_bias", [1, P])
        pick_f = M.sb(f"{key}_pick_f", [P, 2, 3 * P], BF16)
        v_f = M.sb(f"{key}_v_f", [P, QT, 2, OUT_ROWS])
        qk = M.sb(f"{key}_qk", [P, 1 + kinds, T], BF16)
        table = M.sb(f"{key}_table", [P, QW], BF16) if relative else None
        pairs = [(w[:], W[f"{key}_w"]), (small[:], W[f"{key}_small"]),
                 (stack_q[:], W["c_stack_q"]), (stack_k[:], W["c_stack_k"])]
        if relative:
            pairs.append((v_bias[:], W[f"{key}_v_bias"]))
        load(nc, key, pairs)
        if relative:
            position_table(nc, W, key, small, table, bias_cols)
        with stage(nc, "cleared") as (block, S):

            @block.vector
            def _(dve):
                dve.memset(v_f[:], 0.0).then_inc(S.cleared, 1)
                for i, stack in enumerate((stack_q, stack_k)):
                    dve.tensor_copy(pick_f[:, i].rearrange("p (i n) -> p i n", i=3), stack[:, 0]) \
                        .then_inc(S.cleared, 1)
                dve.wait_ge(S.cleared, 3)
        with nc.Fori(0, B) as b:
            project_heads(nc, K, W, key, xn, b, x_b, w, small, parts, values, v_bias, relative)
            with nc.Fori(0, PAIRS) as pair:
                attend_pair(nc, K, key, pair, parts, stack_q, stack_k, pick_f, values, v_f, qk,
                            bias_cols, table, merged, relative)
            merge_heads(nc, K, key, b, merged, x, w, relative)


def position_table(nc, W, key, small, table, bias_cols):
    with ExitStack() as ctx:
        M = Memory(nc, ctx)
        full = M.sb(f"{key}_full", [P, QW + 2])
        rest = M.sb(f"{key}_rest", [P, QW + 2])
        parts = M.sb(f"{key}_table_parts", [P, 3, QW + 2], BF16)
        chosen = M.sb(f"{key}_chosen", [P, QW + 2])
        with stage(nc, "loaded", "dve_chain") as (block, S):

            @block.sync
            def _(sp):
                sp.dma_start(full[:], W[f"{key}_positions"]).then_inc(S.loaded, 16)

            @block.vector
            def _(dve):
                chain = Chain(dve, S.dve_chain)
                dve.wait_ge(S.loaded, 16)
                split_parts(chain, dve, full[:], [parts[:, i] for i in range(3)], rest[:])
                masked_parts(chain, dve, [parts[:, i] for i in range(3)], small[:, 6:9], chosen[:])
                chain(dve.tensor_copy(table[:], chosen[:, 0:QW]))
                chain(dve.tensor_copy(bias_cols[:, 0:1], small[:, 9:10]))
                chain(dve.memset(bias_cols[:, 1:2], 0.0))
                chain(dve.tensor_copy(bias_cols[:, 2:4], chosen[:, QW:QW + 2]))


def project_heads(nc, K, W, key, xn, b, x_b, w, small, parts, values, v_bias, relative):
    with ExitStack() as ctx:
        M = Memory(nc, ctx)
        half = T // QW
        q_f = M.sb(f"{key}_q_f", [P, T])
        k_f = M.sb(f"{key}_k_f", [P, 3, T])
        rest = M.sb(f"{key}_split_rest", [P, T])
        turn = M.sb(f"{key}_turn", [P, 2, T]) if not relative else None
        qk_ps = M.ps(f"{key}_qk_ps", [P, 3, half, QW])
        v_ps = M.ps(f"{key}_v_ps", [P, 2, 4, P])
        with stage(nc, "x_loaded", "turn_loaded", "q_ready", "k_ready", "v_ready", "rotated_ready",
                   "values_ready", "ps_free", "dve_chain", "v_copied") as (block, S):

            @block.gpsimd
            def _(pool):
                pool.tensor_copy(x_b[:], xn[:, bass.ts(b, T)]).then_inc(S.x_loaded, 1)
                pool.memset(values[:, :, :, HD:HD + 1], 1.0).then_inc(S.v_copied, 1)
                pool.wait_ge(S.v_copied, 1)

            if not relative:
                @block.sync
                def _(sp):
                    sp.dma_start(turn[:], W["c_turn"]).then_inc(S.turn_loaded, 16)

            @block.tensor
            def _(pe):
                pe.wait_ge(S.x_loaded, 1)

                def product(i, slot):
                    for j in range(half):
                        ins = pe.matmul(qk_ps[:, slot, j], w[:, i], x_b[:, cols(j, QW)], start=True,
                                        stop=True)
                    return ins

                product(0, 0).then_inc(S.q_ready, 1)
                product(1, 1).then_inc(S.k_ready, 1)
                if not relative:
                    product(3, 2).then_inc(S.rotated_ready, 1)
                    pe.wait_ge(S.ps_free, 1)
                    product(4, 2).then_inc(S.rotated_ready, 1)
                for t in range(QT):
                    ins = pe.matmul(v_ps[:, t // 4, t % 4], x_b[:, cols(t, P)], w[:, 2], start=True,
                                    stop=not relative)
                    if relative:
                        ins = pe.matmul(v_ps[:, t // 4, t % 4], K.ones[0:1, 0:P], v_bias[:],
                                        start=False, stop=True)
                ins.then_inc(S.v_ready, 1)

            @block.vector
            def _(dve):
                chain = Chain(dve, S.dve_chain)
                flat = lambda slot: qk_ps[:, slot].rearrange("p j n -> p (j n)")
                dve.wait_ge(S.q_ready, 1)
                if relative:
                    chain(dve.tensor_scalar(q_f[:], flat(0), small[:, 0:1], None, ALU.add))
                    dve.wait_ge(S.k_ready, 1)
                    chain(dve.tensor_scalar(k_f[:, 0], flat(1), small[:, 1:2], float(HD) ** -0.5,
                                            ALU.add, ALU.mult))
                    chain(dve.tensor_scalar(k_f[:, 1], k_f[:, 0], small[:, 3:4], None, ALU.add))
                    chain(dve.tensor_scalar(k_f[:, 2], k_f[:, 0], small[:, 4:5], None, ALU.add))
                else:
                    dve.wait_ge(S.turn_loaded, 16)
                    for i, dst in enumerate((q_f[:], k_f[:, 0])):
                        if i == 1:
                            dve.wait_ge(S.k_ready, 1)
                        chain(dve.tensor_tensor(dst, flat(i), turn[:, 0], ALU.mult))
                        dve.wait_ge(S.rotated_ready, i + 1)
                        ins = dve.tensor_tensor(rest[:], flat(2), turn[:, 1], ALU.mult)
                        ins.then_inc(S.ps_free, 1)
                        dve.wait_ge(S.ps_free, i + 1)
                        chain(dve.tensor_tensor(dst, dst, rest[:], ALU.add))
                    chain(dve.tensor_scalar(k_f[:, 0], k_f[:, 0], float(HD) ** -0.5, None, ALU.mult))
                split_parts(chain, dve, q_f[:], [parts[:, 0, i] for i in range(3)], rest[:])
                for kind in range(parts.shape[1] - 1):
                    split_parts(chain, dve, k_f[:, kind], [parts[:, 1 + kind, i] for i in range(3)],
                                rest[:])
                dve.wait_ge(S.v_ready, 1)
                chain(dve.tensor_copy(values[:, :, :, 0:HD],
                                      v_ps[:].rearrange("p a c (h d) -> p (a c) h d", d=HD)))


def attend_pair(nc, K, key, pair, parts, stack_q, stack_k, pick_f, values, v_f, qk, bias_cols,
                table, merged, relative):
    n_ops = qk.shape[1]
    half = T // QW
    units = [(t, h) for t in range(QT) for h in range(2)]
    n_units = len(units)
    e_lead = 6
    ring = 4
    with ExitStack() as ctx:
        M = Memory(nc, ctx)
        weights = M.sb(f"{key}_weights", [P, 3, T])
        turned = M.sb(f"{key}_turned", [P, 2, QT, P])
        neg_max = M.sb(f"{key}_neg_max", [P, n_units])
        recip = M.sb(f"{key}_recip", [P, QT, 2])
        s_ps = M.ps(f"{key}_s_ps", [P, 2, T])
        t_ps = M.ps(f"{key}_t_ps", [P, 2, 4, P])
        o_ps = M.ps(f"{key}_o_ps", [P, QW])
        o_sb = M.sb(f"{key}_o_sb", [P, QW])
        if relative:
            e_sb = M.sb(f"{key}_e_sb", [P, ring, 2, QW])
            band = M.sb(f"{key}_band", [P, ring, 2, BAND])
            e_ps = M.ps(f"{key}_e_ps", [P, QW])
            scratch = K.scratch
        with stage(nc, "scores_ready", "masked", "max_ready", "exps_ready", "turned_ready",
                   "copied_dve", "copied_act", "out_ready", "e_ready", "e_copied", "e_written_even",
                   "stacked", "stack_act", "stack_dve", "v_copied", "picked",
                   "e_written_odd", "band_loaded_even", "band_loaded_odd", "o_copied", "o_turned", "dve_chain") as (block, S):

            e_written = (S.e_written_even, S.e_written_odd)
            band_loaded = (S.band_loaded_even, S.band_loaded_odd)

            def nth(t):
                return 16 * (t // 2 + 1)

            def width(t):
                return T if relative else (t + 1) * P

            def blocks(t):
                return width(t) // P

            def near(t):
                return max(0, (t - 1) * P), min(T, (t + 2) * P)

            @block.gpsimd
            def _(pool):
                pool.tensor_copy(v_f[:, :, :, 0:HD + 1], values[:, :, bass.ds(pair * 2, 2), :]) \
                    .then_inc(S.v_copied, 1)
                pool.wait_ge(S.stacked, n_ops)
                following = (pair + 1) % PAIRS
                for i, stack in enumerate((stack_q, stack_k)):
                    pool.tensor_copy(pick_f[:, i].rearrange("p (i n) -> p i n", i=3),
                                     stack[:, bass.ds(following, 1)].squeeze()).then_inc(S.picked, 1)
                pool.wait_ge(S.picked, 2)

            @block.tensor
            def _(pe):
                def stack(i):
                    if i >= 2:
                        pe.wait_ge((S.stack_act, S.stack_dve)[i % 2], 1)
                    for j in range(half):
                        for part in range(3):
                            ins = pe.matmul(s_ps[:, i % 2, cols(j, QW)],
                                            pick_f[:, min(i, 1), cols(part, P)],
                                            parts[:, i, part, cols(j, QW)], start=(part == 0),
                                            stop=(part == 2))
                    ins.then_inc(S.stacked, 1)

                def positions(n):
                    t, h = units[n]
                    if n == 0:
                        pe.wait_ge(S.stack_act, 1)
                    if n >= 1:
                        pe.wait_ge(S.e_copied, n)
                    rows = slice(64 * h, 64 * h + 64)
                    pe.matmul(e_ps[:], qk[rows, 0, cols(t, P)], table[rows, :], start=True,
                              stop=True).then_inc(S.e_ready, 1)

                def scores(n):
                    t, h = units[n]
                    if n < 2:
                        pe.wait_ge(S.stack_act, n_ops // 2)
                        pe.wait_ge(S.stack_dve, n_ops // 2)
                    else:
                        pe.wait_ge(S.exps_ready, n - 1)
                    rows = slice(64 * h, 64 * h + 64)
                    if relative:
                        lo, hi = near(t)
                        spans = [(0, lo, 2), (lo, hi, 1), (hi, T, 3)]
                    else:
                        spans = [(0, width(t), 1)]
                    cuts = [(max(a, c), min(z, c + QW), kind) for a, z, kind in spans
                            for c in range(0, T, QW) if max(a, c) < min(z, c + QW)]
                    for a, z, kind in cuts:
                        ins = pe.matmul(s_ps[:, n % 2, a:z], qk[rows, 0, cols(t, P)],
                                        qk[rows, kind, a:z], start=True, stop=True)
                    ins.then_inc(S.scores_ready, 1)

                def turn(n):
                    t, h = units[n]
                    pe.wait_ge(S.exps_ready, n + 1)
                    if n >= 1:
                        pe.wait_ge(S.copied_dve, n)
                        pe.wait_ge(S.copied_act, n)
                    for j in range(blocks(t)):
                        ins = pe.transpose(t_ps[:, j // 4, j % 4], weights[:, n % 3, cols(j, P)],
                                           K.ident[:])
                    ins.then_inc(S.turned_ready, 1)

                def weighted(n):
                    t, h = units[n]
                    pe.wait_ge(S.copied_dve, n + 1)
                    pe.wait_ge(S.copied_act, n + 1)
                    if n == 0:
                        pe.wait_ge(S.v_copied, 1)
                    at = OUT_ROWS * (2 * (t // 4) + h)
                    for j in range(blocks(t)):
                        ins = pe.matmul(o_ps[at:at + OUT_ROWS, cols(t % 4, P)], v_f[:, j, h],
                                        turned[:, n % 2, j], start=(j == 0),
                                        stop=(j == blocks(t) - 1))
                    ins.then_inc(S.out_ready, 1)

                stack(0)
                stack(1)
                if relative:
                    for n in range(e_lead):
                        positions(n)
                        if n < 2:
                            stack(2 + n)
                for n in range(n_units + 3):
                    if n < n_units:
                        scores(n)
                    if relative and n + e_lead < n_units:
                        positions(n + e_lead)
                    if 2 <= n <= n_units + 1:
                        turn(n - 2)
                    if n >= 3:
                        weighted(n - 3)
                pe.wait_ge(S.o_copied, 1)
                for c in range(4):
                    ins = pe.transpose(t_ps[:, 0, c], o_sb[:, cols(c, P)], K.ident[:])
                ins.then_inc(S.o_turned, 1)

            @block.scalar
            def _(act):
                def copy_positions(n):
                    t, h = units[n]
                    act.wait_ge(S.e_ready, n + 1)
                    if t >= ring:
                        act.wait_ge(e_written[t % 2], nth(t - ring))
                    act.activation(e_sb[:, t % ring, h], e_ps[:], ACT.Copy).then_inc(S.e_copied, 1)

                def exps(n):
                    t, h = units[n]
                    act.wait_ge(S.max_ready, n + 1)
                    if n >= 3:
                        act.wait_ge(S.turned_ready, n - 2)
                    act.activation(weights[:, n % 3, 0:width(t)], s_ps[:, n % 2, 0:width(t)], ACT.Exp,
                                   bias=neg_max[:, n:n + 1]).then_inc(S.exps_ready, 1)

                def copy_turned(n):
                    t, h = units[n]
                    act.wait_ge(S.turned_ready, n + 1)
                    if n >= 2:
                        act.wait_ge(S.out_ready, n - 1)
                    if blocks(t) > 4:
                        act.activation(turned[:, n % 2, 4:blocks(t)], t_ps[:, 1, 0:blocks(t) - 4],
                                       ACT.Copy).then_inc(S.copied_act, 1)
                    else:
                        act.sem_inc(S.copied_act, 1)

                def copy_stacked(i):
                    act.wait_ge(S.stacked, i + 1)
                    kw = {"bias": bias_cols[:, i:i + 1]} if relative else {}
                    act.activation(qk[:, i], s_ps[:, i % 2], ACT.Identity, **kw) \
                        .then_inc(S.stack_act, 1)

                copy_stacked(0)
                if relative:
                    for n in range(e_lead):
                        copy_positions(n)
                        if n == 0:
                            copy_stacked(2)
                for n in range(n_units + 2):
                    if relative and n + e_lead < n_units:
                        copy_positions(n + e_lead)
                    if n < n_units:
                        exps(n)
                    if n >= 2:
                        copy_turned(n - 2)

            if relative:
                @block.sync
                def _(sp):
                    for t in range(QT + 1):
                        if t < QT:
                            sp.wait_ge(S.e_copied, 2 * (t + 1))
                            if t >= ring:
                                sp.wait_ge(band_loaded[t % 2], nth(t - ring))
                            if t >= 2:
                                sp.wait_ge(e_written[t % 2], nth(t - 2))
                            sp.dma_start(scratch[t % ring].rearrange("h p n -> p h n"),
                                         e_sb[:, t % ring]).then_inc(e_written[t % 2], 16)
                        if t >= 1:
                            r = t - 1
                            slot = scratch[r % ring]
                            sp.wait_ge(e_written[r % 2], nth(r))
                            if r >= 2:
                                sp.wait_ge(band_loaded[r % 2], nth(r - 2))
                            if r >= ring:
                                sp.wait_ge(S.masked, 2 * (r - ring + 1))
                            skewed = bass.AP(slot.tensor, slot.offset + P - 1,
                                             [[QW - 1, P], [P * QW, 2], [1, BAND]])
                            sp.dma_start(band[:, r % ring], skewed).then_inc(band_loaded[r % 2], 16)

            @block.vector
            def _(dve):
                chain = Chain(dve, S.dve_chain)

                def maxima(n):
                    t, h = units[n]
                    dve.wait_ge(S.scores_ready, n + 1)
                    if relative:
                        lo, hi = near(t)
                        at = lo - (t - 1) * P
                        dve.wait_ge(band_loaded[t % 2], nth(t))
                        add = band[:, t % ring, h, at:at + hi - lo]
                    else:
                        lo, hi = t * P, (t + 1) * P
                        add = K.causal[:]
                    dve.tensor_tensor(s_ps[:, n % 2, lo:hi], s_ps[:, n % 2, lo:hi], add, ALU.add) \
                        .then_inc(S.masked, 1)
                    dve.wait_ge(S.masked, n + 1)
                    dve.tensor_reduce(neg_max[:, n:n + 1], s_ps[:, n % 2, 0:width(t)], AX_X, ALU.max,
                                      negate=True).then_inc(S.max_ready, 1)

                def copy_turned(n):
                    t, h = units[n]
                    dve.wait_ge(S.turned_ready, n + 1)
                    if n >= 2:
                        dve.wait_ge(S.out_ready, n - 1)
                    k = min(4, blocks(t))
                    dve.tensor_copy(turned[:, n % 2, 0:k], t_ps[:, 0, 0:k]).then_inc(S.copied_dve, 1)

                for i in range(1, n_ops, 2):
                    dve.wait_ge(S.stacked, i + 1)
                    if relative:
                        dve.tensor_scalar(qk[:, i], s_ps[:, i % 2], bias_cols[:, i:i + 1], None,
                                          ALU.add).then_inc(S.stack_dve, 1)
                    else:
                        dve.tensor_copy(qk[:, i], s_ps[:, i % 2]).then_inc(S.stack_dve, 1)
                for n in range(n_units + 2):
                    if n < n_units:
                        maxima(n)
                    if n >= 2:
                        copy_turned(n - 2)
                dve.wait_ge(S.out_ready, n_units)
                dve.tensor_copy(o_sb[:], o_ps[:]).then_inc(S.o_copied, 1)
                dve.wait_ge(S.o_turned, 1)
                for i in range(2):
                    rows = t_ps[:, 0, 0:4, 64 * i:64 * i + 64].rearrange("q c (h d) -> q c h d", h=2)
                    total = recip[:, 4 * i:4 * i + 4]
                    chain(dve.reciprocal(total, rows[:, :, :, HD]))
                    out = merged[:, 4 * i:4 * i + 4, bass.ds(pair, 1), :].rearrange(
                        "p t o (h d) -> p t (o h) d", h=2)
                    chain(dve.tensor_tensor(out, rows[:, :, :, 0:HD],
                                            total.unsqueeze(3).to_broadcast([P, 4, 2, HD]), ALU.mult))


def merge_heads(nc, K, key, b, merged, x, w, relative):
    with ExitStack() as ctx:
        M = Memory(nc, ctx)
        half = T // QW
        rows = M.sb(f"{key}_rows", [P, T])
        m_ps = M.ps(f"{key}_m_ps", [P, half, QW])
        p_ps = M.ps(f"{key}_p_ps", [P, half, QW])
        with stage(nc, "turned_ready", "copied", "projected", "added") as (block, S):

            @block.tensor
            def _(pe):
                for t in range(QT):
                    ins = pe.transpose(m_ps[:, t // 4, cols(t % 4, P)],
                                       merged[:, t].rearrange("p a c -> p (a c)"), K.ident[:])
                ins.then_inc(S.turned_ready, 1)
                if not relative:
                    pe.wait_ge(S.copied, 1)
                    for j in range(half):
                        ins = pe.matmul(p_ps[:, j], w[:, 5], rows[:, cols(j, QW)], start=True,
                                        stop=True)
                    ins.then_inc(S.projected, 1)

            @block.vector
            def _(dve):
                dve.wait_ge(S.turned_ready, 1)
                src = m_ps
                if not relative:
                    dve.tensor_copy(rows[:], m_ps[:].rearrange("p j n -> p (j n)")) \
                        .then_inc(S.copied, 1)
                    dve.wait_ge(S.projected, 1)
                    src = p_ps
                out = x[:, bass.ts(b, T)]
                dve.tensor_tensor(out, out, src[:].rearrange("p j n -> p (j n)"), ALU.add) \
                    .then_inc(S.added, 1)
                dve.wait_ge(S.added, 1)



LEAVES, DEPTH3 = 16, 4
NODES = LEAVES - 1


def walk_tree(nc, K, name, xn, node_w, node_b, reach):
    with ExitStack() as ctx:
        M = Memory(nc, ctx)
        right = M.sb(f"{name}_right", [P, TILES, LEAVES])
        left = M.sb(f"{name}_left", [P, TILES, LEAVES])
        level = M.sb(f"{name}_level", [P, 2, TILES, LEAVES])
        scores = M.ps(f"{name}_scores", [P, TILES, LEAVES])
        with stage(nc, "scores_ready", "dve_chain") as (block, S):

            @block.tensor
            def _(pe):
                for t in range(TILES):
                    pe.matmul(scores[:, t], xn[:, cols(t, P)], node_w, start=True, stop=False)
                    last = pe.matmul(scores[:, t], K.ones[0:1, 0:P], node_b, start=False, stop=True)
                last.then_inc(S.scores_ready, 1)

            @block.vector
            def _(dve):
                chain = Chain(dve, S.dve_chain)
                chain(dve.memset(level[:, 0], 1.0))
                dve.wait_ge(S.scores_ready, 1)
                chain(dve.tensor_scalar(right[:], scores[:], 0.0, None, ALU.is_ge))
                chain(dve.tensor_scalar(left[:], right[:], -1.0, 1.0, ALU.mult, ALU.add))
                for d in range(DEPTH3):
                    n = 1 << d
                    here = level[:, d % 2, :, 0:n]
                    if d == DEPTH3 - 1:
                        below = reach[:]
                    else:
                        below = level[:, (d + 1) % 2, :, 0:2 * n]
                    below = below.rearrange("p t (n two) -> p t n two", two=2)
                    nodes = slice(n - 1, 2 * n - 1)
                    chain(dve.tensor_tensor(below[:, :, :, 0], here, left[:, :, nodes], ALU.mult))
                    chain(dve.tensor_tensor(below[:, :, :, 1], here, right[:, :, nodes], ALU.mult))


def block3_ffn(nc, K, W, xn, x):
    with ExitStack() as ctx:
        M = Memory(nc, ctx)
        qkv = [M.sb(f"b3f_{n}", [P, N]) for n in "qkv"]
        with ExitStack() as inner:
            I = Memory(nc, inner)
            halves = LEAVES // 2
            up = I.sb("b3f_up", [P, halves, P])
            down = I.sb("b3f_down", [P, halves, P])
            b1 = I.sb("b3f_b1", [P, halves])
            b2 = I.sb("b3f_b2", [LEAVES, P])
            node_w = I.sb("b3f_node_w", [P, LEAVES])
            node_b = I.sb("b3f_node_b", [1, LEAVES])
            reach = I.sb("b3f_reach", [P, TILES, LEAVES])
            gates = I.sb("b3f_gates", [LEAVES, N])
            for n, dst in zip("qkv", qkv):
                load(nc, f"b3f_{n}", [(up[:], W[f"b3f_{n}_up"]), (down[:], W[f"b3f_{n}_down"]),
                                      (b1[:], W[f"b3f_{n}_b1"]), (b2[:], W[f"b3f_{n}_b2"]),
                                      (node_w[:], W[f"b3f_{n}_node_w"]),
                                      (node_b[:], W[f"b3f_{n}_node_b"])])
                walk_tree(nc, K, f"b3f_{n}", xn, node_w[:], node_b[:], reach)
                to_rows(nc, K, f"b3f_{n}", reach, LEAVES, gates)
                chunks = [(up[:, c], b1[:, c:c + 1], down[:, c], K.pick16[:, c], c)
                          for c in range(halves)]
                mlp(nc, K, f"b3f_{n}", xn, dst, chunks, ACT.Relu, gates, LEAVES, b2[:], add=False)
        one_head(nc, K, qkv, x)


def one_head(nc, K, qkv, x):
    q_all, k_all, v_all = qkv
    scale = float(P) ** -0.5
    units = [(b, t) for b in range(B) for t in range(QT)]
    n_units = len(units)
    with ExitStack() as ctx:
        M = Memory(nc, ctx)
        v_rows = M.sb("b3f_v_rows", [P, TILES, P])
        weights = M.sb("b3f_weights", [P, 2, T])
        turned = M.sb("b3f_turned", [P, 2, QT, P])
        stats = M.sb("b3f_stats", [P, 4, n_units])
        s_ps = M.ps("b3f_s_ps", [P, 2, T])
        t_ps = M.ps("b3f_t_ps", [P, 2, 4, P])
        o_ps = M.ps("b3f_o_ps", [P, P])
        with stage(nc, "v_turned", "v_copied", "scores_ready", "max_ready", "exps_ready",
                   "weights_ready", "turned_ready", "copied_act", "copied_dve", "out_ready",
                   "stored", "dve_chain") as (block, S):

            @block.tensor
            def _(pe):
                for t in range(TILES):
                    if t % 8 == 0 and t > 0:
                        pe.wait_ge(S.v_copied, t // 8)
                    ins = pe.transpose(t_ps[:, t % 8 // 4, t % 4], v_all[:, cols(t, P)], K.ident[:])
                    if t % 8 == 7:
                        ins.then_inc(S.v_turned, 1)
                pe.wait_ge(S.v_copied, TILES // 8)
                for n in range(n_units + 2):
                    if n < n_units:
                        b, t = units[n]
                        if n >= 2:
                            pe.wait_ge(S.exps_ready, n - 1)
                        for j in range(T // QW):
                            ins = pe.matmul(s_ps[:, n % 2, cols(j, QW)],
                                            q_all[:, cols(b * QT + t, P)],
                                            k_all[:, cols(b * (T // QW) + j, QW)], start=True,
                                            stop=True)
                        ins.then_inc(S.scores_ready, 1)
                    if 1 <= n <= n_units:
                        m = n - 1
                        pe.wait_ge(S.weights_ready, m + 1)
                        pe.wait_ge(S.copied_dve, m)
                        pe.wait_ge(S.copied_act, m)
                        for j in range(QT):
                            ins = pe.transpose(t_ps[:, j // 4, j % 4], weights[:, m % 2, cols(j, P)],
                                               K.ident[:])
                        ins.then_inc(S.turned_ready, 1)
                    if n >= 2:
                        m = n - 2
                        b, t = units[m]
                        pe.wait_ge(S.copied_dve, m + 1)
                        pe.wait_ge(S.copied_act, m + 1)
                        pe.wait_ge(S.stored, m)
                        for j in range(QT):
                            ins = pe.matmul(o_ps[:], v_rows[:, b * QT + j], turned[:, m % 2, j],
                                            start=(j == 0), stop=(j == QT - 1))
                        ins.then_inc(S.out_ready, 1)

            @block.scalar
            def _(act):
                for n in range(n_units + 1):
                    if n < n_units:
                        act.wait_ge(S.max_ready, n + 1)
                        if n >= 2:
                            act.wait_ge(S.turned_ready, n - 1)
                        act.activation(weights[:, n % 2], s_ps[:, n % 2], ACT.Exp, scale=scale,
                                       bias=stats[:, 1, n:n + 1],
                                       accum_out=stats[:, 2, n:n + 1]).then_inc(S.exps_ready, 1)
                    if n >= 1:
                        m = n - 1
                        act.wait_ge(S.turned_ready, m + 1)
                        if m >= 2:
                            act.wait_ge(S.out_ready, m - 1)
                        act.activation(turned[:, m % 2, 4:], t_ps[:, 1], ACT.Copy) \
                            .then_inc(S.copied_act, 1)

            @block.vector
            def _(dve):
                chain = Chain(dve, S.dve_chain)
                for i in range(TILES // 8):
                    dve.wait_ge(S.v_turned, i + 1)
                    dve.tensor_copy(v_rows[:, 8 * i:8 * i + 8], t_ps[:].rearrange("p a c n -> p (a c) n")) \
                        .then_inc(S.v_copied, 1)
                for n in range(n_units + 2):
                    if n < n_units:
                        dve.wait_ge(S.scores_ready, n + 1)
                        chain(dve.tensor_reduce(stats[:, 0, n:n + 1], s_ps[:, n % 2], AX_X, ALU.max))
                        dve.tensor_scalar(stats[:, 1, n:n + 1], stats[:, 0, n:n + 1], -scale, None,
                                          ALU.mult).then_inc(S.max_ready, 1)
                        dve.wait_ge(S.exps_ready, n + 1)
                        chain(dve.reciprocal(stats[:, 3, n:n + 1], stats[:, 2, n:n + 1]))
                        dve.tensor_scalar(weights[:, n % 2], weights[:, n % 2], stats[:, 3, n:n + 1],
                                          None, ALU.mult).then_inc(S.weights_ready, 1)
                    if 1 <= n <= n_units:
                        m = n - 1
                        dve.wait_ge(S.turned_ready, m + 1)
                        if m >= 2:
                            dve.wait_ge(S.out_ready, m - 1)
                        dve.tensor_copy(turned[:, m % 2, 0:4], t_ps[:, 0]).then_inc(S.copied_dve, 1)
                    if n >= 2:
                        b, t = units[n - 2]
                        dve.wait_ge(S.out_ready, n - 1)
                        out = x[:, cols(b * QT + t, P)]
                        dve.tensor_tensor(out, out, o_ps[:], ALU.add).then_inc(S.stored, 1)
                dve.wait_ge(S.stored, n_units)



LAYERS, HD2, WIN = 6, 64, 32
WINS = P // WIN
INNER = HEADS * HD2
FF, FF_PAD = 341, 384
LEAD = WIN
SEQ_COLS = LEAD + T
QK_SCALE = 8.0
TURNS = 6


def block2_ffn(nc, K, W, xn, x):
    with ExitStack() as ctx:
        M = Memory(nc, ctx)
        cur_all = M.sb("b2f_cur", [P, 3 * P + N])
        mid_all = M.sb("b2f_mid", [P, 3 * P + N])
        G = Names(
            cur_all=cur_all, mid_all=mid_all, cur=cur_all[:, 2 * P:2 * P + N], mid=mid_all[:, 2 * P:2 * P + N],
            shifted=M.sb("b2f_shifted", [P, B * SEQ_COLS + 3 * (LEAD + P)]),
            wqkv=M.sb("b2f_wqkv", [P, 3 * INNER]), wo=M.sb("b2f_wo", [P, PAIRS, P]),
            w1=M.sb("b2f_w1", [P, 6, P]), w2=M.sb("b2f_w2", [P, 3, P]),
            small=M.sb("b2f_small", [P, 9]), scales=M.sb("b2f_scales", [P, 4, HD2]),
            rotary=M.sb("b2f_rotary", [P, QT, 4, HD2]), mask=M.sb("b2f_mask", [P, QT, HD2]),
            qt=M.sb("b2f_qt", [P, PAIRS, P]), kt=M.sb("b2f_kt", [P, PAIRS, WIN + P]),
            values=M.sb("b2f_values", [P, 2, WINS, PAIRS * HD2]),
            o_rows=M.sb("b2f_o_rows", [P, PAIRS, 2, HD2]), minus_half=M.sb("b2f_minus_half", [P, 2 * HEADS]),
            xt=M.sb("b2f_xt", [P, WIN + P]),
            turn=M.sb("b2f_turn", [P, 2, 4, HD2]), mask_t=M.sb("b2f_mask_t", [P, 2, HD2]),
            keep=M.sb("b2f_keep", [P, QT]), keep_t=M.sb("b2f_keep_t", [P, 1]))
        with stage(nc, "copied") as (block, S):

            @block.vector
            def _(dve):
                dve.memset(G.cur_all[:, 0:2 * P], 0.0).then_inc(S.copied, 1)
                dve.memset(G.o_rows[:], 0.0).then_inc(S.copied, 1)
                dve.memset(G.minus_half[:], -0.5).then_inc(S.copied, 1)
                dve.memset(G.qt[:], 0.0).then_inc(S.copied, 1)
                dve.memset(G.values[:], 0.0).then_inc(S.copied, 1)
                dve.memset(G.mask_t[:], 0.0).then_inc(S.copied, 1)
                dve.tensor_copy(G.cur, xn[:]).then_inc(S.copied, 1)
                dve.memset(G.shifted[:], 0.0).then_inc(S.copied, 1)
                dve.memset(G.kt[:], 0.0).then_inc(S.copied, 1)
                dve.wait_ge(S.copied, 9)
        load(nc, "b2f_mask", [(G.mask[:], W["c_local_mask"]), (G.keep[:], W["c_keep"])])
        with nc.Fori(0, LAYERS) as layer:
            layer_weights(nc, W, G, layer)
            with nc.Fori(0, (TILES + 2) // TURNS) as i:
                local_tiles(nc, K, G, i * TURNS)
            shift_tokens(nc, G.mid, G.shifted, 0)
            layer_norm(nc, K, "b2n", G.shifted, G.shifted, gain=G.small[:, 0:1],
                       offset=G.small[:, 1:2])
            gated_ffn(nc, K, G)
        add_tokens(nc, x[:], G.cur)


def shift_tokens(nc, src, dst, lead):
    with stage(nc, "moved") as (block, S):
        step = lead + T

        @block.vector
        def _(dve):
            for b in range(B):
                at = b * step + lead
                dve.tensor_copy(dst[0:64, at:at + T], src[0:64, b * T:(b + 1) * T]).then_inc(S.moved, 1)
                dve.memset(dst[64:P, at:at + 1], 0.0).then_inc(S.moved, 1)

        @block.gpsimd
        def _(pool):
            for b in range(B):
                at = b * step + lead
                pool.tensor_copy(dst[64:P, at + 1:at + T], src[64:P, b * T:(b + 1) * T - 1]) \
                    .then_inc(S.moved, 1)
            pool.wait_ge(S.moved, 3 * B)


def layer_weights(nc, W, G, layer):
    with stage(nc, "loaded", "scaled") as (block, S):

        @block.sync
        def _(sp):
            i = layer
            sp.dma_start(G.wqkv[:], W["b2f_wqkv"][bass.ds(i, 1)].squeeze()).then_inc(S.loaded, 16)
            sp.dma_start(G.wo[:], W["b2f_wo"][bass.ds(i, 1)].squeeze()).then_inc(S.loaded, 16)
            sp.dma_start(G.w1[:], W["b2f_w1"][bass.ds(i, 1)].squeeze()).then_inc(S.loaded, 16)
            sp.dma_start(G.w2[:], W["b2f_w2"][bass.ds(i, 1)].squeeze()).then_inc(S.loaded, 16)
            sp.dma_start(G.small[:], W["b2f_small"][bass.ds(i, 1)].squeeze()).then_inc(S.loaded, 16)
            sp.dma_start(G.scales[:], W["b2f_scales"][bass.ds(i, 1)].squeeze()).then_inc(S.loaded, 16)
            sp.dma_start(G.rotary[:], W["c_rotary2"]).then_inc(S.loaded, 16)

        @block.vector
        def _(dve):
            dve.wait_ge(S.loaded, 16 * 7)
            dve.tensor_tensor(G.rotary[:], G.rotary[:],
                              G.scales[:].unsqueeze(1).to_broadcast([P, QT, 4, HD2]), ALU.mult) \
                .then_inc(S.scaled, 1)
            dve.wait_ge(S.scaled, 1)
    shift_tokens(nc, G.cur, G.shifted, LEAD)


def local_tiles(nc, K, G, first):
    with ExitStack() as ctx:
        M = Memory(nc, ctx)
        sq = M.sb("b2t_sq", [P, 2 * HEADS, HD2])
        part = M.sb("b2t_part", [P, 2 * HEADS, HD2])
        qk = M.sb("b2t_qk", [P, 2 * HEADS, HD2])
        norm = M.sb("b2t_norm", [P, 2 * HEADS])
        prob = M.sb("b2t_prob", [P, PAIRS, 2, HD2])
        top = M.sb("b2t_top", [P, PAIRS, 2])
        total = M.sb("b2t_total", [P, PAIRS, 2])
        pt = M.sb("b2t_pt", [P, PAIRS, P])
        o_cols = M.sb("b2t_o_cols", [P, PAIRS, P])
        qk_ps = M.ps("b2t_qk_ps", [P, 4, QW])
        s_ps = M.ps("b2t_s_ps", [P, 2, QW])
        w_ps = M.ps("b2t_w_ps", [P, 2, QW])
        with stage(nc, "xt_loaded", "qk_ready", "squared", "inverted", "summed", "normed",
                   "qk_turned", "qt_copied", "kt_carried", "scores_ready", "masked", "shifted",
                   "exps_ready", "probs_ready", "probs_turned", "pt_low", "pt_high", "out_ready",
                   "o_copied", "o_turned", "o_taken", "y_ready", "y_stored", "v_ready", "v_copied",
                   "v_carried", "table_loaded", "mask_loaded", "dve_chain",
                   "pool_chain") as (block, S):
            PER = {"qk_ready": 4, "squared": 4, "summed": 2, "inverted": 2, "normed": 2,
                   "qk_turned": 4, "qt_copied": 4, "probs_turned": 2, "out_ready": 2,
                   "o_copied": 2, "o_turned": 2, "o_taken": 2, "v_copied": 10, "v_carried": 2}

            def due(k, name, n):
                return k * PER.get(name, 1) + n

            @block.gpsimd
            def _(pool):
                chain = Chain(pool, S.pool_chain)

                def load_turn(k):
                    tile = first + k
                    if k:
                        pool.wait_ge(S.v_ready, due(k, "v_ready", 0))
                    pool.tensor_copy(G.xt[:], G.shifted[:, bass.ds(tile * P + (tile // QT) * LEAD,
                                                                   WIN + P)]).then_inc(S.xt_loaded, 1)
                    if k >= 2:
                        pool.wait_ge(S.normed, due(k - 1, "normed", 0))
                    pool.tensor_copy(G.turn[:, k % 2], G.rotary[:, bass.ds(tile % QT, 1)].squeeze()) \
                        .then_inc(S.table_loaded, 1)
                    if k:
                        pool.wait_ge(S.masked, due(k, "masked", 0))
                    pool.tensor_copy(G.mask_t[:, k % 2], G.mask[:, bass.ds(tile % QT, 1)].squeeze()) \
                        .then_inc(S.mask_loaded, 1)
                    chain(pool.tensor_copy(G.keep_t[:], G.keep[:, bass.ds(tile % QT, 1)]))

                for k in range(TURNS):
                    if k == 0:
                        load_turn(0)
                    if k:
                        pool.wait_ge(S.out_ready, due(k, "out_ready", 0))
                        pool.wait_ge(S.v_copied, due(k, "v_copied", 0))
                        pool.wait_ge(S.inverted, due(k, "inverted", 0))
                    for h in range(2):
                        pool.tensor_copy(G.values[HD2 * h:HD2 * h + WIN, k % 2, 0],
                                         G.values[HD2 * h + WIN:HD2 * h + 2 * WIN, 1 - k % 2,
                                                  WINS - 1]).then_inc(S.v_carried, 1)
                        pool.wait_ge(S.v_carried, due(k, "v_carried", h + 1))
                    pool.wait_ge(S.scores_ready, due(k, "scores_ready", 1))
                    pool.tensor_scalar(G.kt[:, :, 0:WIN], G.kt[:, :, P:P + WIN], G.keep_t[:], None,
                                       ALU.mult).then_inc(S.kt_carried, 1)
                    for i in range(2):
                        pool.wait_ge(S.summed, due(k, "summed", i + 1))
                        pool.tensor_tensor(norm[:, cols(i, HEADS)], norm[:, cols(i, HEADS)],
                                           G.minus_half[:, cols(i, HEADS)], ALU.pow) \
                            .then_inc(S.inverted, 1)
                    if k + 1 < TURNS:
                        pool.wait_ge(S.kt_carried, due(k, "kt_carried", 1))
                        load_turn(k + 1)

            @block.tensor
            def _(pe):
                def project(j):
                    pe.matmul(qk_ps[:, j], G.xt[:, WIN:], G.wqkv[:, cols(j, QW)], start=True,
                              stop=True).then_inc(S.qk_ready, 1)

                def turn_features(k, j):
                    for c in range(4):
                        n = 4 * j + c
                        src = qk[:, 2 * n:2 * n + 2].rearrange("t h d -> t (h d)")
                        ins = pe.transpose(qk_ps[:, j, cols(c, P)], src, K.ident[:])
                    ins.then_inc(S.qk_turned, 1)

                for k in range(TURNS):
                    if k == 0:
                        pe.wait_ge(S.xt_loaded, 1)
                        project(0)
                        project(1)
                    if k:
                        pe.wait_ge(S.qt_copied, due(k, "qt_copied", 0))
                        pe.wait_ge(S.o_copied, due(k, "o_copied", 0))
                    for h in range(2):
                        rows = slice(HD2 * h, HD2 * h + HD2)
                        for p in range(PAIRS):
                            for w in range(WINS):
                                ins = pe.matmul(s_ps[WIN * w:WIN * w + WIN, h, cols(p, HD2)],
                                                G.qt[rows, p, cols(w, WIN)],
                                                G.kt[rows, p, WIN * w:WIN * w + 2 * WIN],
                                                start=True, stop=True)
                    ins.then_inc(S.scores_ready, 1)
                    project(2)
                    project(3)
                    if k:
                        pe.wait_ge(S.y_stored, due(k, "y_stored", 0))
                    wv = G.wqkv[:, 2 * INNER:].rearrange("k (p h d) -> k p h d", h=2, d=HD2)
                    for h in range(2):
                        ins = pe.matmul(w_ps[:, h], G.xt[:, WIN:], wv[:, :, h], start=True, stop=True)
                    ins.then_inc(S.v_ready, 1)
                    pe.wait_ge(S.masked, due(k, "masked", 1))
                    for p in range(PAIRS):
                        ins = pe.transpose(s_ps[:, p // 4, cols(p % 4, P)],
                                           G.o_rows[:, p].rearrange("q h d -> q (h d)"), K.ident[:])
                        if p % 4 == 3:
                            ins.then_inc(S.o_turned, 1)
                    pe.wait_ge(S.probs_ready, due(k, "probs_ready", 1))
                    pe.wait_ge(S.v_copied, due(k, "v_copied", PER["v_copied"]))
                    for p in (4, 5, 6, 7, 0, 1, 2, 3):
                        ins = pe.transpose(w_ps[:, p // 4, cols(p % 4, P)],
                                           prob[:, p].rearrange("q h j -> q (h j)"), K.ident[:])
                        if p % 4 == 3:
                            ins.then_inc(S.probs_turned, 1)
                    pe.wait_ge(S.o_taken, due(k, "o_taken", 2))
                    pe.wait_ge(S.pt_high, due(k, "pt_high", 1))
                    for p in range(PAIRS):
                        ins = pe.matmul(w_ps[:, 1, 0:P], G.wo[:, p], o_cols[:, p], start=(p == 0),
                                        stop=(p == PAIRS - 1))
                    ins.then_inc(S.y_ready, 1)
                    if k:
                        pe.wait_ge(S.v_carried, due(k, "v_carried", 0))
                    pe.wait_ge(S.pt_low, due(k, "pt_low", 1))
                    for h in range(2):
                        rows = slice(HD2 * h, HD2 * h + HD2)
                        for p in range(PAIRS):
                            for w in range(WINS):
                                ins = pe.matmul(s_ps[WIN * w:WIN * w + WIN, h, cols(p, HD2)],
                                                pt[rows, p, cols(w, WIN)],
                                                G.values[rows, 1 - k % 2, w, cols(p, HD2)],
                                                start=True, stop=True)
                        ins.then_inc(S.out_ready, 1)
                    pe.wait_ge(S.normed, due(k, "normed", 1))
                    turn_features(k, 0)
                    turn_features(k, 1)
                    if k + 1 < TURNS:
                        pe.wait_ge(S.xt_loaded, due(k + 1, "xt_loaded", 1))
                        for j in range(2):
                            pe.wait_ge(S.qt_copied, due(k, "qt_copied", j + 1))
                            project(j)
                    pe.wait_ge(S.normed, due(k, "normed", 2))
                    turn_features(k, 2)
                    turn_features(k, 3)

            @block.scalar
            def _(act):
                def square(k, j):
                    if k and j % 2 == 0:
                        act.wait_ge(S.summed, due(k - 1, "summed", j // 2 + 1))
                    act.wait_ge(S.qk_ready, due(k, "qk_ready", j + 1))
                    act.activation(sq[:, 8 * j:8 * j + 8].rearrange("t h d -> t (h d)"),
                                   qk_ps[:, j], ACT.Square).then_inc(S.squared, 1)

                def copy_features(k, j, dst):
                    act.wait_ge(S.qk_turned, due(k, "qk_turned", j + 1))
                    act.activation(dst, qk_ps[:, j].rearrange("p (c n) -> p c n", c=4), ACT.Copy) \
                        .then_inc(S.qt_copied, 1)

                for k in range(TURNS):
                    if k == 0:
                        square(0, 0)
                        square(0, 1)
                    square(k, 2)
                    square(k, 3)
                    act.wait_ge(S.shifted, due(k, "shifted", 1))
                    act.activation(prob[:], prob[:], ACT.Exp).then_inc(S.exps_ready, 1)
                    act.wait_ge(S.v_ready, due(k, "v_ready", 1))
                    if k:
                        act.wait_ge(S.out_ready, due(k, "out_ready", 0))
                        act.wait_ge(S.v_carried, due(k, "v_carried", 0))
                    for h in range(2):
                        for w, src, dst, n in ((1, 0, 0, 64), (3, 64, 0, 64), (2, 32, 0, 32),
                                               (2, 64, 32, 32), (0, 0, 32, 32)):
                            at = HD2 * h + dst
                            act.activation(G.values[at:at + n, k % 2, w], w_ps[src:src + n, h],
                                           ACT.Copy).then_inc(S.v_copied, 1)
                    act.wait_ge(S.probs_turned, due(k, "probs_turned", 1))
                    if k:
                        act.wait_ge(S.out_ready, due(k, "out_ready", 0))
                    act.activation(pt[:, 4:], w_ps[:, 1], ACT.Copy).then_inc(S.pt_high, 1)
                    act.wait_ge(S.o_turned, due(k, "o_turned", 2))
                    for h in range(2):
                        act.wait_ge(S.out_ready, due(k, "out_ready", h + 1))
                        act.activation(G.o_rows[:, :, h],
                                       s_ps[:, h].rearrange("q (p d) -> q p d", d=HD2), ACT.Copy) \
                            .then_inc(S.o_copied, 1)
                    copy_features(k, 0, G.qt[:, 0:4])
                    copy_features(k, 1, G.qt[:, 4:8])
                    if k + 1 < TURNS:
                        square(k + 1, 0)
                        square(k + 1, 1)
                    act.wait_ge(S.kt_carried, due(k, "kt_carried", 1))
                    copy_features(k, 2, G.kt[:, 0:4, WIN:])
                    copy_features(k, 3, G.kt[:, 4:8, WIN:])
                act.wait_ge(S.qt_copied, due(TURNS, "qt_copied", 0))

            @block.vector
            def _(dve):
                chain = Chain(dve, S.dve_chain)
                half = HD2 // 2
                raw = qk_ps[:].rearrange("t j n -> t (j n)").rearrange("t (k h d) -> t k h d",
                                                                       k=2, h=HEADS)
                qk_v = qk[:].rearrange("t (k h) d -> t k h d", k=2)
                part_v = part[:].rearrange("t (k h) d -> t k h d", k=2)

                def rotate(k, i):
                    dve.wait_ge(S.squared, due(k, "squared", 2 * i + 2))
                    cos = G.turn[:, k % 2, 2 * i:2 * i + 1].to_broadcast([P, HEADS, HD2])
                    dve.tensor_tensor(qk_v[:, i], raw[:, i], cos, ALU.mult).then_inc(S.dve_chain, 1)
                    for lo, hi in ((0, half), (half, 0)):
                        sin = G.turn[:, k % 2, 2 * i + 1:2 * i + 2, lo:lo + half].to_broadcast(
                            [P, HEADS, half])
                        dve.tensor_tensor(part_v[:, i, :, lo:lo + half], raw[:, i, :, hi:hi + half],
                                          sin, ALU.mult).then_inc(S.dve_chain, 1)
                    chain.n += 3
                    dve.wait_ge(S.dve_chain, chain.n)
                    chain(dve.tensor_tensor(qk_v[:, i], qk_v[:, i], part_v[:, i], ALU.add))

                def lengths(k, i):
                    part_n = norm[:, cols(i, HEADS)]
                    dve.wait_ge(S.squared, due(k, "squared", 2 * i + 2))
                    if k:
                        dve.wait_ge(S.normed, due(k - 1, "normed", i + 1))
                    chain(dve.tensor_reduce(part_n, sq[:, cols(i, HEADS)], AX_X, ALU.add))
                    dve.tensor_scalar(part_n, part_n, 1e-24, None, ALU.max).then_inc(S.summed, 1)

                def normalise(k, i):
                    dve.wait_ge(S.inverted, due(k, "inverted", i + 1))
                    dve.tensor_tensor(qk_v[:, i], qk_v[:, i],
                                      norm[:, cols(i, HEADS)].unsqueeze(2).to_broadcast(
                                          [P, HEADS, HD2]), ALU.mult).then_inc(S.normed, 1)

                for k in range(TURNS):
                    dve.wait_ge(S.table_loaded, due(k, "table_loaded", 1))
                    if k:
                        dve.wait_ge(S.qk_turned, due(k, "qk_turned", -2))
                    rotate(k, 0)
                    lengths(k, 0)
                    dve.wait_ge(S.scores_ready, due(k, "scores_ready", 1))
                    if k:
                        dve.wait_ge(S.probs_turned, due(k, "probs_turned", 0))
                        dve.wait_ge(S.mask_loaded, k)
                    for h in range(2):
                        ins = dve.scalar_tensor_tensor(
                            out=prob[:, :, h], in0=s_ps[:, h].rearrange("q (p j) -> q p j", p=PAIRS),
                            scalar=QK_SCALE,
                            in1=G.mask_t[:, 1 - k % 2].unsqueeze(1).to_broadcast([P, PAIRS, HD2]),
                            op0=ALU.mult, op1=ALU.add)
                        if h == 0:
                            chain(ins)
                    ins.then_inc(S.masked, 1)
                    dve.wait_ge(S.masked, k + 1)
                    chain(dve.tensor_reduce(top[:], prob[:], AX_X, ALU.max))
                    flat = prob[:].rearrange("q p h j -> q (p h) j")
                    bc = lambda a: a[:].rearrange("q p h -> q (p h)").unsqueeze(2).to_broadcast(
                        [P, HEADS, HD2])
                    dve.tensor_tensor(flat, flat, bc(top), ALU.subtract).then_inc(S.shifted, 1)
                    lengths(k, 1)
                    dve.wait_ge(S.exps_ready, due(k, "exps_ready", 1))
                    chain(dve.tensor_reduce(total[:], prob[:], AX_X, ALU.add))
                    chain(dve.reciprocal(total[:], total[:]))
                    dve.tensor_tensor(flat, flat, bc(total), ALU.mult).then_inc(S.probs_ready, 1)
                    if k:
                        dve.wait_ge(S.y_ready, due(k, "y_ready", 0))
                    for i in range(2):
                        dve.wait_ge(S.o_turned, due(k, "o_turned", i + 1))
                        dve.tensor_copy(o_cols[:, 4 * i:4 * i + 4],
                                        s_ps[:, i].rearrange("p (a n) -> p a n", a=4)) \
                            .then_inc(S.o_taken, 1)
                    dve.wait_ge(S.probs_turned, due(k, "probs_turned", 2))
                    if k:
                        dve.wait_ge(S.out_ready, due(k, "out_ready", 0))
                    dve.tensor_copy(pt[:, 0:4], w_ps[:, 0].rearrange("p (a n) -> p a n", a=4)) \
                        .then_inc(S.pt_low, 1)
                    normalise(k, 0)
                    dve.wait_ge(S.y_ready, due(k, "y_ready", 1))
                    dve.tensor_tensor(G.mid_all[:, bass.ds((first + k) * P, P)],
                                      G.cur_all[:, bass.ds((first + k) * P, P)], w_ps[:, 1, 0:P],
                                      ALU.add).then_inc(S.y_stored, 1)
                    if k:
                        dve.wait_ge(S.qk_turned, due(k, "qk_turned", 0))
                    rotate(k, 1)
                    normalise(k, 1)
                dve.wait_ge(S.normed, due(TURNS, "normed", 0))


def gated_ffn(nc, K, G):
    chunks = FF_PAD // P
    units = [(q, c) for q in range(QUARTERS) for c in range(chunks)]
    with ExitStack() as ctx:
        M = Memory(nc, ctx)
        gate = M.sb("b2g_gate", [P, 3, QW])
        hidden = M.sb("b2g_hidden", [P, 3, QW])
        a_ps = M.ps("b2g_a_ps", [P, 2, QW])
        g_ps = M.ps("b2g_g_ps", [P, 2, QW])
        y_ps = M.ps("b2g_y_ps", [P, 2, QW])
        with stage(nc, "g_ready", "a_ready", "gelu_ready", "hidden_ready", "y_added",
                   "stored") as (block, S):

            @block.tensor
            def _(pe):
                for u in range(len(units) + 2):
                    if u < len(units):
                        q, c = units[u]
                        if u >= 2:
                            pe.wait_ge(S.hidden_ready, u - 1)
                        x_q = G.shifted[:, cols(q, QW)]
                        pe.matmul(g_ps[:, u % 2], G.w1[:, chunks + c], x_q, start=True, stop=True) \
                            .then_inc(S.g_ready, 1)
                        pe.matmul(a_ps[:, u % 2], G.w1[:, c], x_q, start=True, stop=True) \
                            .then_inc(S.a_ready, 1)
                    if u >= 2:
                        q, c = units[u - 2]
                        pe.wait_ge(S.hidden_ready, u - 1)
                        if c == 0 and q >= 2:
                            pe.wait_ge(S.stored, q - 1)
                        pe.matmul(y_ps[:, q % 2], G.w2[:, c], hidden[:, (u - 2) % 3],
                                  start=(c == 0), stop=(c == chunks - 1)).then_inc(S.y_added, 1)

            @block.scalar
            def _(act):
                for u, (q, c) in enumerate(units):
                    act.wait_ge(S.g_ready, u + 1)
                    if u >= 3:
                        act.wait_ge(S.hidden_ready, u - 2)
                    act.activation(gate[:, u % 3], g_ps[:, u % 2], ACT.Gelu,
                                   bias=G.small[:, 5 + c:6 + c]).then_inc(S.gelu_ready, 1)

            @block.vector
            def _(dve):
                for u, (q, c) in enumerate(units):
                    dve.wait_ge(S.gelu_ready, u + 1)
                    dve.wait_ge(S.a_ready, u + 1)
                    if u >= 3:
                        dve.wait_ge(S.y_added, u - 2)
                    dve.scalar_tensor_tensor(out=hidden[:, u % 3], in0=a_ps[:, u % 2],
                                             scalar=G.small[:, 2 + c:3 + c], in1=gate[:, u % 3],
                                             op0=ALU.add, op1=ALU.mult).then_inc(S.hidden_ready, 1)
                    if c == chunks - 1:
                        dve.wait_ge(S.y_added, u + 1)
                        dve.scalar_tensor_tensor(out=G.cur[:, cols(q, QW)], in0=y_ps[:, q % 2],
                                                 scalar=G.small[:, 8:9], in1=G.mid[:, cols(q, QW)],
                                                 op0=ALU.add, op1=ALU.add).then_inc(S.stored, 1)
                dve.wait_ge(S.stored, QUARTERS)



def rotary_tables2():
    f = np.float32
    half = np.arange(0, HD2, 2, dtype=f)
    inv_freq = (1.0 / (f(10000.0) ** (half / f(HD2)))).astype(f)
    t = np.arange(T, dtype=f)
    freqs = (t[:, None] * inv_freq[None, :]).astype(f)
    freqs = np.concatenate([freqs, freqs], -1)
    base = ((half + f(0.4 * HD2)) / f(1.4 * HD2)).astype(f)
    power = ((t - T // 2) / f(WIN // 2)).astype(f)
    scale = (base[None, :] ** power[:, None]).astype(f)
    scale = np.concatenate([scale, scale], -1)
    sign = np.where(np.arange(HD2) < HD2 // 2, f(-1.0), f(1.0))
    table = np.stack([np.cos(freqs) * scale, np.sin(freqs) * scale * sign,
                      np.cos(freqs) / scale, np.sin(freqs) / scale * sign], axis=1).astype(f)
    return table.reshape(QT, P, 4, HD2).transpose(1, 0, 2, 3)


def local_mask():
    i = np.arange(P)[:, None] % WIN
    j = np.arange(2 * WIN)[None, :]
    seen = (j >= i) & (j <= i + WIN)
    first = seen & ((j >= WIN) | (np.arange(P)[:, None] >= WIN))
    m = np.repeat(seen[:, None], QT, 1)
    m[:, 0] = first
    return np.where(m, 0.0, -3e38).astype(np.float32)


def stack_matrix(slots):
    m = np.zeros((P, PAIRS, 3, P), np.float32)
    for pair in range(PAIRS):
        for h in range(2):
            for slot, part in enumerate(slots):
                for d in range(HD):
                    m[(2 * pair + h) * HD + d, pair, part, 64 * h + HD * slot + d] = 1.0
    return m


def rotary_heads():
    freq = (1.0 / 10000.0 ** (np.arange(0, HD, 2, dtype=np.float32) / HD)).astype(np.float32)
    angle = np.arange(T, dtype=np.float32)[None, :] * freq[:, None]
    angle = angle.astype(np.float32)
    table = np.zeros((HD, 2, T), np.float32)
    table[0::2, 0] = table[1::2, 0] = np.cos(angle)
    table[0::2, 1] = -np.sin(angle)
    table[1::2, 1] = np.sin(angle)
    return np.tile(table, (HEADS, 1, 1))


def row_masks():
    m = np.zeros((P, 4), np.float32)
    for h in range(2):
        for slot, part in enumerate(SLOTS_K):
            m[64 * h + HD * slot:64 * h + HD * (slot + 1), part] = 1.0
        for part in range(3):
            m[64 * h + ONES_AT + part, part] = 1.0
            m[64 * h + ONES_AT + part, 3] = 1.0
    return m


def pick_matrix(experts, per_expert):
    chunks = max(1, experts * per_expert // P)
    if per_expert >= P:
        m = np.zeros((experts, experts, P), np.float32)
        m[np.arange(experts), np.arange(experts)] = 1.0
        return m
    m = np.zeros((experts, chunks, P), np.float32)
    for c in range(chunks):
        for p in range(P):
            m[(c * P + p) // per_expert, c, p] = 1.0
    return m


def constants():
    return {
        "c_ident": np.eye(P, dtype=np.float32),
        "c_mean": np.full((P, P), 1.0 / P, np.float32),
        "c_ones": np.ones((P, QW), np.float32),
        "c_pick16": pick_matrix(16, 64),
        "c_pick4": pick_matrix(4, 512),
        "c_pick9": pick_matrix(9, 512),
        "c_one_row": np.ones((1, N), np.float32),
        "c_stack_q": stack_matrix(SLOTS_Q).astype(BF16_NP),
        "c_stack_k": stack_matrix(SLOTS_K).astype(BF16_NP),
        "c_turn": rotary_heads(),
        "c_rotary2": rotary_tables2(),
        "c_local_mask": local_mask(),
        "c_keep": np.repeat((np.arange(QT) > 0).astype(np.float32)[None], P, 0),
        "c_causal": np.where(np.tril(np.ones((P, P))) > 0, 0.0, -1e10).astype(np.float32),
    }


def layouts(v):
    a = {}
    a["x"] = v["L0_attn_x"].reshape(N, P).T
    up = np.concatenate([v["L0_ffn_routed_up"], v["L0_ffn_shared_up"]]).reshape(9, P, P)
    a["b0f_up"] = up.transpose(2, 0, 1)
    down = np.concatenate([v["L0_ffn_routed_down"], v["L0_ffn_shared_down"]])
    a["b0f_down"] = down.transpose(0, 2, 1).reshape(9, P, P).transpose(1, 0, 2)
    a["b0f_router"] = v["L0_ffn_router_w"].T
    a["b0a_wd"] = v["L0_attn_Wd"]
    rep = lambda r: np.repeat(r.reshape(1, -1), P, 0)
    col = lambda c: c.reshape(P, 1)
    a["b0a_small"] = np.concatenate(
        [v["L0_attn_WB"], v["L0_attn_WC"], rep(v["L0_attn_bB"]), rep(v["L0_attn_bC"]),
         v["L0_attn_A_log"], col(v["L0_attn_D_param"]), col(v["L0_attn_bd"]), col(v["L0_attn_ln_w"]),
         col(v["L0_attn_ln_b"]), np.zeros((P, 4), np.float32)], axis=1)
    a["b0m_up"] = v["L0_attn_up_w"].reshape(4, P, 4, P).transpose(1, 0, 2, 3)
    a["b0m_down"] = v["L0_attn_down_w"].reshape(4, 4, P, P).transpose(2, 0, 1, 3)
    a["b0m_b1"] = v["L0_attn_up_b"].reshape(16, P).T
    a["b0m_b2"] = v["L0_attn_down_b"]
    a["b0m_router"] = v["L0_attn_Wr"]
    a["b0m_router_b"] = v["L0_attn_br"].reshape(1, 4)
    w1 = np.concatenate([v["L1_ffn_W1"], v["L1_ffn_Ws1"][None]])
    w2 = np.concatenate([v["L1_ffn_W2"], v["L1_ffn_Ws2"][None]])
    a["b1f_up"] = w1.reshape(9, P, 4, P).transpose(1, 0, 2, 3)
    a["b1f_down"] = w2.reshape(9, 4, P, P).transpose(2, 0, 1, 3)
    a["b1f_b1"] = np.concatenate([v["L1_ffn_b1"], v["L1_ffn_bs1"][None]]).reshape(36, P).T
    a["b1f_b2"] = np.concatenate([v["L1_ffn_b2"], v["L1_ffn_bs2"][None]])
    a["b1f_gate_w"] = v["L1_ffn_gate"]
    wqkv = v["L1_attn_Wqkv"].reshape(HEADS, 3, HD, P).transpose(3, 1, 0, 2).reshape(P, 3, P)
    bqkv = v["L1_attn_bqkv"].reshape(HEADS, 3, HD).transpose(1, 0, 2).reshape(3, P)
    a["b1a_w"] = wqkv
    a["b1a_v_bias"] = bqkv[2:3]
    wr, br = v["L1_attn_Wr"], v["L1_attn_br"]
    near_at = np.clip(np.arange(QW) - (2 * P - 1), -WINDOW1, WINDOW1) + WINDOW1
    masks = row_masks()
    positions = np.zeros((P, QW + 2), wr.dtype)
    for h in range(2):
        for slot in range(len(SLOTS_K)):
            rows = slice(64 * h + HD * slot, 64 * h + HD * (slot + 1))
            positions[rows, 0:QW] = wr[near_at].T
        rows = slice(64 * h + ONES_AT, 64 * h + ONES_AT + 3)
        positions[rows, 0:QW] = br[near_at]
        positions[rows, QW] = br[0]
        positions[rows, QW + 1] = br[-1]
    a["b1a_positions"] = positions
    a["b1a_small"] = np.concatenate(
        [bqkv.T, np.tile(wr[0], HEADS)[:, None], np.tile(wr[-1], HEADS)[:, None],
         np.zeros((P, 1), np.float32), masks, np.zeros((P, 2), np.float32)], axis=1)
    swap = np.arange(P) ^ 1
    a["b3a_w"] = np.stack([v["L3_attn_qw"], v["L3_attn_kw"], v["L3_attn_vw"],
                           v["L3_attn_qw"][:, swap], v["L3_attn_kw"][:, swap],
                           v["L3_attn_ow"]], axis=1)
    a["b2f_wqkv"] = v["L2_ffn_Wqkv"]
    a["b2f_wo"] = v["L2_ffn_Wo"].reshape(LAYERS, PAIRS, P, P).transpose(0, 2, 1, 3)
    zeros = lambda *shape: np.zeros(shape, np.float32)
    w1 = v["L2_ffn_W1"].reshape(LAYERS, P, 2, FF)
    a["b2f_w1"] = np.concatenate([w1, zeros(LAYERS, P, 2, FF_PAD - FF)], 3).reshape(LAYERS, P, 6, P)
    w2 = np.concatenate([v["L2_ffn_W2"], zeros(LAYERS, FF_PAD - FF, P)], 1)
    a["b2f_w2"] = w2.reshape(LAYERS, 3, P, P).transpose(0, 2, 1, 3)
    fb1 = np.concatenate([v["L2_ffn_b1"].reshape(LAYERS, 2, FF), zeros(LAYERS, 2, FF_PAD - FF)], 2)
    a["b2f_small"] = np.concatenate(
        [v["L2_ffn_ln_g"][:, :, None], v["L2_ffn_ln_b"][:, :, None],
         fb1.reshape(LAYERS, 6, P).transpose(0, 2, 1), v["L2_ffn_b2"][:, :, None]], axis=2)
    rot = np.arange(HD2) ^ (HD2 // 2)
    qs, ks = v["L2_ffn_q_scale"], v["L2_ffn_k_scale"]
    scales = np.stack([qs, qs[:, rot], ks, ks[:, rot]], axis=1)
    a["b2f_scales"] = np.repeat(scales[:, None], P, 1)
    for n in "qkv":
        f = lambda key: v[f"L3_ffn_{n}_{key}"]
        a[f"b3f_{n}_up"] = f("w1").reshape(8, 2, P, 64).transpose(2, 0, 1, 3).reshape(P, 8, P)
        a[f"b3f_{n}_down"] = f("w2").reshape(8, P, P).transpose(1, 0, 2)
        a[f"b3f_{n}_b1"] = f("b1").reshape(8, P).T
        a[f"b3f_{n}_b2"] = f("b2")
        a[f"b3f_{n}_node_w"] = np.concatenate([f("node_w").T, np.zeros((P, 1), np.float32)], axis=1)
        a[f"b3f_{n}_node_b"] = np.concatenate([f("node_b"), np.zeros(1, np.float32)])[None]
    a["b3a_small"] = np.zeros((P, 12), np.float32)
    a["b2a_w"] = np.stack([v["L2_attn_Wk"].T, v["L2_attn_Wv"].T, v["L2_attn_Wr"].T,
                           v["L2_attn_Wo"].T], axis=1)
    a["b2a_small"] = np.concatenate(
        [v["L2_attn_time_decay"], v["L2_attn_time_first"], v["L2_attn_time_mix_k"][0].T,
         v["L2_attn_time_mix_v"][0].T, v["L2_attn_time_mix_r"][0].T], axis=1)
    return {k: np.ascontiguousarray(x) for k, x in a.items()}


def load_constants(nc, M, W):
    shapes = {"ident": [P, P], "mean": [P, P], "ones": [P, QW], "pick16": [16, 8, P], "pick4": [4, 4, P],
              "pick9": [9, 9, P], "causal": [P, P]}
    tiles = {n: M.sb(f"c_{n}", s) for n, s in shapes.items()}
    load(nc, "constants", [(tiles[n][:], W[f"c_{n}"]) for n in shapes])
    return Names(flag=M.sb("c_flag", [1, 1], mybir.dt.int32),
                 scratch=nc.dram_tensor("position_scratch", [4, 2, P, QW], F32, kind="Internal").ap(),
                 **tiles)



def build(nc, W, out):
    with ExitStack() as ctx:
        M = Memory(nc, ctx)
        K = load_constants(nc, M, W)
        x = M.sb("x", [P, N])
        xn = M.sb("xn", [P, N])
        load(nc, "x", [(x[:], W["x"])])
        layer_norm(nc, K, "n0", x, xn)
        block0_attn(nc, K, W, xn, x)
        block0_ffn(nc, K, W, xn, x)
        layer_norm(nc, K, "n1", x, xn)
        head_attention(nc, K, W, "b1a", xn, x, relative=True)
        block1_ffn(nc, K, W, xn, x)
        layer_norm(nc, K, "n2", x, xn)
        block2_attn(nc, K, W, xn, x)
        block2_ffn(nc, K, W, xn, x)
        layer_norm(nc, K, "n3", x, xn)
        head_attention(nc, K, W, "b3a", xn, x, relative=False)
        block3_ffn(nc, K, W, xn, x)
        load(nc, "out", [(out, x[:])])


def kernel(**inputs):
    import concourse.bacc as bacc
    from concourse.bass_utils import run_bass_kernel_spmd

    nc = bacc.Bacc("TRN2", target_bir_lowering=False, num_devices=1)
    arrays = {**constants(), **layouts({k: np.asarray(a) for k, a in inputs.items()})}
    W = {name: nc.dram_tensor(f"in_{name}", a.shape, mybir.dt.from_np(a.dtype),
                              kind="ExternalInput").ap() for name, a in arrays.items()}
    out = nc.dram_tensor("out", (P, N), F32, kind="ExternalOutput").ap()
    build(nc, W, out)
    run = run_bass_kernel_spmd(nc, [{f"in_{n}": a for n, a in arrays.items()}], core_ids=[0])
    return np.ascontiguousarray(run.results[0]["out"].T).reshape(B, T, P)
```

```python
from collections import namedtuple
from contextlib import ExitStack, contextmanager

import numpy as np
import concourse.bass as bass
from concourse import mybir

P = 128
B, T = 2, 1024
N = B * T
TILES = N // P
QW = 512
QUARTERS = N // QW
FIRST_SEM = 120

F32 = mybir.dt.float32
BF16 = mybir.dt.bfloat16
ALU = mybir.AluOpType
ACT = mybir.ActivationFunctionType
AX_X = mybir.AxisListType.X
BF16_NP = mybir.dt.np(BF16)



@contextmanager
def stage(nc, *names):
    sems = [nc.alloc_semaphore(n, num=FIRST_SEM + i) for i, n in enumerate(names)]
    with nc.Block() as block:
        yield block, Names(**dict(zip(names, sems)))
    nc.all_engine_barrier(sems_to_clear=range(FIRST_SEM, FIRST_SEM + len(sems)))
    for s in sems:
        nc.release_semaphore(s)


def Names(**things):
    return namedtuple("Names", things)(**things)


class Chain:

    def __init__(self, eng, sem):
        self.eng, self.sem, self.n = eng, sem, 0

    def __call__(self, ins):
        self.n += 1
        ins.then_inc(self.sem, 1)
        self.eng.wait_ge(self.sem, self.n)


class Memory:

    def __init__(self, nc, ctx):
        self.nc, self.ctx = nc, ctx

    def sb(self, name, shape, dt=F32):
        return self.ctx.enter_context(self.nc.sbuf_tensor(name, shape, dt))

    def ps(self, name, shape, dt=F32):
        return self.ctx.enter_context(self.nc.psum_tensor(name, shape, dt))


def cols(i, width):
    return slice(i * width, (i + 1) * width)



def layer_norm(nc, K, name, src, dst, eps=1e-5, gain=None, offset=None, add_to=None):
    with ExitStack() as ctx:
        M = Memory(nc, ctx)
        per = QW // P
        centred = M.sb(f"{name}_centred", [P, QUARTERS, QW])
        squares = M.sb(f"{name}_squares", [P, 2, QW])
        inverse = M.sb(f"{name}_inverse", [P, TILES])
        mean_ps = M.ps(f"{name}_mean_ps", [P, 2, QW])
        var_ps = M.ps(f"{name}_var_ps", [P, TILES])
        spread_ps = M.ps(f"{name}_spread_ps", [P, 2, QW])
        with stage(nc, "mean_ready", "centred_ready", "squared", "var_ready", "shifted", "rooted",
                   "inverted", "spread_ready", "normed", "dve_chain") as (block, S):

            @block.tensor
            def _(pe):
                for q in range(QUARTERS + 1):
                    if q < QUARTERS:
                        if q >= 2:
                            pe.wait_ge(S.centred_ready, q - 1)
                        pe.matmul(mean_ps[:, q % 2], K.mean[:], src[:, cols(q, QW)], start=True,
                                  stop=True).then_inc(S.mean_ready, 1)
                    if q >= 1:
                        pe.wait_ge(S.squared, q)
                        for j in range(per):
                            t = (q - 1) * per + j
                            ins = pe.matmul(var_ps[:, t:t + 1], squares[:, (q - 1) % 2, cols(j, P)],
                                            K.mean[:, 0:1], start=True, stop=True)
                        ins.then_inc(S.var_ready, 1)
                pe.wait_ge(S.inverted, 1)
                for q in range(QUARTERS):
                    if q >= 2:
                        pe.wait_ge(S.normed, q - 1)
                    for j in range(per):
                        t = q * per + j
                        ins = pe.matmul(spread_ps[:, q % 2, cols(j, P)],
                                        inverse[:, t:t + 1].to_broadcast([P, P]), K.ident[:],
                                        start=True, stop=True)
                    ins.then_inc(S.spread_ready, 1)

            @block.scalar
            def _(act):
                for q in range(QUARTERS):
                    act.wait_ge(S.centred_ready, q + 1)
                    if q >= 2:
                        act.wait_ge(S.var_ready, q - 1)
                    act.activation(squares[:, q % 2], centred[:, q], ACT.Square).then_inc(S.squared, 1)
                act.wait_ge(S.shifted, 1)
                act.activation(inverse[:], inverse[:], ACT.Sqrt).then_inc(S.rooted, 1)

            @block.vector
            def _(dve):
                chain = Chain(dve, S.dve_chain)
                for q in range(QUARTERS):
                    dve.wait_ge(S.mean_ready, q + 1)
                    dve.tensor_tensor(centred[:, q], src[:, cols(q, QW)], mean_ps[:, q % 2],
                                      ALU.subtract).then_inc(S.centred_ready, 1)
                dve.wait_ge(S.var_ready, QUARTERS)
                dve.tensor_scalar(inverse[:], var_ps[:], eps, None, ALU.add).then_inc(S.shifted, 1)
                dve.wait_ge(S.rooted, 1)
                dve.reciprocal(inverse[:], inverse[:]).then_inc(S.inverted, 1)
                dve.wait_ge(S.centred_ready, QUARTERS)
                for q in range(QUARTERS):
                    dve.wait_ge(S.spread_ready, q + 1)
                    out = dst[:, cols(q, QW)]
                    if gain is None:
                        dve.tensor_tensor(out, centred[:, q], spread_ps[:, q % 2], ALU.mult) \
                            .then_inc(S.normed, 1)
                        continue
                    chain(dve.scalar_tensor_tensor(out=centred[:, q], in0=centred[:, q], scalar=gain,
                                                   in1=spread_ps[:, q % 2], op0=ALU.mult,
                                                   op1=ALU.mult))
                    if add_to is None:
                        dve.tensor_scalar(out, centred[:, q], offset, None, ALU.add) \
                            .then_inc(S.normed, 1)
                    else:
                        dve.scalar_tensor_tensor(out=out, in0=centred[:, q], scalar=offset,
                                                 in1=add_to[:, cols(q, QW)], op0=ALU.add,
                                                 op1=ALU.add).then_inc(S.normed, 1)



def router_probs(nc, K, name, flat, weight, bias_row, experts, probs):
    with ExitStack() as ctx:
        M = Memory(nc, ctx)
        wide = TILES * experts
        logits = M.ps(f"{name}_logits", [P, QW])
        top = M.sb(f"{name}_top", [P, TILES])
        total = M.sb(f"{name}_total", [P, TILES])
        lg = logits[:, 0:wide].rearrange("p (t e) -> p t e", e=experts)
        with stage(nc, "logits_ready", "shifted", "exps_ready", "dve_chain") as (block, S):

            @block.tensor
            def _(pe):
                for t in range(TILES):
                    last = pe.matmul(lg[:, t], flat[:, cols(t, P)], weight, start=True,
                                     stop=bias_row is None)
                    if bias_row is not None:
                        last = pe.matmul(lg[:, t], K.ones[0:1, 0:P], bias_row, start=False, stop=True)
                last.then_inc(S.logits_ready, 1)

            @block.vector
            def _(dve):
                chain = Chain(dve, S.dve_chain)
                dve.wait_ge(S.logits_ready, 1)
                chain(dve.tensor_reduce(top[:], lg, AX_X, ALU.max))
                spread = top[:].unsqueeze(2).to_broadcast([P, TILES, experts])
                dve.tensor_tensor(probs[:], lg, spread, ALU.subtract).then_inc(S.shifted, 1)
                dve.wait_ge(S.exps_ready, 1)
                chain(dve.tensor_reduce(total[:], probs[:], AX_X, ALU.add))
                chain(dve.reciprocal(total[:], total[:]))
                spread = total[:].unsqueeze(2).to_broadcast([P, TILES, experts])
                chain(dve.tensor_tensor(probs[:], probs[:], spread, ALU.mult))

            @block.scalar
            def _(act):
                act.wait_ge(S.shifted, 1)
                act.activation(probs[:], probs[:], ACT.Exp).then_inc(S.exps_ready, 1)


def keep_top(nc, name, probs, experts, k):
    with ExitStack() as ctx:
        M = Memory(nc, ctx)
        rank = M.sb(f"{name}_rank", [P, TILES, experts])
        ahead = M.sb(f"{name}_ahead", [P, 2, TILES, experts])
        with stage(nc, "compared", "counted") as (block, S):

            @block.vector
            def _(dve):
                n = 0
                dve.memset(rank[:], 0.0).then_inc(S.counted, 1)
                for e in range(experts):
                    it = probs[:, :, e:e + 1]
                    if e >= 2:
                        dve.wait_ge(S.counted, e)
                    if e > 0:
                        n += 1
                        dve.tensor_tensor(ahead[:, e % 2, :, 0:e], it.to_broadcast([P, TILES, e]),
                                          probs[:, :, 0:e], ALU.is_gt).then_inc(S.compared, 1)
                    n += 1
                    dve.tensor_tensor(ahead[:, e % 2, :, e:], it.to_broadcast([P, TILES, experts - e]),
                                      probs[:, :, e:], ALU.is_ge).then_inc(S.compared, 1)
                    dve.wait_ge(S.compared, n)
                    dve.wait_ge(S.counted, e + 1)
                    dve.tensor_tensor(rank[:], rank[:], ahead[:, e % 2], ALU.add).then_inc(S.counted, 1)
                dve.wait_ge(S.counted, experts + 1)
                dve.scalar_tensor_tensor(out=probs[:], in0=rank[:], scalar=k + 0.5, in1=probs[:],
                                         op0=ALU.is_lt, op1=ALU.mult).then_inc(S.counted, 1)
                dve.wait_ge(S.counted, experts + 2)


def to_rows(nc, K, name, table, rows, dst, short=None):
    with ExitStack() as ctx:
        M = Memory(nc, ctx)
        turned = M.ps(f"{name}_turned", [P, QUARTERS, QW])
        per = QW // P
        with stage(nc, "turned_ready", "copied") as (block, S):

            @block.tensor
            def _(pe):
                for t in range(TILES):
                    ins = pe.transpose(turned[0:rows, t // per, cols(t % per, P)], table[:, t],
                                       K.ident[:])
                    if t % per == per - 1:
                        ins.then_inc(S.turned_ready, 1)

            @block.vector
            def _(dve):
                for q in range(QUARTERS):
                    dve.wait_ge(S.turned_ready, q + 1)
                    dve.tensor_copy(dst[0:rows, cols(q, QW)], turned[0:rows, q]).then_inc(S.copied, 1)
                    if short is not None:
                        dve.tensor_copy(short[0:rows, cols(q, QW)], turned[0:rows, q]) \
                            .then_inc(S.copied, 1)
                dve.wait_ge(S.copied, QUARTERS * (1 if short is None else 2))



def mlp(nc, K, name, src, dst, chunks, func, gates=None, gate_rows=0, out_bias=None, add=True,
        select_from=None):
    if select_from is None:
        select_from = gates
    n_chunks = len(chunks)
    quarters = 2
    ring = 4
    units = [(i, c) for i in range(quarters) for c in range(n_chunks)]
    gated = [chunks[c][3] is not None for i, c in units]
    gated_until = [sum(gated[:u]) for u in range(len(units) + 1)]
    starts = [gated[u] and (c == 0 or not gated[u - 1] or chunks[c - 1][4] != chunks[c][4])
              for u, (i, c) in enumerate(units)]
    group = [sum(starts[:u + 1]) - 1 for u in range(len(units))]
    last_gated = {g: max(u for u in range(len(units)) if gated[u] and group[u] == g)
                  for g in set(group) if g >= 0}
    with ExitStack() as ctx:
        M = Memory(nc, ctx)
        hidden = M.sb(f"{name}_hidden", [P, ring, QW])
        scaled = M.sb(f"{name}_scaled", [P, ring, QW])
        h_ps = M.ps(f"{name}_h_ps", [P, 3, QW])
        g_ps = M.ps(f"{name}_g_ps", [P, 2, QW])
        y_ps = M.ps(f"{name}_y_ps", [P, quarters, QW])
        with nc.Fori(0, QUARTERS // quarters) as turn, stage(
                nc, "h_ready", "g_ready", "h_done", "h_scaled", "y_added",
                "y_ready", "y_stored") as (block, S):

            def tokens(i):
                return bass.ds((turn * quarters + i) * QW, QW)

            @block.tensor
            def _(pe):
                def hidden_product(u):
                    i, c = units[u]
                    w1, _, _, select, _ = chunks[c]
                    if starts[u]:
                        g = group[u]
                        if g >= 2:
                            pe.wait_ge(S.h_scaled, gated_until[last_gated[g - 2] + 1])
                        pe.matmul(g_ps[:, g % 2], select, select_from[0:gate_rows, tokens(i)],
                                  start=True, stop=True).then_inc(S.g_ready, 1)
                    if u >= 3:
                        pe.wait_ge(S.h_done, u - 2)
                    pe.matmul(h_ps[:, u % 3], w1, src[:, tokens(i)], start=True, stop=True) \
                        .then_inc(S.h_ready, 1)

                def output_product(u):
                    i, c = units[u]
                    if gated[u]:
                        pe.wait_ge(S.h_scaled, gated_until[u + 1])
                    else:
                        pe.wait_ge(S.h_done, u + 1)
                    h = (scaled if gated[u] else hidden)[:, u % ring]
                    last = c == n_chunks - 1
                    pe.matmul(y_ps[:, i], chunks[c][2], h, start=(c == 0),
                              stop=(last and out_bias is None)).then_inc(S.y_added, 1)
                    if last and out_bias is not None:
                        pe.matmul(y_ps[:, i], out_bias, gates[0:gate_rows, tokens(i)], start=False,
                                  stop=True).then_inc(S.y_ready, 1)

                for u in range(len(units) + 2):
                    if u < len(units):
                        hidden_product(u)
                    if u >= 2:
                        output_product(u - 2)

            @block.scalar
            def _(act):
                for u, (i, c) in enumerate(units):
                    act.wait_ge(S.h_ready, u + 1)
                    if u >= ring:
                        act.wait_ge(S.y_added, u - ring + 1)
                    b1 = chunks[c][1]
                    kw = {} if b1 is None else {"bias": b1}
                    act.activation(hidden[:, u % ring], h_ps[:, u % 3], func, **kw).then_inc(S.h_done, 1)

            @block.vector
            def _(dve):
                def store(u):
                    i, c = units[u]
                    if c == n_chunks - 1:
                        if out_bias is not None:
                            dve.wait_ge(S.y_ready, i + 1)
                        else:
                            dve.wait_ge(S.y_added, u + 1)
                        out = dst[:, tokens(i)]
                        if add:
                            dve.tensor_tensor(out, out, y_ps[:, i], ALU.add).then_inc(S.y_stored, 1)
                        else:
                            dve.tensor_copy(out, y_ps[:, i]).then_inc(S.y_stored, 1)

                for u, (i, c) in enumerate(units):
                    if gated[u]:
                        dve.wait_ge(S.h_done, u + 1)
                        if starts[u]:
                            dve.wait_ge(S.g_ready, group[u] + 1)
                        if u >= ring:
                            dve.wait_ge(S.y_added, u - ring + 1)
                        dve.tensor_tensor(scaled[:, u % ring], hidden[:, u % ring],
                                          g_ps[:, group[u] % 2], ALU.mult).then_inc(S.h_scaled, 1)
                    if u >= 2:
                        store(u - 2)
                store(len(units) - 2)
                store(len(units) - 1)
                dve.wait_ge(S.y_stored, quarters)



def load(nc, name, pairs):
    with stage(nc, "loaded") as (block, S):
        half = (len(pairs) + 1) // 2

        @block.sync
        def _(sp):
            for dst, src in pairs[:half]:
                sp.dma_start(dst, src).then_inc(S.loaded, 16)
            sp.wait_ge(S.loaded, 16 * len(pairs))

        @block.scalar
        def _(act):
            for dst, src in pairs[half:]:
                act.dma_start(dst, src).then_inc(S.loaded, 16)


SHARED0, ROUTED0, WIDE0, TOP0 = 2, 16, 64, 4


def block0_ffn(nc, K, W, xn, x):
    with ExitStack() as ctx:
        M = Memory(nc, ctx)
        pairs = ROUTED0 // 2
        up = M.sb("b0f_up", [P, pairs + 1, P])
        down = M.sb("b0f_down", [P, pairs + 1, P])
        rw = M.sb("b0f_router", [P, ROUTED0])
        gates = M.sb("b0f_gates", [ROUTED0, N])
        load(nc, "b0f", [(up[:], W["b0f_up"]), (down[:], W["b0f_down"]), (rw[:], W["b0f_router"])])
        with ExitStack() as inner:
            probs = Memory(nc, inner).sb("b0f_probs", [P, TILES, ROUTED0])
            router_probs(nc, K, "b0f", xn, rw[:], None, ROUTED0, probs)
            keep_top(nc, "b0f", probs, ROUTED0, TOP0)
            to_rows(nc, K, "b0f", probs, ROUTED0, gates)
        chunks = [(up[:, c], None, down[:, c], K.pick16[:, c], c) for c in range(pairs)]
        chunks.append((up[:, pairs], None, down[:, pairs], None, -1))
        mlp(nc, K, "b0f", xn, x, chunks, ACT.Gelu, gates, ROUTED0)



STATES = 16
H_LIMIT = 100.0


def ssm_states(nc, K, w, name, xn, delta, flat, peak, stepwise):
    units = [(s, q) for s in range(STATES) for q in range(QUARTERS)]
    per_seq = T // QW
    with ExitStack() as ctx:
        M = Memory(nc, ctx)
        decay = M.sb(f"{name}_decay", [P, 3, QW])
        raw = M.sb(f"{name}_raw", [P, 2, QW])
        drive = M.sb(f"{name}_drive", [P, 2, QW])
        h = M.sb(f"{name}_h", [P, 3, QW])
        hc = M.sb(f"{name}_hc", [P, 3, QW])
        peaks = M.sb(f"{name}_peaks", [P, len(units)])
        b_ps = M.ps(f"{name}_b_ps", [P, 2, QW])
        c_ps = M.ps(f"{name}_c_ps", [P, 2, QW])
        y_ps = M.ps(f"{name}_y_ps", [P, QUARTERS, QW])
        with stage(nc, "b_ready", "c_ready", "decay_ready", "clipped", "drive_ready", "state_ready",
                   "peak_read", "hc_ready", "y_added", "dve_chain") as (block, S):

            @block.tensor
            def _(pe):
                for u in range(len(units) + 2):
                    if u < len(units):
                        s, q = units[u]
                        if u >= 2:
                            pe.wait_ge(S.clipped, u - 1)
                            pe.wait_ge(S.hc_ready, u - 1)
                        pe.matmul(b_ps[:, u % 2], w.wb[:, s:s + 1].to_broadcast([P, P]),
                                  xn[:, cols(q, QW)], start=True, stop=True).then_inc(S.b_ready, 1)
                        pe.matmul(c_ps[:, u % 2], w.wc[:, s:s + 1].to_broadcast([P, P]),
                                  xn[:, cols(q, QW)], start=True, stop=True).then_inc(S.c_ready, 1)
                    if u >= 2:
                        s, q = units[u - 2]
                        pe.wait_ge(S.hc_ready, u - 1)
                        pe.matmul(y_ps[:, q], K.ident[:], hc[:, (u - 2) % 3], start=(s == 0),
                                  stop=(s == STATES - 1)).then_inc(S.y_added, 1)

            @block.scalar
            def _(act):
                for u, (s, q) in enumerate(units):
                    if u >= 3:
                        act.wait_ge(S.state_ready, u - 2)
                    act.activation(decay[:, u % 3], delta[:, cols(q, QW)], ACT.Exp,
                                   scale=w.a[:, s:s + 1]).then_inc(S.decay_ready, 1)

            @block.gpsimd
            def _(pool):
                for u, (s, q) in enumerate(units):
                    pool.wait_ge(S.clipped, u + 1)
                    if u >= 2:
                        pool.wait_ge(S.state_ready, u - 1)
                    pool.tensor_tensor(drive[:, u % 2], raw[:, u % 2], xn[:, cols(q, QW)], ALU.mult) \
                        .then_inc(S.drive_ready, 1)

            @block.vector
            def _(dve):
                chain = Chain(dve, S.dve_chain)

                def drive_factor(u):
                    s, q = units[u]
                    dve.wait_ge(S.b_ready, u + 1)
                    if u >= 2:
                        dve.wait_ge(S.drive_ready, u - 1)
                    chain(dve.scalar_tensor_tensor(out=raw[:, u % 2], in0=b_ps[:, u % 2],
                                                   scalar=w.bb[:, s:s + 1], in1=delta[:, cols(q, QW)],
                                                   op0=ALU.add, op1=ALU.mult))
                    dve.tensor_scalar(raw[:, u % 2], raw[:, u % 2], 2.0, -2.0, ALU.min, ALU.max) \
                        .then_inc(S.clipped, 1)

                def scan(u):
                    s, q = units[u]
                    initial = 0.0 if q % per_seq == 0 else h[:, (u - 1) % 3, QW - 1:QW]
                    dve.wait_ge(S.drive_ready, u + 1)
                    dve.wait_ge(S.decay_ready, u + 1)
                    if u >= 3:
                        dve.wait_ge(S.peak_read, u - 2)
                    dve.tensor_tensor_scan(h[:, u % 3], decay[:, u % 3], drive[:, u % 2], initial,
                                           ALU.mult, ALU.add).then_inc(S.state_ready, 1)

                def walk(u):
                    s, q = units[u]
                    now, dec, drv = h[:, u % 3], decay[:, u % 3], drive[:, u % 2]
                    dve.wait_ge(S.drive_ready, u + 1)
                    dve.wait_ge(S.decay_ready, u + 1)
                    if q % per_seq == 0:
                        chain(dve.tensor_copy(now[:, 0:1], drv[:, 0:1]))
                    else:
                        chain(dve.scalar_tensor_tensor(out=now[:, 0:1], in0=h[:, (u - 1) % 3, QW - 1:QW],
                                                       scalar=dec[:, 0:1], in1=drv[:, 0:1],
                                                       op0=ALU.mult, op1=ALU.add))
                    chain(dve.tensor_scalar(now[:, 0:1], now[:, 0:1], H_LIMIT, -H_LIMIT,
                                            ALU.min, ALU.max))
                    with dve.Fori(1, QW) as t:
                        dve.drain()
                        dve.tensor_tensor(now[:, bass.ds(t, 1)], now[:, bass.ds(t - 1, 1)],
                                          dec[:, bass.ds(t, 1)], ALU.mult)
                        dve.drain()
                        dve.tensor_tensor(now[:, bass.ds(t, 1)], now[:, bass.ds(t, 1)],
                                          drv[:, bass.ds(t, 1)], ALU.add)
                        dve.drain()
                        dve.tensor_scalar(now[:, bass.ds(t, 1)], now[:, bass.ds(t, 1)], H_LIMIT,
                                          -H_LIMIT, ALU.min, ALU.max)
                    dve.drain()
                    dve.tensor_copy(now[:, 0:1], now[:, 0:1]).then_inc(S.state_ready, 1)

                def output(u):
                    s, q = units[u]
                    dve.wait_ge(S.state_ready, u + 1)
                    dve.tensor_reduce(peaks[:, u:u + 1], h[:, u % 3], AX_X, ALU.max,
                                      apply_absolute_value=True).then_inc(S.peak_read, 1)
                    dve.wait_ge(S.c_ready, u + 1)
                    if u >= 3:
                        dve.wait_ge(S.y_added, u - 2)
                    dve.scalar_tensor_tensor(out=hc[:, u % 3], in0=c_ps[:, u % 2],
                                             scalar=w.bc[:, s:s + 1], in1=h[:, u % 3],
                                             op0=ALU.add, op1=ALU.mult).then_inc(S.hc_ready, 1)

                for u in range(len(units) + 1):
                    if u < len(units):
                        drive_factor(u)
                    if u >= 1:
                        (walk if stepwise else scan)(u - 1)
                        output(u - 1)
                for q in range(QUARTERS):
                    dve.wait_ge(S.y_added, len(units) - QUARTERS + q + 1)
                    chain(dve.scalar_tensor_tensor(out=flat[:, cols(q, QW)], in0=xn[:, cols(q, QW)],
                                                   scalar=w.d[:], in1=y_ps[:, q], op0=ALU.mult,
                                                   op1=ALU.add))
                dve.wait_ge(S.peak_read, len(units))
                chain(dve.tensor_reduce(peak, peaks[:], AX_X, ALU.max))


def block0_attn(nc, K, W, xn, x):
    with ExitStack() as ctx:
        M = Memory(nc, ctx)
        wd = M.sb("b0a_wd", [P, P])
        small = M.sb("b0a_small", [P, 5 * STATES + 8])
        w = Names(wb=small[:, 0:16], wc=small[:, 16:32], bb=small[:, 32:48],
                            bc=small[:, 48:64], a=small[:, 64:80], d=small[:, 80:81],
                            bd=small[:, 81:82], ln_w=small[:, 82:83], ln_b=small[:, 83:84])
        flat = M.sb("b0a_flat", [P, N])
        peak = M.sb("b0a_peak", [P, 1])
        load(nc, "b0a", [(wd[:], W["b0a_wd"]), (small[:], W["b0a_small"])])
        with ExitStack() as inner:
            delta = Memory(nc, inner).sb("b0a_delta", [P, N])
            softplus_delta(nc, K, w, wd, xn, delta)
            ssm_states(nc, K, w, "b0s", xn, delta, flat, peak[:], stepwise=False)
            over = clipped_somewhere(nc, K, peak)
            with nc.If(over > 0):
                ssm_states(nc, K, w, "b0w", xn, delta, flat, peak[:], stepwise=True)
            with nc.Else():
                nc.all_engine_barrier()
        with ExitStack() as inner:
            I = Memory(nc, inner)
            up = I.sb("b0m_up", [P, 4, 4, P])
            down = I.sb("b0m_down", [P, 4, 4, P])
            b1 = I.sb("b0m_b1", [P, 16])
            b2 = I.sb("b0m_b2", [4, P])
            rw = I.sb("b0m_router", [P, 4])
            rb = I.sb("b0m_router_b", [1, 4])
            gates = I.sb("b0m_gates", [4, N])
            moe = I.sb("b0m_out", [P, N])
            load(nc, "b0m", [(up[:], W["b0m_up"]), (down[:], W["b0m_down"]), (b1[:], W["b0m_b1"]),
                             (b2[:], W["b0m_b2"]), (rw[:], W["b0m_router"]), (rb[:], W["b0m_router_b"])])
            with ExitStack() as rt:
                probs = Memory(nc, rt).sb("b0m_probs", [P, TILES, 4])
                router_probs(nc, K, "b0m", flat, rw[:], rb[:], 4, probs)
                keep_top(nc, "b0m", probs, 4, 1)
                to_rows(nc, K, "b0m", probs, 4, gates)
            chunks = [(up[:, e, c], b1[:, 4 * e + c:4 * e + c + 1], down[:, e, c],
                       K.pick4[:, e], e) for e in range(4) for c in range(4)]
            mlp(nc, K, "b0m", flat, moe, chunks, ACT.Silu, gates, 4, b2[:], add=False)
            add_tokens(nc, flat[:], moe[:])
        layer_norm(nc, K, "b0n", flat, x, gain=w.ln_w, offset=w.ln_b, add_to=x)


def add_tokens(nc, dst, src):
    with stage(nc, "added") as (block, S):

        @block.vector
        def _(dve):
            dve.tensor_tensor(dst, dst, src, ALU.add).then_inc(S.added, 1)
            dve.wait_ge(S.added, 1)


def softplus_delta(nc, K, w, wd, xn, delta):
    with ExitStack() as ctx:
        M = Memory(nc, ctx)
        u_ps = M.ps("sp_u", [P, QUARTERS, QW])
        tail = M.sb("sp_tail", [P, QUARTERS, QW])
        with stage(nc, "u_ready", "tail_ready", "stored", "act_chain") as (block, S):

            @block.tensor
            def _(pe):
                for q in range(QUARTERS):
                    pe.matmul(u_ps[:, q], wd[:], xn[:, cols(q, QW)], start=True, stop=True) \
                        .then_inc(S.u_ready, 1)

            @block.scalar
            def _(act):
                chain = Chain(act, S.act_chain)
                act.wait_ge(S.u_ready, QUARTERS)
                chain(act.activation(tail[:], u_ps[:], ACT.Abs, bias=w.bd))
                chain(act.activation(tail[:], tail[:], ACT.Exp, scale=-1.0))
                act.activation(tail[:], tail[:], ACT.Ln, bias=1.0).then_inc(S.tail_ready, 1)
                chain(act.activation(w.a, w.a, ACT.Exp))
                chain(act.mul(w.a, w.a, -1.0))

            @block.vector
            def _(dve):
                dve.wait_ge(S.u_ready, QUARTERS)
                dve.wait_ge(S.act_chain, 1)
                dve.tensor_scalar(delta[:], u_ps[:].rearrange("p q n -> p (q n)"), w.bd, 0.0,
                                  ALU.add, ALU.max).then_inc(S.stored, 1)
                dve.wait_ge(S.tail_ready, 1)
                dve.wait_ge(S.stored, 1)
                dve.tensor_tensor(delta[:], delta[:], tail[:].rearrange("p q n -> p (q n)"),
                                  ALU.add).then_inc(S.stored, 1)
                dve.wait_ge(S.stored, 2)


def clipped_somewhere(nc, K, peak):
    flag = K.flag
    with ExitStack() as ctx:
        M = Memory(nc, ctx)
        row = M.ps("peak_row", [P, QW])
        within = M.sb("peak_within", [1, 2])
        with stage(nc, "row_ready", "dve_chain") as (block, S):

            @block.tensor
            def _(pe):
                pe.transpose(row[0:1, 0:P], peak[:], K.ident[:]).then_inc(S.row_ready, 1)

            @block.vector
            def _(dve):
                chain = Chain(dve, S.dve_chain)
                dve.wait_ge(S.row_ready, 1)
                chain(dve.tensor_reduce(within[:, 0:1], row[0:1, 0:P], AX_X, ALU.max))
                chain(dve.tensor_scalar(within[:, 1:2], within[:, 0:1], H_LIMIT, None, ALU.is_le))
                chain(dve.tensor_scalar(flag[:], within[:, 1:2], -1.0, 1.0, ALU.mult, ALU.add))
    return nc.values_load(flag[:], min_val=0, max_val=1)



EXPERTS1, CAPACITY1, HIDDEN1 = 8, N // 8, 512


def choose_tokens(nc, gates):
    with ExitStack() as ctx:
        M = Memory(nc, ctx)
        left = M.sb("b1f_left", [EXPERTS1, N])
        best = M.sb("b1f_best", [EXPERTS1, 8])
        with stage(nc, "dve_chain") as (block, S):

            @block.vector
            def _(dve):
                chain = Chain(dve, S.dve_chain)
                chain(dve.tensor_copy(left[:], gates[0:EXPERTS1]))
                for _ in range(CAPACITY1 // 8):
                    chain(dve.max(best[:], left[:]))
                    chain(dve.match_replace(left[:], best[:], left[:], -1.0))
                chain(dve.scalar_tensor_tensor(out=gates[0:EXPERTS1], in0=left[:], scalar=0.0,
                                               in1=gates[0:EXPERTS1], op0=ALU.is_lt, op1=ALU.mult))


def block1_ffn(nc, K, W, xn, x):
    with ExitStack() as ctx:
        M = Memory(nc, ctx)
        parts = HIDDEN1 // P
        up = M.sb("b1f_up", [P, EXPERTS1 + 1, parts, P])
        down = M.sb("b1f_down", [P, EXPERTS1 + 1, parts, P])
        b1 = M.sb("b1f_b1", [P, (EXPERTS1 + 1) * parts])
        b2 = M.sb("b1f_b2", [EXPERTS1 + 1, P])
        gate_w = M.sb("b1f_gate_w", [P, EXPERTS1])
        gates = M.sb("b1f_gates", [EXPERTS1 + 1, N])
        load(nc, "b1f", [(up[:], W["b1f_up"]), (down[:], W["b1f_down"]), (b1[:], W["b1f_b1"]),
                         (b2[:], W["b1f_b2"]), (gate_w[:], W["b1f_gate_w"]),
                         (gates[EXPERTS1:EXPERTS1 + 1], W["c_one_row"])])
        with ExitStack() as rt:
            probs = Memory(nc, rt).sb("b1f_probs", [P, TILES, EXPERTS1])
            router_probs(nc, K, "b1f", xn, gate_w[:], None, EXPERTS1, probs)
            to_rows(nc, K, "b1f", probs, EXPERTS1, gates)
        choose_tokens(nc, gates)
        chunks = [(up[:, e, c], b1[:, parts * e + c:parts * e + c + 1], down[:, e, c],
                   K.pick9[:, e] if e < EXPERTS1 else None, e)
                  for e in range(EXPERTS1 + 1) for c in range(parts)]
        mlp(nc, K, "b1f", xn, x, chunks, ACT.Gelu_apprx_tanh, gates, EXPERTS1 + 1, b2[:])



K_CLAMP, K_EPS = 60.0, 1e-8


def block2_attn(nc, K, W, xn, x):
    with ExitStack() as ctx:
        M = Memory(nc, ctx)
        w = M.sb("b2a_w", [P, 4, P])
        small = M.sb("b2a_small", [P, 5])
        inv_mix = M.sb("b2a_inv_mix", [P, 3])
        lam = M.sb("b2a_lam", [P, QW])
        mixed = M.sb("b2a_mixed", [P, 3, QW])
        part = M.sb("b2a_part", [P, 3, QW])
        kc = M.sb("b2a_kc", [P, QW])
        kv = M.sb("b2a_kv", [P, QW])
        sr = M.sb("b2a_sr", [P, QW])
        sums = M.sb("b2a_sums", [P, 2, 1 + QW])
        den = M.sb("b2a_den", [P, QW])
        out = M.sb("b2a_out", [P, QW])
        prev = M.sb("b2a_prev", [P, 1 + N])
        kvr_ps = M.ps("b2a_kvr_ps", [P, 3, QW])
        o_ps = M.ps("b2a_o_ps", [P, QW])
        load(nc, "b2a", [(w[:], W["b2a_w"]), (small[:], W["b2a_small"])])
        with stage(nc, "decayed", "mixed_ready", "projected", "act_done", "kc_clamped", "out_ready",
                   "o_ready", "stored", "dve_chain", "act_chain") as (block, S):

            @block.scalar
            def _(act):
                chain = Chain(act, S.act_chain)
                chain(act.activation(small[:, 0:1], small[:, 0:1], ACT.Exp))
                chain(act.activation(small[:, 0:1], small[:, 0:1], ACT.Exp, scale=-1.0))
                act.activation(small[:, 1:2], small[:, 1:2], ACT.Exp).then_inc(S.decayed, 1)
                for q in range(QUARTERS):
                    act.wait_ge(S.kc_clamped, q + 1)
                    act.activation(kc[:], kc[:], ACT.Exp).then_inc(S.act_done, 1)
                    act.activation(sr[:], kvr_ps[:, 2], ACT.Sigmoid).then_inc(S.act_done, 1)

            @block.tensor
            def _(pe):
                for q in range(QUARTERS):
                    pe.wait_ge(S.mixed_ready, q + 1)
                    if q >= 1:
                        pe.wait_ge(S.out_ready, q)
                    for i in range(3):
                        ins = pe.matmul(kvr_ps[:, i], w[:, i], mixed[:, i], start=True, stop=True)
                    ins.then_inc(S.projected, 1)
                    pe.wait_ge(S.out_ready, q + 1)
                    pe.matmul(o_ps[:], w[:, 3], out[:], start=True, stop=True).then_inc(S.o_ready, 1)

            @block.vector
            def _(dve):
                chain = Chain(dve, S.dve_chain)
                chain(dve.tensor_scalar(inv_mix[:], small[:, 2:5], -1.0, 1.0, ALU.mult, ALU.add))
                chain(dve.tensor_copy(prev[:, 1:], xn[:]))
                for b in range(B):
                    chain(dve.memset(prev[:, b * T:b * T + 1], 0.0))
                chain(dve.memset(lam[:], 0.0))
                dve.wait_ge(S.decayed, 1)
                chain(dve.tensor_scalar(lam[:], lam[:], small[:, 0:1], None, ALU.add))
                for q in range(QUARTERS):
                    x_q, prev_q = xn[:, cols(q, QW)], prev[:, cols(q, QW)]
                    for i in range(3):
                        chain(dve.tensor_scalar(part[:, i], x_q, small[:, 2 + i:3 + i], None, ALU.mult))
                    for i in range(3):
                        ins = dve.scalar_tensor_tensor(out=mixed[:, i], in0=prev_q,
                                                       scalar=inv_mix[:, i:i + 1], in1=part[:, i],
                                                       op0=ALU.mult, op1=ALU.add)
                        if i < 2:
                            chain(ins)
                    ins.then_inc(S.mixed_ready, 1)
                    dve.wait_ge(S.projected, q + 1)
                    dve.tensor_scalar(kc[:], kvr_ps[:, 0], K_CLAMP, None, ALU.min) \
                        .then_inc(S.kc_clamped, 1)
                    dve.wait_ge(S.act_done, 2 * q + 2)
                    chain(dve.tensor_tensor(kv[:], kc[:], kvr_ps[:, 1], ALU.mult))
                    for i, a in enumerate((kv, kc)):
                        if q % (T // QW) == 0:
                            chain(dve.memset(sums[:, i, 0:1], 0.0))
                        else:
                            chain(dve.tensor_copy(sums[:, i, 0:1], sums[:, i, QW:QW + 1]))
                        chain(dve.tensor_tensor_scan(sums[:, i, 1:], lam[:], a[:], sums[:, i, 0:1],
                                                     ALU.mult, ALU.add))
                    chain(dve.scalar_tensor_tensor(out=den[:], in0=kc[:], scalar=small[:, 1:2],
                                                   in1=sums[:, 1, 0:QW], op0=ALU.mult, op1=ALU.add))
                    chain(dve.tensor_scalar(den[:], den[:], K_EPS, None, ALU.add))
                    chain(dve.reciprocal(den[:], den[:]))
                    chain(dve.scalar_tensor_tensor(out=kv[:], in0=kv[:], scalar=small[:, 1:2],
                                                   in1=sums[:, 0, 0:QW], op0=ALU.mult, op1=ALU.add))
                    chain(dve.tensor_tensor(kv[:], kv[:], den[:], ALU.mult))
                    if q >= 1:
                        dve.wait_ge(S.o_ready, q)
                    dve.tensor_tensor(out[:], kv[:], sr[:], ALU.mult).then_inc(S.out_ready, 1)
                    dve.wait_ge(S.o_ready, q + 1)
                    x_out = x[:, cols(q, QW)]
                    dve.tensor_tensor(x_out, x_out, o_ps[:], ALU.add).then_inc(S.stored, 1)
                dve.wait_ge(S.stored, QUARTERS)



HEADS, HD = 16, 8
PAIRS = HEADS // 2
WINDOW1 = 128
BAND = 3 * P
QT = T // P
SLOTS_Q = (0, 0, 1, 0, 1, 2)
SLOTS_K = (0, 1, 0, 2, 1, 0)
ONES_AT = HD * len(SLOTS_Q)


OUT_ROWS = 32


def split_parts(chain, dve, src, parts, rest):
    chain(dve.tensor_copy(parts[0], src))
    chain(dve.tensor_tensor(rest, src, parts[0], ALU.subtract))
    chain(dve.tensor_copy(parts[1], rest))
    chain(dve.tensor_tensor(rest, rest, parts[1], ALU.subtract))
    chain(dve.tensor_copy(parts[2], rest))


def masked_parts(chain, dve, parts, masks, out):
    chain(dve.tensor_scalar(out, parts[0], masks[:, 0:1], None, ALU.mult))
    for i in (1, 2):
        chain(dve.scalar_tensor_tensor(out=out, in0=parts[i], scalar=masks[:, i:i + 1], in1=out,
                                       op0=ALU.mult, op1=ALU.add))


def head_attention(nc, K, W, key, xn, x, relative):
    kinds = 3 if relative else 1
    with ExitStack() as ctx:
        M = Memory(nc, ctx)
        n_w = 3 if relative else 6
        w = M.sb(f"{key}_w", [P, n_w, P])
        small = M.sb(f"{key}_small", [P, 12])
        stack_q = M.sb(f"{key}_pick_q", [P, PAIRS, 3, P], BF16)
        stack_k = M.sb(f"{key}_pick_k", [P, PAIRS, 3, P], BF16)
        x_b = M.sb(f"{key}_x_b", [P, T])
        parts = M.sb(f"{key}_parts", [P, 1 + kinds, 3, T], BF16)
        values = M.sb(f"{key}_values", [P, QT, HEADS, HD + 1])
        merged = M.sb(f"{key}_merged", [P, QT, PAIRS, 2 * HD])
        bias_cols = M.sb(f"{key}_bias_cols", [P, 1 + kinds])
        v_bias = M.sb(f"{key}_v_bias", [1, P])
        pick_f = M.sb(f"{key}_pick_f", [P, 2, 2, 3 * P], BF16)
        v_f = M.sb(f"{key}_v_f", [P, QT, 4, OUT_ROWS])
        qk = M.sb(f"{key}_qk", [P, 2, 1 + kinds, T], BF16)
        table = M.sb(f"{key}_table", [P, QW], BF16) if relative else None
        pairs = [(w[:], W[f"{key}_w"]), (small[:], W[f"{key}_small"]),
                 (stack_q[:], W["c_stack_q"]), (stack_k[:], W["c_stack_k"])]
        if relative:
            pairs.append((v_bias[:], W[f"{key}_v_bias"]))
        load(nc, key, pairs)
        if relative:
            position_table(nc, W, key, small, table, bias_cols)
        with stage(nc, "cleared") as (block, S):

            @block.vector
            def _(dve):
                dve.memset(v_f[:], 0.0).then_inc(S.cleared, 1)
                for i, stack in enumerate((stack_q, stack_k)):
                    dve.tensor_copy(pick_f[:, :, i].rearrange("p r (i n) -> p r i n", i=3),
                                    stack[:, 0:2]) \
                        .then_inc(S.cleared, 1)
                dve.wait_ge(S.cleared, 3)
        with nc.Fori(0, B) as b:
            project_heads(nc, K, W, key, xn, b, x_b, w, small, parts, values, v_bias, relative)
            with nc.Fori(0, PAIRS // 2) as turn:
                attend_pairs(nc, K, key, turn, parts, stack_q, stack_k, pick_f, values, v_f, qk,
                             bias_cols, table, merged, relative)
            merge_heads(nc, K, key, b, merged, x, w, relative)


def position_table(nc, W, key, small, table, bias_cols):
    with ExitStack() as ctx:
        M = Memory(nc, ctx)
        full = M.sb(f"{key}_full", [P, QW + 2])
        rest = M.sb(f"{key}_rest", [P, QW + 2])
        parts = M.sb(f"{key}_table_parts", [P, 3, QW + 2], BF16)
        chosen = M.sb(f"{key}_chosen", [P, QW + 2])
        with stage(nc, "loaded", "dve_chain") as (block, S):

            @block.sync
            def _(sp):
                sp.dma_start(full[:], W[f"{key}_positions"]).then_inc(S.loaded, 16)

            @block.vector
            def _(dve):
                chain = Chain(dve, S.dve_chain)
                dve.wait_ge(S.loaded, 16)
                split_parts(chain, dve, full[:], [parts[:, i] for i in range(3)], rest[:])
                masked_parts(chain, dve, [parts[:, i] for i in range(3)], small[:, 6:9], chosen[:])
                chain(dve.tensor_copy(table[:], chosen[:, 0:QW]))
                chain(dve.tensor_copy(bias_cols[:, 0:1], small[:, 9:10]))
                chain(dve.memset(bias_cols[:, 1:2], 0.0))
                chain(dve.tensor_copy(bias_cols[:, 2:4], chosen[:, QW:QW + 2]))


def project_heads(nc, K, W, key, xn, b, x_b, w, small, parts, values, v_bias, relative):
    with ExitStack() as ctx:
        M = Memory(nc, ctx)
        half = T // QW
        q_f = M.sb(f"{key}_q_f", [P, T])
        k_f = M.sb(f"{key}_k_f", [P, 3, T])
        rest = M.sb(f"{key}_split_rest", [P, T])
        turn = M.sb(f"{key}_turn", [P, 2, T]) if not relative else None
        qk_ps = M.ps(f"{key}_qk_ps", [P, 3, half, QW])
        v_ps = M.ps(f"{key}_v_ps", [P, 2, 4, P])
        with stage(nc, "x_loaded", "turn_loaded", "q_ready", "k_ready", "v_ready", "rotated_ready",
                   "values_ready", "ps_free", "dve_chain", "v_copied") as (block, S):

            @block.gpsimd
            def _(pool):
                pool.tensor_copy(x_b[:], xn[:, bass.ts(b, T)]).then_inc(S.x_loaded, 1)
                pool.memset(values[:, :, :, HD:HD + 1], 1.0).then_inc(S.v_copied, 1)
                pool.wait_ge(S.v_copied, 1)

            if not relative:
                @block.sync
                def _(sp):
                    sp.dma_start(turn[:], W["c_turn"]).then_inc(S.turn_loaded, 16)

            @block.tensor
            def _(pe):
                pe.wait_ge(S.x_loaded, 1)

                def product(i, slot):
                    for j in range(half):
                        ins = pe.matmul(qk_ps[:, slot, j], w[:, i], x_b[:, cols(j, QW)], start=True,
                                        stop=True)
                    return ins

                product(0, 0).then_inc(S.q_ready, 1)
                product(1, 1).then_inc(S.k_ready, 1)
                if not relative:
                    product(3, 2).then_inc(S.rotated_ready, 1)
                    pe.wait_ge(S.ps_free, 1)
                    product(4, 2).then_inc(S.rotated_ready, 1)
                for t in range(QT):
                    ins = pe.matmul(v_ps[:, t // 4, t % 4], x_b[:, cols(t, P)], w[:, 2], start=True,
                                    stop=not relative)
                    if relative:
                        ins = pe.matmul(v_ps[:, t // 4, t % 4], K.ones[0:1, 0:P], v_bias[:],
                                        start=False, stop=True)
                ins.then_inc(S.v_ready, 1)

            @block.vector
            def _(dve):
                chain = Chain(dve, S.dve_chain)
                flat = lambda slot: qk_ps[:, slot].rearrange("p j n -> p (j n)")
                dve.wait_ge(S.q_ready, 1)
                if relative:
                    chain(dve.tensor_scalar(q_f[:], flat(0), small[:, 0:1], None, ALU.add))
                    dve.wait_ge(S.k_ready, 1)
                    chain(dve.tensor_scalar(k_f[:, 0], flat(1), small[:, 1:2], float(HD) ** -0.5,
                                            ALU.add, ALU.mult))
                    chain(dve.tensor_scalar(k_f[:, 1], k_f[:, 0], small[:, 3:4], None, ALU.add))
                    chain(dve.tensor_scalar(k_f[:, 2], k_f[:, 0], small[:, 4:5], None, ALU.add))
                else:
                    dve.wait_ge(S.turn_loaded, 16)
                    for i, dst in enumerate((q_f[:], k_f[:, 0])):
                        if i == 1:
                            dve.wait_ge(S.k_ready, 1)
                        chain(dve.tensor_tensor(dst, flat(i), turn[:, 0], ALU.mult))
                        dve.wait_ge(S.rotated_ready, i + 1)
                        ins = dve.tensor_tensor(rest[:], flat(2), turn[:, 1], ALU.mult)
                        ins.then_inc(S.ps_free, 1)
                        dve.wait_ge(S.ps_free, i + 1)
                        chain(dve.tensor_tensor(dst, dst, rest[:], ALU.add))
                    chain(dve.tensor_scalar(k_f[:, 0], k_f[:, 0], float(HD) ** -0.5, None, ALU.mult))
                split_parts(chain, dve, q_f[:], [parts[:, 0, i] for i in range(3)], rest[:])
                for kind in range(parts.shape[1] - 1):
                    split_parts(chain, dve, k_f[:, kind], [parts[:, 1 + kind, i] for i in range(3)],
                                rest[:])
                dve.wait_ge(S.v_ready, 1)
                chain(dve.tensor_copy(values[:, :, :, 0:HD],
                                      v_ps[:].rearrange("p a c (h d) -> p (a c) h d", d=HD)))


def attend_pairs(nc, K, key, two, parts, stack_q, stack_k, pick_f, values, v_f, qk, bias_cols,
                 table, merged, relative):
    n_ops = qk.shape[2]
    half = T // QW
    units = [(pr, t, h) for pr in range(2) for t in range(QT) for h in range(2)]
    n_units = len(units)
    per_pair = n_units // 2
    stack_before = {6 + i: i for i in range(n_ops)}
    passing = [("stack", 0, i) for i in range(n_ops)]
    for n in range(n_units):
        if n in stack_before:
            passing.append(("stack", 1, stack_before[n]))
        passing.append(("unit", n))
    e_lead = 6
    ring = 4
    with ExitStack() as ctx:
        M = Memory(nc, ctx)
        weights = M.sb(f"{key}_weights", [P, 3, T])
        turned = M.sb(f"{key}_turned", [P, 2, QT, P])
        neg_max = M.sb(f"{key}_neg_max", [P, n_units])
        recip = M.sb(f"{key}_recip", [P, QT, 2])
        s_ps = M.ps(f"{key}_s_ps", [P, 2, T])
        t_ps = M.ps(f"{key}_t_ps", [P, 2, 4, P])
        o_ps = M.ps(f"{key}_o_ps", [P, QW])
        o_sb = M.sb(f"{key}_o_sb", [P, QW])
        if relative:
            e_sb = M.sb(f"{key}_e_sb", [P, ring, 2, QW])
            band = M.sb(f"{key}_band", [P, ring, 2, BAND])
            e_ps = M.ps(f"{key}_e_ps", [P, QW])
            scratch = K.scratch
        with stage(nc, "scores_ready", "masked", "max_ready", "exps_ready", "turned_ready",
                   "copied_dve", "copied_act", "out_ready", "e_ready", "e_copied", "e_written_even",
                   "stacked", "stack_act", "stack_dve", "v_copied", "picked",
                   "e_written_odd", "band_loaded_even", "band_loaded_odd",
                   "o_copied", "o_turned", "merged", "dve_chain") as (block, S):

            e_written = (S.e_written_even, S.e_written_odd)
            band_loaded = (S.band_loaded_even, S.band_loaded_odd)

            def nth(tile):
                return 16 * (tile // 2 + 1)

            def stacked_by(pr, i):
                return (S.stack_act, S.stack_dve)[i % 2], pr * (n_ops // 2) + i // 2 + 1

            def slot(*what):
                return passing.index(what) % 2

            def wait_for_slot(pe, *what):
                at = passing.index(what)
                if at >= 2:
                    before = passing[at - 2]
                    if before[0] == "unit":
                        pe.wait_ge(S.exps_ready, before[1] + 1)
                    else:
                        pe.wait_ge(*stacked_by(*before[1:]))

            def width(t):
                return T if relative else (t + 1) * P

            def blocks(t):
                return width(t) // P

            def near(t):
                return max(0, (t - 1) * P), min(T, (t + 2) * P)

            @block.gpsimd
            def _(pool):
                pool.tensor_copy(v_f[:, :, :, 0:HD + 1], values[:, :, bass.ds(two * 4, 4), :]) \
                    .then_inc(S.v_copied, 1)
                pool.wait_ge(S.stacked, 2 * n_ops)
                following = (two + 1) % (PAIRS // 2)
                for i, stack in enumerate((stack_q, stack_k)):
                    pool.tensor_copy(pick_f[:, :, i].rearrange("p r (i n) -> p r i n", i=3),
                                     stack[:, bass.ds(following * 2, 2)]).then_inc(S.picked, 1)
                pool.wait_ge(S.picked, 2)

            @block.tensor
            def _(pe):
                def stack(pr, i):
                    wait_for_slot(pe, "stack", pr, i)
                    for j in range(half):
                        for part in range(3):
                            ins = pe.matmul(s_ps[:, slot("stack", pr, i), cols(j, QW)],
                                            pick_f[:, pr, min(i, 1), cols(part, P)],
                                            parts[:, i, part, cols(j, QW)], start=(part == 0),
                                            stop=(part == 2))
                    ins.then_inc(S.stacked, 1)

                def positions(n):
                    pr, t, h = units[n]
                    if n % per_pair == 0:
                        pe.wait_ge(*stacked_by(pr, 0))
                    if n >= 1:
                        pe.wait_ge(S.e_copied, n)
                    rows = slice(64 * h, 64 * h + 64)
                    pe.matmul(e_ps[:], qk[rows, pr, 0, cols(t, P)], table[rows, :], start=True,
                              stop=True).then_inc(S.e_ready, 1)

                def scores(n):
                    pr, t, h = units[n]
                    wait_for_slot(pe, "unit", n)
                    if n % per_pair == 0:
                        for i in range(n_ops - 2, n_ops):
                            pe.wait_ge(*stacked_by(pr, i))
                    rows = slice(64 * h, 64 * h + 64)
                    if relative:
                        lo, hi = near(t)
                        spans = [(0, lo, 2), (lo, hi, 1), (hi, T, 3)]
                    else:
                        spans = [(0, width(t), 1)]
                    cuts = [(max(a, c), min(z, c + QW), kind) for a, z, kind in spans
                            for c in range(0, T, QW) if max(a, c) < min(z, c + QW)]
                    for a, z, kind in cuts:
                        ins = pe.matmul(s_ps[:, slot("unit", n), a:z], qk[rows, pr, 0, cols(t, P)],
                                        qk[rows, pr, kind, a:z], start=True, stop=True)
                    ins.then_inc(S.scores_ready, 1)

                def turn(n):
                    pr, t, h = units[n]
                    pe.wait_ge(S.exps_ready, n + 1)
                    if n >= 1:
                        pe.wait_ge(S.copied_dve, n)
                        pe.wait_ge(S.copied_act, n)
                    if n >= per_pair + 2:
                        pe.wait_ge(S.merged, 1)
                    for j in range(blocks(t)):
                        ins = pe.transpose(t_ps[:, j // 4, j % 4], weights[:, n % 3, cols(j, P)],
                                           K.ident[:])
                    ins.then_inc(S.turned_ready, 1)

                def weighted(n):
                    pr, t, h = units[n]
                    pe.wait_ge(S.copied_dve, n + 1)
                    pe.wait_ge(S.copied_act, n + 1)
                    if n == 0:
                        pe.wait_ge(S.v_copied, 1)
                    if n == per_pair:
                        pe.wait_ge(S.o_copied, 1)
                    at = OUT_ROWS * (2 * (t // 4) + h)
                    for j in range(blocks(t)):
                        ins = pe.matmul(o_ps[at:at + OUT_ROWS, cols(t % 4, P)], v_f[:, j, 2 * pr + h],
                                        turned[:, n % 2, j], start=(j == 0),
                                        stop=(j == blocks(t) - 1))
                    ins.then_inc(S.out_ready, 1)

                def turn_outputs(pr):
                    units_done = n_units if pr else per_pair + 2
                    pe.wait_ge(S.copied_dve, units_done)
                    pe.wait_ge(S.copied_act, units_done)
                    pe.wait_ge(S.o_copied, pr + 1)
                    for c in range(4):
                        ins = pe.transpose(t_ps[:, 0, c], o_sb[:, cols(c, P)], K.ident[:])
                    ins.then_inc(S.o_turned, 1)

                stack(0, 0)
                stack(0, 1)
                if relative:
                    for n in range(e_lead):
                        positions(n)
                        if n < 2:
                            stack(0, 2 + n)
                for n in range(n_units + 3):
                    if n in stack_before:
                        stack(1, stack_before[n])
                    if n < n_units:
                        scores(n)
                    if relative and n + e_lead < n_units:
                        positions(n + e_lead)
                    if n == per_pair + 4:
                        turn_outputs(0)
                    if 2 <= n <= n_units + 1:
                        turn(n - 2)
                    if n >= 3:
                        weighted(n - 3)
                turn_outputs(1)

            @block.scalar
            def _(act):
                def copy_positions(n):
                    pr, t, h = units[n]
                    act.wait_ge(S.e_ready, n + 1)
                    tile = pr * QT + t
                    if tile >= ring:
                        act.wait_ge(e_written[tile % 2], nth(tile - ring))
                    act.activation(e_sb[:, tile % ring, h], e_ps[:], ACT.Copy).then_inc(S.e_copied, 1)

                def exps(n):
                    pr, t, h = units[n]
                    act.wait_ge(S.max_ready, n + 1)
                    if n >= 3:
                        act.wait_ge(S.turned_ready, n - 2)
                    act.activation(weights[:, n % 3, 0:width(t)],
                                   s_ps[:, slot("unit", n), 0:width(t)], ACT.Exp,
                                   bias=neg_max[:, n:n + 1]).then_inc(S.exps_ready, 1)

                def copy_turned(n):
                    pr, t, h = units[n]
                    act.wait_ge(S.turned_ready, n + 1)
                    if n >= 2:
                        act.wait_ge(S.out_ready, n - 1)
                    if blocks(t) > 4:
                        act.activation(turned[:, n % 2, 4:blocks(t)], t_ps[:, 1, 0:blocks(t) - 4],
                                       ACT.Copy).then_inc(S.copied_act, 1)
                    else:
                        act.sem_inc(S.copied_act, 1)

                def copy_stacked(pr, i):
                    act.wait_ge(S.stacked, pr * n_ops + i + 1)
                    kw = {"bias": bias_cols[:, i:i + 1]} if relative else {}
                    act.activation(qk[:, pr, i], s_ps[:, slot("stack", pr, i)], ACT.Identity, **kw) \
                        .then_inc(S.stack_act, 1)

                copy_stacked(0, 0)
                if relative:
                    for n in range(e_lead):
                        copy_positions(n)
                        if n == 0:
                            copy_stacked(0, 2)
                for n in range(n_units + 2):
                    if stack_before.get(n, 1) % 2 == 0:
                        copy_stacked(1, stack_before[n])
                    if relative and n + e_lead < n_units:
                        copy_positions(n + e_lead)
                    if n < n_units:
                        exps(n)
                    if n >= 2:
                        copy_turned(n - 2)

            if relative:
                @block.sync
                def _(sp):
                    tiles = 2 * QT
                    for t in range(tiles + 1):
                        if t < tiles:
                            sp.wait_ge(S.e_copied, 2 * (t + 1))
                            if t >= ring:
                                sp.wait_ge(band_loaded[t % 2], nth(t - ring))
                            if t >= 2:
                                sp.wait_ge(e_written[t % 2], nth(t - 2))
                            sp.dma_start(scratch[t % ring].rearrange("h p n -> p h n"),
                                         e_sb[:, t % ring]).then_inc(e_written[t % 2], 16)
                        if t >= 1:
                            r = t - 1
                            place = scratch[r % ring]
                            sp.wait_ge(e_written[r % 2], nth(r))
                            if r >= 2:
                                sp.wait_ge(band_loaded[r % 2], nth(r - 2))
                            if r >= ring:
                                sp.wait_ge(S.masked, 2 * (r - ring + 1))
                            skewed = bass.AP(place.tensor, place.offset + P - 1,
                                             [[QW - 1, P], [P * QW, 2], [1, BAND]])
                            sp.dma_start(band[:, r % ring], skewed).then_inc(band_loaded[r % 2], 16)

            @block.vector
            def _(dve):
                chain = Chain(dve, S.dve_chain)

                def maxima(n):
                    pr, t, h = units[n]
                    dve.wait_ge(S.scores_ready, n + 1)
                    if relative:
                        lo, hi = near(t)
                        at = lo - (t - 1) * P
                        tile = pr * QT + t
                        dve.wait_ge(band_loaded[tile % 2], nth(tile))
                        add = band[:, tile % ring, h, at:at + hi - lo]
                    else:
                        lo, hi = t * P, (t + 1) * P
                        add = K.causal[:]
                    tile_scores = s_ps[:, slot("unit", n)]
                    dve.tensor_tensor(tile_scores[:, lo:hi], tile_scores[:, lo:hi], add, ALU.add) \
                        .then_inc(S.masked, 1)
                    dve.wait_ge(S.masked, n + 1)
                    dve.tensor_reduce(neg_max[:, n:n + 1], tile_scores[:, 0:width(t)], AX_X, ALU.max,
                                      negate=True).then_inc(S.max_ready, 1)

                def copy_turned(n):
                    pr, t, h = units[n]
                    dve.wait_ge(S.turned_ready, n + 1)
                    if n >= 2:
                        dve.wait_ge(S.out_ready, n - 1)
                    k = min(4, blocks(t))
                    dve.tensor_copy(turned[:, n % 2, 0:k], t_ps[:, 0, 0:k]).then_inc(S.copied_dve, 1)

                def copy_stacked(pr, i):
                    dve.wait_ge(S.stacked, pr * n_ops + i + 1)
                    src = s_ps[:, slot("stack", pr, i)]
                    if relative:
                        dve.tensor_scalar(qk[:, pr, i], src, bias_cols[:, i:i + 1], None, ALU.add) \
                            .then_inc(S.stack_dve, 1)
                    else:
                        dve.tensor_copy(qk[:, pr, i], src).then_inc(S.stack_dve, 1)

                def copy_outputs(pr):
                    dve.wait_ge(S.out_ready, per_pair * (pr + 1))
                    if pr:
                        dve.wait_ge(S.o_turned, pr)
                    dve.tensor_copy(o_sb[:], o_ps[:]).then_inc(S.o_copied, 1)

                def merge(pr):
                    dve.wait_ge(S.o_turned, pr + 1)
                    for i in range(2):
                        rows = t_ps[:, 0, 0:4, 64 * i:64 * i + 64].rearrange(
                            "q c (h d) -> q c h d", h=2)
                        total = recip[:, 4 * i:4 * i + 4]
                        chain(dve.reciprocal(total, rows[:, :, :, HD]))
                        out = merged[:, 4 * i:4 * i + 4, bass.ds(two * 2 + pr, 1), :].rearrange(
                            "p t o (h d) -> p t (o h) d", h=2)
                        ins = dve.tensor_tensor(out, rows[:, :, :, 0:HD],
                                                total.unsqueeze(3).to_broadcast([P, 4, 2, HD]),
                                                ALU.mult)
                        if i == 0:
                            chain(ins)
                    ins.then_inc(S.merged, 1)

                for i in range(1, n_ops, 2):
                    copy_stacked(0, i)
                for n in range(n_units + 2):
                    if stack_before.get(n, 0) % 2 == 1:
                        copy_stacked(1, stack_before[n])
                    if n == per_pair + 3:
                        copy_outputs(0)
                    if n < n_units:
                        maxima(n)
                    if n == per_pair + 4:
                        merge(0)
                    if n >= 2:
                        copy_turned(n - 2)
                copy_outputs(1)
                merge(1)
                dve.wait_ge(S.merged, 2)


def merge_heads(nc, K, key, b, merged, x, w, relative):
    with ExitStack() as ctx:
        M = Memory(nc, ctx)
        half = T // QW
        rows = M.sb(f"{key}_rows", [P, T])
        m_ps = M.ps(f"{key}_m_ps", [P, half, QW])
        p_ps = M.ps(f"{key}_p_ps", [P, half, QW])
        with stage(nc, "turned_ready", "copied", "projected", "added") as (block, S):

            @block.tensor
            def _(pe):
                for t in range(QT):
                    ins = pe.transpose(m_ps[:, t // 4, cols(t % 4, P)],
                                       merged[:, t].rearrange("p a c -> p (a c)"), K.ident[:])
                ins.then_inc(S.turned_ready, 1)
                if not relative:
                    pe.wait_ge(S.copied, 1)
                    for j in range(half):
                        ins = pe.matmul(p_ps[:, j], w[:, 5], rows[:, cols(j, QW)], start=True,
                                        stop=True)
                    ins.then_inc(S.projected, 1)

            @block.vector
            def _(dve):
                dve.wait_ge(S.turned_ready, 1)
                src = m_ps
                if not relative:
                    dve.tensor_copy(rows[:], m_ps[:].rearrange("p j n -> p (j n)")) \
                        .then_inc(S.copied, 1)
                    dve.wait_ge(S.projected, 1)
                    src = p_ps
                out = x[:, bass.ts(b, T)]
                dve.tensor_tensor(out, out, src[:].rearrange("p j n -> p (j n)"), ALU.add) \
                    .then_inc(S.added, 1)
                dve.wait_ge(S.added, 1)



LEAVES, DEPTH3 = 16, 4
NODES = LEAVES - 1


def walk_tree(nc, K, name, xn, node_w, node_b, reach):
    with ExitStack() as ctx:
        M = Memory(nc, ctx)
        right = M.sb(f"{name}_right", [P, TILES, LEAVES])
        left = M.sb(f"{name}_left", [P, TILES, LEAVES])
        level = M.sb(f"{name}_level", [P, 2, TILES, LEAVES])
        scores = M.ps(f"{name}_scores", [P, TILES, LEAVES])
        with stage(nc, "scores_ready", "dve_chain") as (block, S):

            @block.tensor
            def _(pe):
                for t in range(TILES):
                    pe.matmul(scores[:, t], xn[:, cols(t, P)], node_w, start=True, stop=False)
                    last = pe.matmul(scores[:, t], K.ones[0:1, 0:P], node_b, start=False, stop=True)
                last.then_inc(S.scores_ready, 1)

            @block.vector
            def _(dve):
                chain = Chain(dve, S.dve_chain)
                chain(dve.memset(level[:, 0], 1.0))
                dve.wait_ge(S.scores_ready, 1)
                chain(dve.tensor_scalar(right[:], scores[:], 0.0, None, ALU.is_ge))
                chain(dve.tensor_scalar(left[:], right[:], -1.0, 1.0, ALU.mult, ALU.add))
                for d in range(DEPTH3):
                    n = 1 << d
                    here = level[:, d % 2, :, 0:n]
                    if d == DEPTH3 - 1:
                        below = reach[:]
                    else:
                        below = level[:, (d + 1) % 2, :, 0:2 * n]
                    below = below.rearrange("p t (n two) -> p t n two", two=2)
                    nodes = slice(n - 1, 2 * n - 1)
                    chain(dve.tensor_tensor(below[:, :, :, 0], here, left[:, :, nodes], ALU.mult))
                    chain(dve.tensor_tensor(below[:, :, :, 1], here, right[:, :, nodes], ALU.mult))


def block3_ffn(nc, K, W, xn, x):
    with ExitStack() as ctx:
        M = Memory(nc, ctx)
        qkv = [M.sb(f"b3f_{n}", [P, N]) for n in "qkv"]
        with ExitStack() as inner:
            I = Memory(nc, inner)
            halves = LEAVES // 2
            up = I.sb("b3f_up", [P, halves, P])
            down = I.sb("b3f_down", [P, halves, P])
            b1 = I.sb("b3f_b1", [P, halves])
            b2 = I.sb("b3f_b2", [LEAVES, P])
            node_w = I.sb("b3f_node_w", [P, LEAVES])
            node_b = I.sb("b3f_node_b", [1, LEAVES])
            reach = I.sb("b3f_reach", [P, TILES, LEAVES])
            gates = I.sb("b3f_gates", [LEAVES, N])
            gates_short = I.sb("b3f_gates_short", [LEAVES, N], BF16)
            pick = I.sb("b3f_pick", [LEAVES, halves, P], BF16)
            load(nc, "b3f_pick", [(pick[:], W["c_pick16_short"])])
            for n, dst in zip("qkv", qkv):
                load(nc, f"b3f_{n}", [(up[:], W[f"b3f_{n}_up"]), (down[:], W[f"b3f_{n}_down"]),
                                      (b1[:], W[f"b3f_{n}_b1"]), (b2[:], W[f"b3f_{n}_b2"]),
                                      (node_w[:], W[f"b3f_{n}_node_w"]),
                                      (node_b[:], W[f"b3f_{n}_node_b"])])
                walk_tree(nc, K, f"b3f_{n}", xn, node_w[:], node_b[:], reach)
                to_rows(nc, K, f"b3f_{n}", reach, LEAVES, gates, gates_short)
                chunks = [(up[:, c], b1[:, c:c + 1], down[:, c], pick[:, c], c)
                          for c in range(halves)]
                mlp(nc, K, f"b3f_{n}", xn, dst, chunks, ACT.Relu, gates, LEAVES, b2[:], add=False,
                    select_from=gates_short)
        one_head(nc, K, qkv, x)


def one_head(nc, K, qkv, x):
    q_all, k_all, v_all = qkv
    scale = float(P) ** -0.5
    units = [(b, t) for b in range(B) for t in range(QT)]
    n_units = len(units)
    with ExitStack() as ctx:
        M = Memory(nc, ctx)
        v_rows = M.sb("b3f_v_rows", [P, TILES, P])
        weights = M.sb("b3f_weights", [P, 2, T])
        turned = M.sb("b3f_turned", [P, 2, QT, P])
        stats = M.sb("b3f_stats", [P, 4, n_units])
        s_ps = M.ps("b3f_s_ps", [P, 2, T])
        t_ps = M.ps("b3f_t_ps", [P, 2, 4, P])
        o_ps = M.ps("b3f_o_ps", [P, P])
        with stage(nc, "v_turned", "v_copied", "scores_ready", "max_ready", "exps_ready",
                   "weights_ready", "turned_ready", "copied_act", "copied_dve", "out_ready",
                   "stored", "dve_chain") as (block, S):

            @block.tensor
            def _(pe):
                for t in range(TILES):
                    if t % 8 == 0 and t > 0:
                        pe.wait_ge(S.v_copied, t // 8)
                    ins = pe.transpose(t_ps[:, t % 8 // 4, t % 4], v_all[:, cols(t, P)], K.ident[:])
                    if t % 8 == 7:
                        ins.then_inc(S.v_turned, 1)
                pe.wait_ge(S.v_copied, TILES // 8)
                for n in range(n_units + 2):
                    if n < n_units:
                        b, t = units[n]
                        if n >= 2:
                            pe.wait_ge(S.exps_ready, n - 1)
                        for j in range(T // QW):
                            ins = pe.matmul(s_ps[:, n % 2, cols(j, QW)],
                                            q_all[:, cols(b * QT + t, P)],
                                            k_all[:, cols(b * (T // QW) + j, QW)], start=True,
                                            stop=True)
                        ins.then_inc(S.scores_ready, 1)
                    if 1 <= n <= n_units:
                        m = n - 1
                        pe.wait_ge(S.weights_ready, m + 1)
                        pe.wait_ge(S.copied_dve, m)
                        pe.wait_ge(S.copied_act, m)
                        for j in range(QT):
                            ins = pe.transpose(t_ps[:, j // 4, j % 4], weights[:, m % 2, cols(j, P)],
                                               K.ident[:])
                        ins.then_inc(S.turned_ready, 1)
                    if n >= 2:
                        m = n - 2
                        b, t = units[m]
                        pe.wait_ge(S.copied_dve, m + 1)
                        pe.wait_ge(S.copied_act, m + 1)
                        pe.wait_ge(S.stored, m)
                        for j in range(QT):
                            ins = pe.matmul(o_ps[:], v_rows[:, b * QT + j], turned[:, m % 2, j],
                                            start=(j == 0), stop=(j == QT - 1))
                        ins.then_inc(S.out_ready, 1)

            @block.scalar
            def _(act):
                for n in range(n_units + 1):
                    if n < n_units:
                        act.wait_ge(S.max_ready, n + 1)
                        if n >= 2:
                            act.wait_ge(S.turned_ready, n - 1)
                        act.activation(weights[:, n % 2], s_ps[:, n % 2], ACT.Exp, scale=scale,
                                       bias=stats[:, 1, n:n + 1],
                                       accum_out=stats[:, 2, n:n + 1]).then_inc(S.exps_ready, 1)
                    if n >= 1:
                        m = n - 1
                        act.wait_ge(S.turned_ready, m + 1)
                        if m >= 2:
                            act.wait_ge(S.out_ready, m - 1)
                        act.activation(turned[:, m % 2, 4:], t_ps[:, 1], ACT.Copy) \
                            .then_inc(S.copied_act, 1)

            @block.vector
            def _(dve):
                chain = Chain(dve, S.dve_chain)
                for i in range(TILES // 8):
                    dve.wait_ge(S.v_turned, i + 1)
                    dve.tensor_copy(v_rows[:, 8 * i:8 * i + 8], t_ps[:].rearrange("p a c n -> p (a c) n")) \
                        .then_inc(S.v_copied, 1)
                for n in range(n_units + 2):
                    if n < n_units:
                        dve.wait_ge(S.scores_ready, n + 1)
                        chain(dve.tensor_reduce(stats[:, 0, n:n + 1], s_ps[:, n % 2], AX_X, ALU.max))
                        dve.tensor_scalar(stats[:, 1, n:n + 1], stats[:, 0, n:n + 1], -scale, None,
                                          ALU.mult).then_inc(S.max_ready, 1)
                        dve.wait_ge(S.exps_ready, n + 1)
                        chain(dve.reciprocal(stats[:, 3, n:n + 1], stats[:, 2, n:n + 1]))
                        dve.tensor_scalar(weights[:, n % 2], weights[:, n % 2], stats[:, 3, n:n + 1],
                                          None, ALU.mult).then_inc(S.weights_ready, 1)
                    if 1 <= n <= n_units:
                        m = n - 1
                        dve.wait_ge(S.turned_ready, m + 1)
                        if m >= 2:
                            dve.wait_ge(S.out_ready, m - 1)
                        dve.tensor_copy(turned[:, m % 2, 0:4], t_ps[:, 0]).then_inc(S.copied_dve, 1)
                    if n >= 2:
                        b, t = units[n - 2]
                        dve.wait_ge(S.out_ready, n - 1)
                        out = x[:, cols(b * QT + t, P)]
                        dve.tensor_tensor(out, out, o_ps[:], ALU.add).then_inc(S.stored, 1)
                dve.wait_ge(S.stored, n_units)



LAYERS, HD2, WIN = 6, 64, 32
WINS = P // WIN
INNER = HEADS * HD2
FF, FF_PAD = 341, 384
LEAD = WIN
SEQ_COLS = LEAD + T
QK_SCALE = 8.0
TURNS = 6


def block2_ffn(nc, K, W, xn, x):
    with ExitStack() as ctx:
        M = Memory(nc, ctx)
        cur_all = M.sb("b2f_cur", [P, 3 * P + N])
        mid_all = M.sb("b2f_mid", [P, 3 * P + N])
        G = Names(
            cur_all=cur_all, mid_all=mid_all, cur=cur_all[:, 2 * P:2 * P + N], mid=mid_all[:, 2 * P:2 * P + N],
            shifted=M.sb("b2f_shifted", [P, B * SEQ_COLS + 3 * (LEAD + P)]),
            wqkv=M.sb("b2f_wqkv", [P, 3 * INNER]), wo=M.sb("b2f_wo", [P, PAIRS, P]),
            w1=M.sb("b2f_w1", [P, 6, P]), w2=M.sb("b2f_w2", [P, 3, P]),
            small=M.sb("b2f_small", [P, 9]), scales=M.sb("b2f_scales", [P, 4, HD2]),
            rotary=M.sb("b2f_rotary", [P, QT, 4, HD2]), mask=M.sb("b2f_mask", [P, QT, HD2]),
            qt=M.sb("b2f_qt", [P, PAIRS, P]), kt=M.sb("b2f_kt", [P, PAIRS, WIN + P]),
            values=M.sb("b2f_values", [P, 2, WINS, PAIRS * HD2]),
            o_rows=M.sb("b2f_o_rows", [P, PAIRS, 2, HD2]), minus_half=M.sb("b2f_minus_half", [P, 2 * HEADS]),
            xt=M.sb("b2f_xt", [P, WIN + P]),
            turn=M.sb("b2f_turn", [P, 2, 4, HD2]), mask_t=M.sb("b2f_mask_t", [P, 2, HD2]),
            keep=M.sb("b2f_keep", [P, QT]), keep_t=M.sb("b2f_keep_t", [P, 1]))
        with stage(nc, "copied") as (block, S):

            @block.vector
            def _(dve):
                dve.memset(G.cur_all[:, 0:2 * P], 0.0).then_inc(S.copied, 1)
                dve.memset(G.o_rows[:], 0.0).then_inc(S.copied, 1)
                dve.memset(G.minus_half[:], -0.5).then_inc(S.copied, 1)
                dve.memset(G.qt[:], 0.0).then_inc(S.copied, 1)
                dve.memset(G.values[:], 0.0).then_inc(S.copied, 1)
                dve.memset(G.mask_t[:], 0.0).then_inc(S.copied, 1)
                dve.tensor_copy(G.cur, xn[:]).then_inc(S.copied, 1)
                dve.memset(G.shifted[:], 0.0).then_inc(S.copied, 1)
                dve.memset(G.kt[:], 0.0).then_inc(S.copied, 1)
                dve.wait_ge(S.copied, 9)
        load(nc, "b2f_mask", [(G.mask[:], W["c_local_mask"]), (G.keep[:], W["c_keep"])])
        first_weights(nc, W, G)
        with nc.Fori(0, LAYERS) as layer:
            shift_tokens(nc, G.cur, G.shifted, LEAD, ffn_loads(W, G, layer))
            with nc.Fori(0, (TILES + 2) // TURNS) as i:
                local_tiles(nc, K, G, i * TURNS)
            shift_tokens(nc, G.mid, G.shifted, 0)
            layer_norm(nc, K, "b2n", G.shifted, G.shifted, gain=G.small[:, 0:1],
                       offset=G.small[:, 1:2])
            gated_ffn(nc, K, G, attention_loads(W, G, (layer + 1) % LAYERS))
        add_tokens(nc, x[:], G.cur)


def shift_tokens(nc, src, dst, lead, loads=()):
    with stage(nc, "moved", "loaded") as (block, S):
        step = lead + T

        @block.sync
        def _(sp):
            for tile, array in loads:
                sp.dma_start(tile, array).then_inc(S.loaded, 16)
            if loads:
                sp.wait_ge(S.loaded, 16 * len(loads))

        @block.vector
        def _(dve):
            for b in range(B):
                at = b * step + lead
                dve.tensor_copy(dst[0:64, at:at + T], src[0:64, b * T:(b + 1) * T]).then_inc(S.moved, 1)
                dve.memset(dst[64:P, at:at + 1], 0.0).then_inc(S.moved, 1)

        @block.scalar
        def _(act):
            for b in range(B):
                at = b * step + lead
                act.activation(dst[64:P, at + 1:at + T], src[64:P, b * T:(b + 1) * T - 1], ACT.Copy) \
                    .then_inc(S.moved, 1)
            act.wait_ge(S.moved, 3 * B)


def attention_loads(W, G, layer):
    of_layer = lambda key: W[key][bass.ds(layer, 1)].squeeze()
    return [(G.wqkv[:], of_layer("b2f_wqkv")), (G.wo[:], of_layer("b2f_wo")),
            (G.scales[:], of_layer("b2f_scales")), (G.rotary[:], W["c_rotary2"])]


def ffn_loads(W, G, layer):
    of_layer = lambda key: W[key][bass.ds(layer, 1)].squeeze()
    return [(G.w1[:], of_layer("b2f_w1")), (G.w2[:], of_layer("b2f_w2")),
            (G.small[:], of_layer("b2f_small"))]


def scale_rotary(dve, G):
    return dve.tensor_tensor(G.rotary[:], G.rotary[:],
                             G.scales[:].unsqueeze(1).to_broadcast([P, QT, 4, HD2]), ALU.mult)


def first_weights(nc, W, G):
    with stage(nc, "loaded", "scaled") as (block, S):
        loads = attention_loads(W, G, 0)

        @block.sync
        def _(sp):
            for tile, array in loads:
                sp.dma_start(tile, array).then_inc(S.loaded, 16)

        @block.vector
        def _(dve):
            dve.wait_ge(S.loaded, 16 * len(loads))
            scale_rotary(dve, G).then_inc(S.scaled, 1)
            dve.wait_ge(S.scaled, 1)


def local_tiles(nc, K, G, first):
    with ExitStack() as ctx:
        M = Memory(nc, ctx)
        sq = M.sb("b2t_sq", [P, 2 * HEADS, HD2])
        part = M.sb("b2t_part", [P, 2 * HEADS, HD2])
        qk = M.sb("b2t_qk", [P, 2 * HEADS, HD2])
        norm = M.sb("b2t_norm", [P, 2 * HEADS])
        prob = M.sb("b2t_prob", [P, PAIRS, 2, HD2])
        top = M.sb("b2t_top", [P, PAIRS, 2])
        total = M.sb("b2t_total", [P, PAIRS, 2])
        pt = M.sb("b2t_pt", [P, PAIRS, P])
        o_cols = M.sb("b2t_o_cols", [P, PAIRS, P])
        qk_ps = M.ps("b2t_qk_ps", [P, 4, QW])
        s_ps = M.ps("b2t_s_ps", [P, 2, QW])
        w_ps = M.ps("b2t_w_ps", [P, 2, QW])
        with stage(nc, "xt_loaded", "qk_ready", "squared", "inverted", "summed", "normed",
                   "qk_turned", "qt_copied", "kt_carried", "scores_ready", "masked", "shifted",
                   "exps_ready", "probs_turned", "pt_low", "pt_high", "out_ready",
                   "o_copied", "o_turned", "o_taken", "y_ready", "y_stored", "v_ready", "v_copied",
                   "v_carried", "table_loaded", "mask_loaded", "dve_chain",
                   "pool_chain") as (block, S):
            PER = {"qk_ready": 4, "squared": 4, "summed": 2, "inverted": 2, "normed": 2,
                   "qk_turned": 4, "qt_copied": 4, "probs_turned": 2, "out_ready": 2,
                   "o_copied": 2, "o_turned": 2, "o_taken": 2, "v_copied": 10, "v_carried": 2}

            def due(k, name, n):
                return k * PER.get(name, 1) + n

            @block.gpsimd
            def _(pool):
                chain = Chain(pool, S.pool_chain)

                def load_tokens(k):
                    tile = first + k
                    if k:
                        pool.wait_ge(S.v_ready, due(k, "v_ready", 0))
                        pool.wait_ge(S.qk_ready, due(k, "qk_ready", 0))
                    pool.tensor_copy(G.xt[:], G.shifted[:, bass.ds(tile * P + (tile // QT) * LEAD,
                                                                   WIN + P)]).then_inc(S.xt_loaded, 1)

                def load_turn(k):
                    tile = first + k
                    if k >= 2:
                        pool.wait_ge(S.normed, due(k - 1, "normed", 0))
                    pool.tensor_copy(G.turn[:, k % 2], G.rotary[:, bass.ds(tile % QT, 1)].squeeze()) \
                        .then_inc(S.table_loaded, 1)
                    if k:
                        pool.wait_ge(S.masked, due(k, "masked", 0))
                    pool.tensor_copy(G.mask_t[:, k % 2], G.mask[:, bass.ds(tile % QT, 1)].squeeze()) \
                        .then_inc(S.mask_loaded, 1)
                    chain(pool.tensor_copy(G.keep_t[:], G.keep[:, bass.ds(tile % QT, 1)]))

                for k in range(TURNS):
                    if k == 0:
                        load_tokens(0)
                        load_turn(0)
                    if k:
                        pool.wait_ge(S.out_ready, due(k, "out_ready", 0))
                        pool.wait_ge(S.v_copied, due(k, "v_copied", 0))
                        pool.wait_ge(S.inverted, due(k, "inverted", 0))
                    for h in range(2):
                        pool.tensor_copy(G.values[HD2 * h:HD2 * h + WIN, k % 2, 0],
                                         G.values[HD2 * h + WIN:HD2 * h + 2 * WIN, 1 - k % 2,
                                                  WINS - 1]).then_inc(S.v_carried, 1)
                        pool.wait_ge(S.v_carried, due(k, "v_carried", h + 1))
                    pool.wait_ge(S.scores_ready, due(k, "scores_ready", 1))
                    pool.tensor_scalar(G.kt[:, :, 0:WIN], G.kt[:, :, P:P + WIN], G.keep_t[:], None,
                                       ALU.mult).then_inc(S.kt_carried, 1)
                    for i in range(2):
                        if i == 1 and k + 1 < TURNS:
                            load_tokens(k + 1)
                        pool.wait_ge(S.summed, due(k, "summed", i + 1))
                        pool.tensor_tensor(norm[:, cols(i, HEADS)], norm[:, cols(i, HEADS)],
                                           G.minus_half[:, cols(i, HEADS)], ALU.pow) \
                            .then_inc(S.inverted, 1)
                    if k + 1 < TURNS:
                        pool.wait_ge(S.kt_carried, due(k, "kt_carried", 1))
                        load_turn(k + 1)

            @block.tensor
            def _(pe):
                def project(j):
                    pe.matmul(qk_ps[:, j], G.xt[:, WIN:], G.wqkv[:, cols(j, QW)], start=True,
                              stop=True).then_inc(S.qk_ready, 1)

                def turn_features(k, j):
                    for c in range(4):
                        n = 4 * j + c
                        src = qk[:, 2 * n:2 * n + 2].rearrange("t h d -> t (h d)")
                        ins = pe.transpose(qk_ps[:, j, cols(c, P)], src, K.ident[:])
                    ins.then_inc(S.qk_turned, 1)

                for k in range(TURNS):
                    if k == 0:
                        pe.wait_ge(S.xt_loaded, 1)
                        project(0)
                        project(1)
                    if k:
                        pe.wait_ge(S.qt_copied, due(k, "qt_copied", 0))
                        pe.wait_ge(S.o_copied, due(k, "o_copied", 0))
                    for h in range(2):
                        rows = slice(HD2 * h, HD2 * h + HD2)
                        for p in range(PAIRS):
                            for w in range(WINS):
                                ins = pe.matmul(s_ps[WIN * w:WIN * w + WIN, h, cols(p, HD2)],
                                                G.qt[rows, p, cols(w, WIN)],
                                                G.kt[rows, p, WIN * w:WIN * w + 2 * WIN],
                                                start=True, stop=True)
                    ins.then_inc(S.scores_ready, 1)
                    if k:
                        pe.wait_ge(S.pt_low, due(k, "pt_low", 0))
                        pe.wait_ge(S.pt_high, due(k, "pt_high", 0))
                    wv = G.wqkv[:, 2 * INNER:].rearrange("k (p h d) -> k p h d", h=2, d=HD2)
                    for h in range(2):
                        ins = pe.matmul(w_ps[:, h], G.xt[:, WIN:], wv[:, :, h], start=True, stop=True)
                    ins.then_inc(S.v_ready, 1)
                    pe.wait_ge(S.masked, due(k, "masked", 1))
                    for p in range(PAIRS):
                        ins = pe.transpose(s_ps[:, p // 4, cols(p % 4, P)],
                                           G.o_rows[:, p].rearrange("q h d -> q (h d)"), K.ident[:])
                        if p % 4 == 3:
                            ins.then_inc(S.o_turned, 1)
                    project(2)
                    project(3)
                    pe.wait_ge(S.exps_ready, due(k, "exps_ready", 1))
                    for half in range(2):
                        pe.wait_ge(S.v_copied, due(k, "v_copied", 5 * (half + 1)))
                        for p in range(4 * half, 4 * half + 4):
                            ins = pe.transpose(w_ps[:, half, cols(p % 4, P)],
                                               prob[:, p].rearrange("q h j -> q (h j)"), K.ident[:])
                        ins.then_inc(S.probs_turned, 1)
                        if half == 0:
                            pe.wait_ge(S.o_taken, due(k, "o_taken", 2))
                            for p in range(PAIRS):
                                ins = pe.matmul(s_ps[:, 0, 0:P], G.wo[:, p], o_cols[:, p],
                                                start=(p == 0), stop=(p == PAIRS - 1))
                            ins.then_inc(S.y_ready, 1)
                    pe.wait_ge(S.normed, due(k, "normed", 1))
                    turn_features(k, 0)
                    turn_features(k, 1)
                    if k:
                        pe.wait_ge(S.v_carried, due(k, "v_carried", 0))
                    pe.wait_ge(S.pt_low, due(k, "pt_low", 1))
                    pe.wait_ge(S.pt_high, due(k, "pt_high", 1))
                    pe.wait_ge(S.y_stored, due(k, "y_stored", 1))
                    for h in range(2):
                        rows = slice(HD2 * h, HD2 * h + HD2)
                        for p in range(PAIRS):
                            for w in range(WINS):
                                ins = pe.matmul(s_ps[WIN * w:WIN * w + WIN, h, cols(p, HD2)],
                                                pt[rows, p, cols(w, WIN)],
                                                G.values[rows, 1 - k % 2, w, cols(p, HD2)],
                                                start=True, stop=True)
                        ins.then_inc(S.out_ready, 1)
                    if k + 1 < TURNS:
                        pe.wait_ge(S.xt_loaded, due(k + 1, "xt_loaded", 1))
                        for j in range(2):
                            pe.wait_ge(S.qt_copied, due(k, "qt_copied", j + 1))
                            project(j)
                    pe.wait_ge(S.normed, due(k, "normed", 2))
                    turn_features(k, 2)
                    turn_features(k, 3)

            @block.scalar
            def _(act):
                def square(k, j):
                    if k and j % 2 == 0:
                        act.wait_ge(S.summed, due(k - 1, "summed", j // 2 + 1))
                    act.wait_ge(S.qk_ready, due(k, "qk_ready", j + 1))
                    act.activation(sq[:, 8 * j:8 * j + 8].rearrange("t h d -> t (h d)"),
                                   qk_ps[:, j], ACT.Square).then_inc(S.squared, 1)

                def copy_features(k, j, dst):
                    act.wait_ge(S.qk_turned, due(k, "qk_turned", j + 1))
                    act.activation(dst, qk_ps[:, j].rearrange("p (c n) -> p c n", c=4), ACT.Copy) \
                        .then_inc(S.qt_copied, 1)

                def copy_values(k, h):
                    for w, src, dst, n in ((1, 0, 0, 64), (3, 64, 0, 64), (2, 32, 0, 32),
                                           (2, 64, 32, 32), (0, 0, 32, 32)):
                        at = HD2 * h + dst
                        act.activation(G.values[at:at + n, k % 2, w], w_ps[src:src + n, h],
                                       ACT.Copy).then_inc(S.v_copied, 1)

                for k in range(TURNS):
                    if k == 0:
                        square(0, 0)
                        square(0, 1)
                    act.wait_ge(S.v_ready, due(k, "v_ready", 1))
                    if k:
                        act.wait_ge(S.out_ready, due(k, "out_ready", 0))
                        act.wait_ge(S.v_carried, due(k, "v_carried", 0))
                    copy_values(k, 0)
                    act.wait_ge(S.shifted, due(k, "shifted", 1))
                    act.activation(prob[:], prob[:], ACT.Exp).then_inc(S.exps_ready, 1)
                    copy_values(k, 1)
                    square(k, 2)
                    square(k, 3)
                    act.wait_ge(S.probs_turned, due(k, "probs_turned", 2))
                    if k:
                        act.wait_ge(S.out_ready, due(k, "out_ready", 0))
                    act.activation(pt[:, 4:], w_ps[:, 1], ACT.Copy).then_inc(S.pt_high, 1)
                    copy_features(k, 0, G.qt[:, 0:4])
                    copy_features(k, 1, G.qt[:, 4:8])
                    if k + 1 < TURNS:
                        square(k + 1, 0)
                        square(k + 1, 1)
                    act.wait_ge(S.kt_carried, due(k, "kt_carried", 1))
                    copy_features(k, 2, G.kt[:, 0:4, WIN:])
                    copy_features(k, 3, G.kt[:, 4:8, WIN:])
                act.wait_ge(S.qt_copied, due(TURNS, "qt_copied", 0))

            @block.vector
            def _(dve):
                chain = Chain(dve, S.dve_chain)
                half = HD2 // 2
                raw = qk_ps[:].rearrange("t j n -> t (j n)").rearrange("t (k h d) -> t k h d",
                                                                       k=2, h=HEADS)
                qk_v = qk[:].rearrange("t (k h) d -> t k h d", k=2)
                part_v = part[:].rearrange("t (k h) d -> t k h d", k=2)

                def rotate(k, i):
                    dve.wait_ge(S.squared, due(k, "squared", 2 * i + 2))
                    cos = G.turn[:, k % 2, 2 * i:2 * i + 1].to_broadcast([P, HEADS, HD2])
                    dve.tensor_tensor(qk_v[:, i], raw[:, i], cos, ALU.mult).then_inc(S.dve_chain, 1)
                    for lo, hi in ((0, half), (half, 0)):
                        sin = G.turn[:, k % 2, 2 * i + 1:2 * i + 2, lo:lo + half].to_broadcast(
                            [P, HEADS, half])
                        dve.tensor_tensor(part_v[:, i, :, lo:lo + half], raw[:, i, :, hi:hi + half],
                                          sin, ALU.mult).then_inc(S.dve_chain, 1)
                    chain.n += 3
                    dve.wait_ge(S.dve_chain, chain.n)
                    chain(dve.tensor_tensor(qk_v[:, i], qk_v[:, i], part_v[:, i], ALU.add))

                def lengths(k, i):
                    part_n = norm[:, cols(i, HEADS)]
                    dve.wait_ge(S.squared, due(k, "squared", 2 * i + 2))
                    if k:
                        dve.wait_ge(S.normed, due(k - 1, "normed", i + 1))
                    chain(dve.tensor_reduce(part_n, sq[:, cols(i, HEADS)], AX_X, ALU.add))
                    dve.tensor_scalar(part_n, part_n, 1e-24, None, ALU.max).then_inc(S.summed, 1)

                def normalise(k, i):
                    dve.wait_ge(S.inverted, due(k, "inverted", i + 1))
                    dve.tensor_tensor(qk_v[:, i], qk_v[:, i],
                                      norm[:, cols(i, HEADS)].unsqueeze(2).to_broadcast(
                                          [P, HEADS, HD2]), ALU.mult).then_inc(S.normed, 1)

                for k in range(TURNS):
                    dve.wait_ge(S.table_loaded, due(k, "table_loaded", 1))
                    if k:
                        dve.wait_ge(S.qk_turned, due(k, "qk_turned", -2))
                    rotate(k, 0)
                    lengths(k, 0)
                    dve.wait_ge(S.scores_ready, due(k, "scores_ready", 1))
                    if k:
                        dve.wait_ge(S.probs_turned, due(k, "probs_turned", 0))
                        dve.wait_ge(S.mask_loaded, k)
                    for h in range(2):
                        ins = dve.scalar_tensor_tensor(
                            out=prob[:, :, h], in0=s_ps[:, h].rearrange("q (p j) -> q p j", p=PAIRS),
                            scalar=QK_SCALE,
                            in1=G.mask_t[:, 1 - k % 2].unsqueeze(1).to_broadcast([P, PAIRS, HD2]),
                            op0=ALU.mult, op1=ALU.add)
                        if h == 0:
                            chain(ins)
                    ins.then_inc(S.masked, 1)
                    dve.wait_ge(S.masked, k + 1)
                    chain(dve.tensor_reduce(top[:], prob[:], AX_X, ALU.max))
                    flat = prob[:].rearrange("q p h j -> q (p h) j")
                    bc = lambda a: a[:].rearrange("q p h -> q (p h)").unsqueeze(2).to_broadcast(
                        [P, HEADS, HD2])
                    dve.tensor_tensor(flat, flat, bc(top), ALU.subtract).then_inc(S.shifted, 1)
                    if k:
                        dve.wait_ge(S.y_ready, due(k, "y_ready", 0))
                    for i in range(2):
                        dve.wait_ge(S.o_turned, due(k, "o_turned", i + 1))
                        dve.tensor_copy(o_cols[:, 4 * i:4 * i + 4],
                                        s_ps[:, i].rearrange("p (a n) -> p a n", a=4)) \
                            .then_inc(S.o_taken, 1)
                    dve.wait_ge(S.exps_ready, due(k, "exps_ready", 1))
                    if k:
                        dve.wait_ge(S.o_copied, due(k, "o_copied", 0))
                    chain(dve.tensor_reduce(total[:], prob[:], AX_X, ALU.add))
                    chain(dve.reciprocal(total[:], total[:]))
                    dve.wait_ge(S.probs_turned, due(k, "probs_turned", 1))
                    if k:
                        dve.wait_ge(S.out_ready, due(k, "out_ready", 0))
                    dve.tensor_copy(pt[:, 0:4], w_ps[:, 0].rearrange("p (a n) -> p a n", a=4)) \
                        .then_inc(S.pt_low, 1)
                    normalise(k, 0)
                    dve.wait_ge(S.y_ready, due(k, "y_ready", 1))
                    dve.tensor_tensor(G.mid_all[:, bass.ds((first + k) * P, P)],
                                      G.cur_all[:, bass.ds((first + k) * P, P)], s_ps[:, 0, 0:P],
                                      ALU.add).then_inc(S.y_stored, 1)
                    lengths(k, 1)
                    if k:
                        dve.wait_ge(S.qk_turned, due(k, "qk_turned", 0))
                    rotate(k, 1)
                    normalise(k, 1)
                    dve.wait_ge(S.o_turned, due(k, "o_turned", 2))
                    for h in range(2):
                        dve.wait_ge(S.out_ready, due(k, "out_ready", h + 1))
                        dve.tensor_tensor(G.o_rows[:, :, h],
                                          s_ps[:, h].rearrange("q (p d) -> q p d", d=HD2),
                                          total[:, :, h:h + 1].to_broadcast([P, PAIRS, HD2]),
                                          ALU.mult).then_inc(S.o_copied, 1)
                dve.wait_ge(S.normed, due(TURNS, "normed", 0))


def gated_ffn(nc, K, G, loads):
    chunks = FF_PAD // P
    units = [(q, c) for q in range(QUARTERS) for c in range(chunks)]
    with ExitStack() as ctx:
        M = Memory(nc, ctx)
        gate = M.sb("b2g_gate", [P, 3, QW])
        hidden = M.sb("b2g_hidden", [P, 3, QW])
        a_ps = M.ps("b2g_a_ps", [P, 2, QW])
        g_ps = M.ps("b2g_g_ps", [P, 2, QW])
        y_ps = M.ps("b2g_y_ps", [P, 2, QW])
        with stage(nc, "g_ready", "a_ready", "gelu_ready", "hidden_ready", "y_added",
                   "stored", "loaded", "scaled") as (block, S):

            @block.sync
            def _(sp):
                for tile, array in loads:
                    sp.dma_start(tile, array).then_inc(S.loaded, 16)

            @block.tensor
            def _(pe):
                for u in range(len(units) + 2):
                    if u < len(units):
                        q, c = units[u]
                        if u >= 2:
                            pe.wait_ge(S.hidden_ready, u - 1)
                        x_q = G.shifted[:, cols(q, QW)]
                        pe.matmul(g_ps[:, u % 2], G.w1[:, chunks + c], x_q, start=True, stop=True) \
                            .then_inc(S.g_ready, 1)
                        pe.matmul(a_ps[:, u % 2], G.w1[:, c], x_q, start=True, stop=True) \
                            .then_inc(S.a_ready, 1)
                    if u >= 2:
                        q, c = units[u - 2]
                        pe.wait_ge(S.hidden_ready, u - 1)
                        if c == 0 and q >= 2:
                            pe.wait_ge(S.stored, q - 1)
                        pe.matmul(y_ps[:, q % 2], G.w2[:, c], hidden[:, (u - 2) % 3],
                                  start=(c == 0), stop=(c == chunks - 1)).then_inc(S.y_added, 1)

            @block.scalar
            def _(act):
                for u, (q, c) in enumerate(units):
                    act.wait_ge(S.g_ready, u + 1)
                    if u >= 3:
                        act.wait_ge(S.hidden_ready, u - 2)
                    act.activation(gate[:, u % 3], g_ps[:, u % 2], ACT.Gelu,
                                   bias=G.small[:, 5 + c:6 + c]).then_inc(S.gelu_ready, 1)

            @block.vector
            def _(dve):
                def store(u):
                    q, c = units[u]
                    if c == chunks - 1:
                        dve.wait_ge(S.y_added, u + 1)
                        dve.scalar_tensor_tensor(out=G.cur[:, cols(q, QW)], in0=y_ps[:, q % 2],
                                                 scalar=G.small[:, 8:9], in1=G.mid[:, cols(q, QW)],
                                                 op0=ALU.add, op1=ALU.add).then_inc(S.stored, 1)

                for u, (q, c) in enumerate(units):
                    dve.wait_ge(S.gelu_ready, u + 1)
                    dve.wait_ge(S.a_ready, u + 1)
                    if u >= 3:
                        dve.wait_ge(S.y_added, u - 2)
                    dve.scalar_tensor_tensor(out=hidden[:, u % 3], in0=a_ps[:, u % 2],
                                             scalar=G.small[:, 2 + c:3 + c], in1=gate[:, u % 3],
                                             op0=ALU.add, op1=ALU.mult).then_inc(S.hidden_ready, 1)
                    if u >= 2:
                        store(u - 2)
                store(len(units) - 2)
                store(len(units) - 1)
                dve.wait_ge(S.loaded, 16 * len(loads))
                scale_rotary(dve, G).then_inc(S.scaled, 1)
                dve.wait_ge(S.scaled, 1)
                dve.wait_ge(S.stored, QUARTERS)



def rotary_tables2():
    f = np.float32
    half = np.arange(0, HD2, 2, dtype=f)
    inv_freq = (1.0 / (f(10000.0) ** (half / f(HD2)))).astype(f)
    t = np.arange(T, dtype=f)
    freqs = (t[:, None] * inv_freq[None, :]).astype(f)
    freqs = np.concatenate([freqs, freqs], -1)
    base = ((half + f(0.4 * HD2)) / f(1.4 * HD2)).astype(f)
    power = ((t - T // 2) / f(WIN // 2)).astype(f)
    scale = (base[None, :] ** power[:, None]).astype(f)
    scale = np.concatenate([scale, scale], -1)
    sign = np.where(np.arange(HD2) < HD2 // 2, f(-1.0), f(1.0))
    table = np.stack([np.cos(freqs) * scale, np.sin(freqs) * scale * sign,
                      np.cos(freqs) / scale, np.sin(freqs) / scale * sign], axis=1).astype(f)
    return table.reshape(QT, P, 4, HD2).transpose(1, 0, 2, 3)


def local_mask():
    i = np.arange(P)[:, None] % WIN
    j = np.arange(2 * WIN)[None, :]
    seen = (j >= i) & (j <= i + WIN)
    first = seen & ((j >= WIN) | (np.arange(P)[:, None] >= WIN))
    m = np.repeat(seen[:, None], QT, 1)
    m[:, 0] = first
    return np.where(m, 0.0, -3e38).astype(np.float32)


def stack_matrix(slots):
    m = np.zeros((P, PAIRS, 3, P), np.float32)
    for pair in range(PAIRS):
        for h in range(2):
            for slot, part in enumerate(slots):
                for d in range(HD):
                    m[(2 * pair + h) * HD + d, pair, part, 64 * h + HD * slot + d] = 1.0
    return m


def rotary_heads():
    freq = (1.0 / 10000.0 ** (np.arange(0, HD, 2, dtype=np.float32) / HD)).astype(np.float32)
    angle = np.arange(T, dtype=np.float32)[None, :] * freq[:, None]
    angle = angle.astype(np.float32)
    table = np.zeros((HD, 2, T), np.float32)
    table[0::2, 0] = table[1::2, 0] = np.cos(angle)
    table[0::2, 1] = -np.sin(angle)
    table[1::2, 1] = np.sin(angle)
    return np.tile(table, (HEADS, 1, 1))


def row_masks():
    m = np.zeros((P, 4), np.float32)
    for h in range(2):
        for slot, part in enumerate(SLOTS_K):
            m[64 * h + HD * slot:64 * h + HD * (slot + 1), part] = 1.0
        for part in range(3):
            m[64 * h + ONES_AT + part, part] = 1.0
            m[64 * h + ONES_AT + part, 3] = 1.0
    return m


def pick_matrix(experts, per_expert):
    chunks = max(1, experts * per_expert // P)
    if per_expert >= P:
        m = np.zeros((experts, experts, P), np.float32)
        m[np.arange(experts), np.arange(experts)] = 1.0
        return m
    m = np.zeros((experts, chunks, P), np.float32)
    for c in range(chunks):
        for p in range(P):
            m[(c * P + p) // per_expert, c, p] = 1.0
    return m


def constants():
    return {
        "c_ident": np.eye(P, dtype=np.float32),
        "c_mean": np.full((P, P), 1.0 / P, np.float32),
        "c_ones": np.ones((P, QW), np.float32),
        "c_pick16": pick_matrix(16, 64),
        "c_pick16_short": pick_matrix(16, 64).astype(BF16_NP),
        "c_pick4": pick_matrix(4, 512),
        "c_pick9": pick_matrix(9, 512),
        "c_one_row": np.ones((1, N), np.float32),
        "c_stack_q": stack_matrix(SLOTS_Q).astype(BF16_NP),
        "c_stack_k": stack_matrix(SLOTS_K).astype(BF16_NP),
        "c_turn": rotary_heads(),
        "c_rotary2": rotary_tables2(),
        "c_local_mask": local_mask(),
        "c_keep": np.repeat((np.arange(QT) > 0).astype(np.float32)[None], P, 0),
        "c_causal": np.where(np.tril(np.ones((P, P))) > 0, 0.0, -1e10).astype(np.float32),
    }


def layouts(v):
    a = {}
    a["x"] = v["L0_attn_x"].reshape(N, P).T
    up = np.concatenate([v["L0_ffn_routed_up"], v["L0_ffn_shared_up"]]).reshape(9, P, P)
    a["b0f_up"] = up.transpose(2, 0, 1)
    down = np.concatenate([v["L0_ffn_routed_down"], v["L0_ffn_shared_down"]])
    a["b0f_down"] = down.transpose(0, 2, 1).reshape(9, P, P).transpose(1, 0, 2)
    a["b0f_router"] = v["L0_ffn_router_w"].T
    a["b0a_wd"] = v["L0_attn_Wd"]
    rep = lambda r: np.repeat(r.reshape(1, -1), P, 0)
    col = lambda c: c.reshape(P, 1)
    a["b0a_small"] = np.concatenate(
        [v["L0_attn_WB"], v["L0_attn_WC"], rep(v["L0_attn_bB"]), rep(v["L0_attn_bC"]),
         v["L0_attn_A_log"], col(v["L0_attn_D_param"]), col(v["L0_attn_bd"]), col(v["L0_attn_ln_w"]),
         col(v["L0_attn_ln_b"]), np.zeros((P, 4), np.float32)], axis=1)
    a["b0m_up"] = v["L0_attn_up_w"].reshape(4, P, 4, P).transpose(1, 0, 2, 3)
    a["b0m_down"] = v["L0_attn_down_w"].reshape(4, 4, P, P).transpose(2, 0, 1, 3)
    a["b0m_b1"] = v["L0_attn_up_b"].reshape(16, P).T
    a["b0m_b2"] = v["L0_attn_down_b"]
    a["b0m_router"] = v["L0_attn_Wr"]
    a["b0m_router_b"] = v["L0_attn_br"].reshape(1, 4)
    w1 = np.concatenate([v["L1_ffn_W1"], v["L1_ffn_Ws1"][None]])
    w2 = np.concatenate([v["L1_ffn_W2"], v["L1_ffn_Ws2"][None]])
    a["b1f_up"] = w1.reshape(9, P, 4, P).transpose(1, 0, 2, 3)
    a["b1f_down"] = w2.reshape(9, 4, P, P).transpose(2, 0, 1, 3)
    a["b1f_b1"] = np.concatenate([v["L1_ffn_b1"], v["L1_ffn_bs1"][None]]).reshape(36, P).T
    a["b1f_b2"] = np.concatenate([v["L1_ffn_b2"], v["L1_ffn_bs2"][None]])
    a["b1f_gate_w"] = v["L1_ffn_gate"]
    wqkv = v["L1_attn_Wqkv"].reshape(HEADS, 3, HD, P).transpose(3, 1, 0, 2).reshape(P, 3, P)
    bqkv = v["L1_attn_bqkv"].reshape(HEADS, 3, HD).transpose(1, 0, 2).reshape(3, P)
    a["b1a_w"] = wqkv
    a["b1a_v_bias"] = bqkv[2:3]
    wr, br = v["L1_attn_Wr"], v["L1_attn_br"]
    near_at = np.clip(np.arange(QW) - (2 * P - 1), -WINDOW1, WINDOW1) + WINDOW1
    masks = row_masks()
    positions = np.zeros((P, QW + 2), wr.dtype)
    for h in range(2):
        for slot in range(len(SLOTS_K)):
            rows = slice(64 * h + HD * slot, 64 * h + HD * (slot + 1))
            positions[rows, 0:QW] = wr[near_at].T
        rows = slice(64 * h + ONES_AT, 64 * h + ONES_AT + 3)
        positions[rows, 0:QW] = br[near_at]
        positions[rows, QW] = br[0]
        positions[rows, QW + 1] = br[-1]
    a["b1a_positions"] = positions
    a["b1a_small"] = np.concatenate(
        [bqkv.T, np.tile(wr[0], HEADS)[:, None], np.tile(wr[-1], HEADS)[:, None],
         np.zeros((P, 1), np.float32), masks, np.zeros((P, 2), np.float32)], axis=1)
    swap = np.arange(P) ^ 1
    a["b3a_w"] = np.stack([v["L3_attn_qw"], v["L3_attn_kw"], v["L3_attn_vw"],
                           v["L3_attn_qw"][:, swap], v["L3_attn_kw"][:, swap],
                           v["L3_attn_ow"]], axis=1)
    a["b2f_wqkv"] = v["L2_ffn_Wqkv"]
    a["b2f_wo"] = v["L2_ffn_Wo"].reshape(LAYERS, PAIRS, P, P).transpose(0, 2, 1, 3)
    zeros = lambda *shape: np.zeros(shape, np.float32)
    w1 = v["L2_ffn_W1"].reshape(LAYERS, P, 2, FF)
    a["b2f_w1"] = np.concatenate([w1, zeros(LAYERS, P, 2, FF_PAD - FF)], 3).reshape(LAYERS, P, 6, P)
    w2 = np.concatenate([v["L2_ffn_W2"], zeros(LAYERS, FF_PAD - FF, P)], 1)
    a["b2f_w2"] = w2.reshape(LAYERS, 3, P, P).transpose(0, 2, 1, 3)
    fb1 = np.concatenate([v["L2_ffn_b1"].reshape(LAYERS, 2, FF), zeros(LAYERS, 2, FF_PAD - FF)], 2)
    a["b2f_small"] = np.concatenate(
        [v["L2_ffn_ln_g"][:, :, None], v["L2_ffn_ln_b"][:, :, None],
         fb1.reshape(LAYERS, 6, P).transpose(0, 2, 1), v["L2_ffn_b2"][:, :, None]], axis=2)
    rot = np.arange(HD2) ^ (HD2 // 2)
    qs, ks = v["L2_ffn_q_scale"], v["L2_ffn_k_scale"]
    scales = np.stack([qs, qs[:, rot], ks, ks[:, rot]], axis=1)
    a["b2f_scales"] = np.repeat(scales[:, None], P, 1)
    for n in "qkv":
        f = lambda key: v[f"L3_ffn_{n}_{key}"]
        a[f"b3f_{n}_up"] = f("w1").reshape(8, 2, P, 64).transpose(2, 0, 1, 3).reshape(P, 8, P)
        a[f"b3f_{n}_down"] = f("w2").reshape(8, P, P).transpose(1, 0, 2)
        a[f"b3f_{n}_b1"] = f("b1").reshape(8, P).T
        a[f"b3f_{n}_b2"] = f("b2")
        a[f"b3f_{n}_node_w"] = np.concatenate([f("node_w").T, np.zeros((P, 1), np.float32)], axis=1)
        a[f"b3f_{n}_node_b"] = np.concatenate([f("node_b"), np.zeros(1, np.float32)])[None]
    a["b3a_small"] = np.zeros((P, 12), np.float32)
    a["b2a_w"] = np.stack([v["L2_attn_Wk"].T, v["L2_attn_Wv"].T, v["L2_attn_Wr"].T,
                           v["L2_attn_Wo"].T], axis=1)
    a["b2a_small"] = np.concatenate(
        [v["L2_attn_time_decay"], v["L2_attn_time_first"], v["L2_attn_time_mix_k"][0].T,
         v["L2_attn_time_mix_v"][0].T, v["L2_attn_time_mix_r"][0].T], axis=1)
    return {k: np.ascontiguousarray(x) for k, x in a.items()}


def load_constants(nc, M, W):
    shapes = {"ident": [P, P], "mean": [P, P], "ones": [P, QW], "pick16": [16, 8, P], "pick4": [4, 4, P],
              "pick9": [9, 9, P], "causal": [P, P]}
    tiles = {n: M.sb(f"c_{n}", s) for n, s in shapes.items()}
    load(nc, "constants", [(tiles[n][:], W[f"c_{n}"]) for n in shapes])
    return Names(flag=M.sb("c_flag", [1, 1], mybir.dt.int32),
                 scratch=nc.dram_tensor("position_scratch", [4, 2, P, QW], F32, kind="Internal").ap(),
                 **tiles)



def build(nc, W, out):
    with ExitStack() as ctx:
        M = Memory(nc, ctx)
        K = load_constants(nc, M, W)
        x = M.sb("x", [P, N])
        xn = M.sb("xn", [P, N])
        load(nc, "x", [(x[:], W["x"])])
        layer_norm(nc, K, "n0", x, xn)
        block0_attn(nc, K, W, xn, x)
        block0_ffn(nc, K, W, xn, x)
        layer_norm(nc, K, "n1", x, xn)
        head_attention(nc, K, W, "b1a", xn, x, relative=True)
        block1_ffn(nc, K, W, xn, x)
        layer_norm(nc, K, "n2", x, xn)
        block2_attn(nc, K, W, xn, x)
        block2_ffn(nc, K, W, xn, x)
        layer_norm(nc, K, "n3", x, xn)
        head_attention(nc, K, W, "b3a", xn, x, relative=False)
        block3_ffn(nc, K, W, xn, x)
        load(nc, "out", [(out, x[:])])


def kernel(**inputs):
    import concourse.bacc as bacc
    from concourse.bass_utils import run_bass_kernel_spmd

    nc = bacc.Bacc("TRN2", target_bir_lowering=False, num_devices=1)
    arrays = {**constants(), **layouts({k: np.asarray(a) for k, a in inputs.items()})}
    W = {name: nc.dram_tensor(f"in_{name}", a.shape, mybir.dt.from_np(a.dtype),
                              kind="ExternalInput").ap() for name, a in arrays.items()}
    out = nc.dram_tensor("out", (P, N), F32, kind="ExternalOutput").ap()
    build(nc, W, out)
    run = run_bass_kernel_spmd(nc, [{f"in_{n}": a for n, a in arrays.items()}], core_ids=[0])
    return np.ascontiguousarray(run.results[0]["out"].T).reshape(B, T, P)
```
